# Optimizing a Trainium2 kernel written in Bass

```python
import numpy as np
import jax
import jax.numpy as jnp

def _softmax(x, axis=-1):
    return jax.nn.softmax(x, axis=axis)

def _gelu(x):
    return jax.nn.gelu(x, approximate=True)

def _silu(x):
    return jax.nn.silu(x)

def _sigmoid(x):
    return jax.nn.sigmoid(x)

def _layernorm(x, axis=-1, eps=1e-05):
    m = jnp.mean(x, axis=axis, keepdims=True)
    v = jnp.var(x, axis=axis, keepdims=True)
    return (x - m) / jnp.sqrt(v + eps)

def _scatter_add(tgt, idx, src, axis=0):
    return tgt.at[idx].add(src)

def _segment_sum(src, seg, n):
    return jax.ops.segment_sum(src, seg, n)
kernel_name = 'mk_perceiver_d1_seqx_r4_7cbc0b'

def setup_inputs(seed: int=0):
    np.random.seed(seed)
    _w = jnp.asarray

    def _rec_inputs():
        import jax
        import jax.numpy as jnp
        _rk = jax.random.key(seed)
        x = -0.0003929 + 0.9999 * jax.random.normal(jax.random.fold_in(_rk, 1), (32, 32, 256), jnp.float32)
        _lenS = 32 - jax.random.randint(jax.random.fold_in(_rk, 7), (32,), 0, max(1, 32 // 4) + 1, jnp.int32)
        _lenS2 = 257 - jax.random.randint(jax.random.fold_in(_rk, 8), (32,), 0, max(1, 257 // 4) + 1, jnp.int32)
        _ctx_768P = jax.random.normal(jax.random.fold_in(_rk, 11), (32, 16, 192), jnp.float32)
        _ctx_768c = jax.random.dirichlet(jax.random.fold_in(_rk, 511), 0.3 * jnp.ones((16,), jnp.float32), (32, 257))
        _ctx_768t = jnp.einsum('bsk,bkd->bsd', _ctx_768c, _ctx_768P)
        _ctx_768t = _ctx_768t * jax.lax.rsqrt(jnp.mean(jnp.square(_ctx_768t)) + 1e-12) * 0.953939
        ctx_768 = 0.00095986 + 0.999812 * (_ctx_768t + 0.3 * jax.random.normal(jax.random.fold_in(_rk, 611), (32, 257, 192), jnp.float32))
        _validS = jnp.arange(32)[None, :] < _lenS[:, None]
        _validS2 = jnp.arange(257)[None, :] < _lenS2[:, None]
        _causal = jnp.tril(jnp.ones((32, 32), dtype=bool))
        mask_BxS2_bf1 = jnp.ones((32, 257), dtype=bool)
        return (x, ctx_768, mask_BxS2_bf1)
    x, ctx_768, mask_BxS2_bf1 = _rec_inputs()

    def _L0_xattn_setup():
        import jax, jax.numpy as jnp
        import numpy as np
        DIM = 256
        CTX_DIM = 192
        HEADS = 16
        key = jax.random.key(seed)
        ks = jax.random.split(key, 7)
        B, N, M = (4, 1024, 64)
        x = jax.random.normal(ks[0], (B, N, DIM), dtype=jnp.float32)
        context = jax.random.normal(ks[1], (B, M, CTX_DIM), dtype=jnp.float32)
        context_mask = jnp.ones((B, M), dtype=bool)
        s_d = 1.0 / np.sqrt(DIM)
        s_c = 1.0 / np.sqrt(CTX_DIM)
        Wq = jax.random.normal(ks[2], (DIM, DIM), dtype=jnp.float32) * s_d
        Wk = jax.random.normal(ks[3], (CTX_DIM, DIM), dtype=jnp.float32) * s_c
        Wv = jax.random.normal(ks[4], (CTX_DIM, DIM), dtype=jnp.float32) * s_c
        Wo = jax.random.normal(ks[5], (DIM, DIM), dtype=jnp.float32) * s_d
        return {'x': x, 'context': context, 'context_mask': context_mask, 'Wq': Wq, 'Wk': Wk, 'Wv': Wv, 'Wo': Wo}
    _L0_xattn_all = _L0_xattn_setup()
    _L0_xattn_in = {k: v for k, v in _L0_xattn_all.items() if k in ('Wq', 'Wk', 'Wv', 'Wo')}
    del _L0_xattn_all

    def _L0_attn_setup():
        import jax, jax.numpy as jnp
        import numpy as np
        NHEADS = 16
        SCALE_BASE = 128
        GN_EPS = 1e-05

        def rotate_every_two(x):
            x1 = x[..., ::2]
            x2 = x[..., 1::2]
            return jnp.stack((-x2, x1), axis=-1).reshape(x.shape)

        def xpos_apply(x, downscale, offset=0):
            B, T, C = x.shape
            half = C // 2
            scale_vec = (jnp.arange(0, C, 2, dtype=jnp.float32) + 0.4 * C) / (1.4 * C)
            min_pos = -(T + offset) // 2
            max_pos = T + offset + min_pos
            power = jnp.arange(min_pos, max_pos, dtype=jnp.float32) / SCALE_BASE
            scale = scale_vec[None, :] ** power[:, None]
            L = scale.shape[0]
            inv_freq = 1.0 / 10000.0 ** (jnp.arange(half, dtype=jnp.float32) / half)
            sinusoid = jnp.arange(L, dtype=jnp.float32)[:, None] * inv_freq[None, :]
            sin, cos = (jnp.sin(sinusoid), jnp.cos(sinusoid))
            if L > T:
                scale, sin, cos = (scale[-T:], sin[-T:], cos[-T:])
            if downscale:
                scale = 1.0 / scale
            sin = jnp.repeat(sin * scale, 2, axis=-1)
            cos = jnp.repeat(cos * scale, 2, axis=-1)
            return x * cos + rotate_every_two(x) * sin

        def decay_mask(nheads, T):
            gamma = 1.0 - 2.0 ** (-5.0 - jnp.arange(nheads, dtype=jnp.float32))
            idx = jnp.arange(T)
            diff = idx[:, None] - idx[None, :]
            keep = diff >= 0
            m = gamma[:, None, None] ** jnp.where(keep, diff, 0).astype(jnp.float32)
            return jnp.where(keep[None, :, :], m, 0.0)
        key = jax.random.key(seed)
        ks = jax.random.split(key, 6)
        B, T, C = (2, 512, 256)
        w_std = 0.02
        return {'x': jax.random.normal(ks[0], (B, T, C), jnp.float32), 'w_qkvff': jax.random.normal(ks[1], (5 * C, C), jnp.float32) * w_std, 'w_gated': jax.random.normal(ks[2], (C, C), jnp.float32) * w_std, 'b_gated': jnp.zeros((C,), jnp.float32), 'w_proj': jax.random.normal(ks[3], (C, C), jnp.float32) * w_std, 'b_proj': jnp.zeros((C,), jnp.float32), 'gn_w': jnp.ones((C,), jnp.float32), 'gn_b': jnp.zeros((C,), jnp.float32), 'w_ff': jax.random.normal(ks[4], (C, 2 * C), jnp.float32) * w_std, 'rms_w': jnp.ones((C,), jnp.float32)}
    _L0_attn_all = _L0_attn_setup()
    _L0_attn_in = {k: v for k, v in _L0_attn_all.items() if k in ('w_qkvff', 'w_gated', 'b_gated', 'w_proj', 'b_proj', 'gn_w', 'gn_b', 'w_ff', 'rms_w')}
    del _L0_attn_all

    def _L0_ffn_setup():
        import jax, jax.numpy as jnp
        import numpy as np
        EMB = 256
        FF = 4 * EMB

        def _ternary(w):
            scale = jnp.maximum(jnp.mean(jnp.abs(w)), 1e-08)
            w_t = jnp.clip(jnp.round(w / scale), -1.0, 1.0)
            return w + jax.lax.stop_gradient(w_t - w)
        key = jax.random.key(seed)
        kx, k1, k2, kb1, kb2 = jax.random.split(key, 5)
        x = jax.random.normal(kx, (4, 512, EMB), dtype=jnp.float32)
        lim1 = 1.0 / np.sqrt(EMB)
        lim2 = 1.0 / np.sqrt(FF)
        W1 = jax.random.uniform(k1, (FF, EMB), jnp.float32, -lim1, lim1)
        b1 = jax.random.uniform(kb1, (FF,), jnp.float32, -lim1, lim1)
        W2 = jax.random.uniform(k2, (EMB, FF), jnp.float32, -lim2, lim2)
        b2 = jax.random.uniform(kb2, (EMB,), jnp.float32, -lim2, lim2)
        return {'x': x, 'W1': W1, 'b1': b1, 'W2': W2, 'b2': b2}
    _L0_ffn_all = _L0_ffn_setup()
    _L0_ffn_in = {k: v for k, v in _L0_ffn_all.items() if k in ('W1', 'b1', 'W2', 'b2')}
    del _L0_ffn_all
    return {'x': x, 'ctx_768': ctx_768, 'mask_BxS2_bf1': mask_BxS2_bf1, 'L0_xattn_Wq': _L0_xattn_in['Wq'], 'L0_xattn_Wk': _L0_xattn_in['Wk'], 'L0_xattn_Wv': _L0_xattn_in['Wv'], 'L0_xattn_Wo': _L0_xattn_in['Wo'], 'L0_attn_w_qkvff': _L0_attn_in['w_qkvff'], 'L0_attn_w_gated': _L0_attn_in['w_gated'], 'L0_attn_b_gated': _L0_attn_in['b_gated'], 'L0_attn_w_proj': _L0_attn_in['w_proj'], 'L0_attn_b_proj': _L0_attn_in['b_proj'], 'L0_attn_gn_w': _L0_attn_in['gn_w'], 'L0_attn_gn_b': _L0_attn_in['gn_b'], 'L0_attn_w_ff': _L0_attn_in['w_ff'], 'L0_attn_rms_w': _L0_attn_in['rms_w'], 'L0_ffn_W1': _L0_ffn_in['W1'], 'L0_ffn_b1': _L0_ffn_in['b1'], 'L0_ffn_W2': _L0_ffn_in['W2'], 'L0_ffn_b2': _L0_ffn_in['b2']}

def reference(x, ctx_768, mask_BxS2_bf1, L0_xattn_Wq, L0_xattn_Wk, L0_xattn_Wv, L0_xattn_Wo, L0_attn_w_qkvff, L0_attn_w_gated, L0_attn_b_gated, L0_attn_w_proj, L0_attn_b_proj, L0_attn_gn_w, L0_attn_gn_b, L0_attn_w_ff, L0_attn_rms_w, L0_ffn_W1, L0_ffn_b1, L0_ffn_W2, L0_ffn_b2):
    import jax
    import jax.numpy as jnp

    def _L0_xattn_ref(x, context, context_mask, Wq, Wk, Wv, Wo):
        import jax, jax.numpy as jnp
        import numpy as np
        DIM = 256
        CTX_DIM = 192
        HEADS = 16
        B, N, _ = x.shape
        M = context.shape[1]
        hd = DIM // HEADS
        scale = hd ** (-0.5)
        q = (x @ Wq).reshape(B, N, HEADS, hd).transpose(0, 2, 1, 3)
        k = (context @ Wk).reshape(B, M, HEADS, hd).transpose(0, 2, 1, 3)
        v = (context @ Wv).reshape(B, M, HEADS, hd).transpose(0, 2, 1, 3)
        scores = jnp.einsum('bhid,bhjd->bhij', q, k) * scale
        max_neg = -jnp.finfo(scores.dtype).max
        scores = jnp.where(context_mask[:, None, None, :], scores, max_neg)
        attn = jax.nn.softmax(scores, axis=-1)
        out = jnp.einsum('bhij,bhjd->bhid', attn, v)
        out = out.transpose(0, 2, 1, 3).reshape(B, N, DIM)
        return out @ Wo

    def _L0_attn_ref(x, w_qkvff, w_gated, b_gated, w_proj, b_proj, gn_w, gn_b, w_ff, rms_w):
        import jax, jax.numpy as jnp
        import numpy as np
        NHEADS = 16
        SCALE_BASE = 128
        GN_EPS = 1e-05

        def rotate_every_two(x):
            x1 = x[..., ::2]
            x2 = x[..., 1::2]
            return jnp.stack((-x2, x1), axis=-1).reshape(x.shape)

        def xpos_apply(x, downscale, offset=0):
            B, T, C = x.shape
            half = C // 2
            scale_vec = (jnp.arange(0, C, 2, dtype=jnp.float32) + 0.4 * C) / (1.4 * C)
            min_pos = -(T + offset) // 2
            max_pos = T + offset + min_pos
            power = jnp.arange(min_pos, max_pos, dtype=jnp.float32) / SCALE_BASE
            scale = scale_vec[None, :] ** power[:, None]
            L = scale.shape[0]
            inv_freq = 1.0 / 10000.0 ** (jnp.arange(half, dtype=jnp.float32) / half)
            sinusoid = jnp.arange(L, dtype=jnp.float32)[:, None] * inv_freq[None, :]
            sin, cos = (jnp.sin(sinusoid), jnp.cos(sinusoid))
            if L > T:
                scale, sin, cos = (scale[-T:], sin[-T:], cos[-T:])
            if downscale:
                scale = 1.0 / scale
            sin = jnp.repeat(sin * scale, 2, axis=-1)
            cos = jnp.repeat(cos * scale, 2, axis=-1)
            return x * cos + rotate_every_two(x) * sin

        def decay_mask(nheads, T):
            gamma = 1.0 - 2.0 ** (-5.0 - jnp.arange(nheads, dtype=jnp.float32))
            idx = jnp.arange(T)
            diff = idx[:, None] - idx[None, :]
            keep = diff >= 0
            m = gamma[:, None, None] ** jnp.where(keep, diff, 0).astype(jnp.float32)
            return jnp.where(keep[None, :, :], m, 0.0)
        B, T, C = x.shape
        H = NHEADS
        hd = C // H
        nrm = jnp.sqrt(jnp.sum(x * x, axis=-1, keepdims=True)) * C ** (-0.5)
        x_ = x / jnp.maximum(nrm, 1e-08) * rms_w
        qkvff = jnp.einsum('btc,oc->bto', x_, w_qkvff)
        q, k, v, ff = jnp.split(qkvff, [C, 2 * C, 3 * C], axis=-1)
        q = xpos_apply(q, downscale=False)
        k = xpos_apply(k, downscale=True)
        q = q.reshape(B, T, H, hd).transpose(0, 2, 1, 3)
        k = k.reshape(B, T, H, hd).transpose(0, 2, 1, 3)
        v = v.reshape(B, T, H, hd).transpose(0, 2, 1, 3)
        scores = jnp.einsum('bhtd,bhsd->bhts', q, k) * hd ** (-0.5)
        scores = scores * decay_mask(H, T)[None]
        y = jnp.einsum('bhts,bhsd->bhtd', scores, v)
        yg = y.transpose(0, 2, 1, 3).reshape(B * T, H, hd)
        mu = jnp.mean(yg, axis=-1, keepdims=True)
        var = jnp.mean((yg - mu) ** 2, axis=-1, keepdims=True)
        yg = (yg - mu) / jnp.sqrt(var + GN_EPS)
        y = yg.reshape(B * T, C) * gn_w + gn_b
        y = y.reshape(B, T, C)
        y = jax.nn.silu(jnp.einsum('btc,oc->bto', x, w_gated) + b_gated) * y
        y = jnp.einsum('btc,oc->bto', y, w_proj) + b_proj
        ff_out = jnp.einsum('bte,ce->btc', jax.nn.gelu(ff, approximate=False), w_ff)
        return x + ff_out + y

    def _L0_ffn_ref(x, W1, b1, W2, b2):
        import jax, jax.numpy as jnp
        import numpy as np
        EMB = 256
        FF = 4 * EMB

        def _ternary(w):
            scale = jnp.maximum(jnp.mean(jnp.abs(w)), 1e-08)
            w_t = jnp.clip(jnp.round(w / scale), -1.0, 1.0)
            return w + jax.lax.stop_gradient(w_t - w)
        h = jnp.einsum('bsd,fd->bsf', x, _ternary(W1)) + b1
        h = jax.nn.gelu(h, approximate=False)
        out = jnp.einsum('bsf,df->bsd', h, _ternary(W2)) + b2
        return out
    x = x + _L0_xattn_ref(_layernorm(x, axis=-1), ctx_768, mask_BxS2_bf1, L0_xattn_Wq, L0_xattn_Wk, L0_xattn_Wv, L0_xattn_Wo)
    x = x + _L0_attn_ref(_layernorm(x, axis=-1), L0_attn_w_qkvff, L0_attn_w_gated, L0_attn_b_gated, L0_attn_w_proj, L0_attn_b_proj, L0_attn_gn_w, L0_attn_gn_b, L0_attn_w_ff, L0_attn_rms_w)
    x = x + _L0_ffn_ref(_layernorm(x, axis=-1), L0_ffn_W1, L0_ffn_b1, L0_ffn_W2, L0_ffn_b2)
    return x

_drawn_inputs = setup_inputs


def setup_inputs(seed=0):
    import zlib

    import numpy as np

    out = dict(_drawn_inputs(seed))
    spreads = {'L0_attn_b_gated': (0.0, 0.8),
     'L0_attn_b_proj': (0.0, 0.1),
     'L0_attn_gn_w': (1.0, 0.6),
     'L0_attn_gn_b': (0.0, 0.8),
     'L0_attn_rms_w': (1.0, 0.6)}
    factors = {'L0_ffn_b1': 25.767, 'L0_ffn_b2': 64.0}
    for name, (base, spread) in spreads.items():
        noise = np.random.default_rng([zlib.crc32(name.encode()), seed]).standard_normal(out[name].shape)
        drawn = base * np.exp(spread * noise) if base else spread * noise
        out[name] = jnp.asarray(drawn.astype(out[name].dtype))
    for name, factor in factors.items():
        out[name] = (out[name] * factor).astype(out[name].dtype)
    return out
```

```python
from contextlib import ExitStack

import numpy as np

import concourse.bass as bass
from concourse import mybir

F32, F16, BF16, U8 = mybir.dt.float32, mybir.dt.float16, mybir.dt.bfloat16, mybir.dt.uint8
ALU = mybir.AluOpType
ACT = mybir.ActivationFunctionType
AX_X = mybir.AxisListType.X

B, S, C = 32, 32, 256
M, CC = 257, 192
H, HD = 16, 16
G, A = 4, 4
MF = 256
TB = 4
T = B // TB
P = 128
KR = CC - P
FF = 1024
BIG = 2.0 ** 126
HUGE = 3.0e38
EPS = 1e-5
SLOTS = 5
PASSED = {}

PE_PLAN = {0: "OT", 1: "WO", 2: "T3", 3: "XT", 4: "Q", 5: "H", 6: "T", 7: "G", 8: "QK", 9: "VR",
           10: "O2", 11: "FF", 12: "T2", 14: "ST", 15: "Y", 18: "YT", 19: "ACC"}
STAGE_SLOT = {name: slot for slot, name in PE_PLAN.items()}


def need(engine, semaphore, value):
    if isinstance(value, int) and value <= 0:
        return
    engine.wait_ge(semaphore, value)


def apart(engine, *waits):
    waits = [w for w in waits if not (isinstance(w[1], int) and w[1] <= 0)]
    for semaphore, value in waits:
        engine.wait_ge(semaphore, value)
    if any(not isinstance(value, int) for _, value in waits):
        engine.sem_inc(PASSED[engine], 1)


def block_kernel(nc, d, out, vl_dram):
    with ExitStack() as ctx:
        def sb(name, shape, dt=F32):
            return ctx.enter_context(nc.sbuf_tensor(name, shape, dt))

        def ps(name, shape):
            return ctx.enter_context(nc.psum_tensor(name, shape, F32))

        sems = {}

        def sem(name):
            if name not in sems:
                sems[name] = ctx.enter_context(nc.semaphore(name))
            return sems[name]

        ident = sb("ident", [P, P])
        ident16 = sb("ident16", [P, P], F16)
        ones = sb("ones", [P, P])
        halves = sb("halves", [P, 2, G * TB])
        cos_t = sb("cos_t", [P, 2 * C])
        sin_t = sb("sin_t", [P, 2 * C])
        decay = sb("decay", [P, 2, 2 * P])
        head_mask = sb("head_mask", [P, A])
        batch_mask = sb("batch_mask", [P, TB])
        wq = sb("wq", [P, 2, C])
        wkv32 = sb("wkv32", [P, 4, C])
        wkv_hi = sb("wkv_hi", [P, 4, C], F16)
        wkv_lo = sb("wkv_lo", [P, 4, C], F16)
        wo = sb("wo", [64, A, C])
        qkvff_n = sb("qkvff_n", [P, 10, C])
        gated_n = sb("gated_n", [P, 2, C])
        proj_n = sb("proj_n", [P, 2, C])
        ff_n = sb("ff_n", [P, 2, 2 * C])
        w1_n = sb("w1_n", [P, 8, C])
        w2_n = sb("w2_n", [P, 2, FF])
        rms = sb("rms", [P, 2])
        b_gate = sb("b_gate", [64, A])
        gn_w = sb("gn_w", [64, A])
        gn_b = sb("gn_b", [64, A])
        gn_w2 = sb("gn_w2", [64, A])
        gn_b2 = sb("gn_b2", [64, A])
        b1 = sb("b1", [P, 8])
        b_proj = sb("b_proj", [P, C])
        b2 = sb("b2", [P, C])
        qkvff_hi = sb("qkvff_hi", [P, 2, 5 * C], F16)
        qkvff_lo = sb("qkvff_lo", [P, 2, 5 * C], F16)
        gated_hi = sb("gated_hi", [P, 2, C], F16)
        gated_lo = sb("gated_lo", [P, 2, C], F16)
        wff = sb("wff", [P, 4, C])
        wproj = sb("wproj", [64, A, C])
        w1_t = sb("w1_t", [P, 8, C], F16)
        w2_t = sb("w2_t", [P, 2, FF], F16)
        below = sb("below", [P, 2 * FF], F16)
        scratch = sb("scratch", [P, 2 * FF])
        w1 = sb("w1", [P, 2, FF], F16)
        w2 = sb("w2", [P, 8, C], F16)
        abs_sum = sb("abs_sum", [P, 2])
        mean_abs = sb("mean_abs", [P, 2])
        thr_up = sb("thr_up", [P, 2])
        thr_down = sb("thr_down", [P, 2])

        last_n = sb("last_n", [B, CC])
        last_t = sb("last_t", [P, 2, B])
        k_last = sb("k_last", [P, 2, B])
        v_last = sb("v_last", [B, C])
        vl = sb("vl", [P, B, 64])

        xq = sb("xq", [P, C])
        q_stats = sb("q_stats", [P, 6])
        q_mv = sb("q_mv", [P, 2])
        q_ve = sb("q_ve", [P, 1])
        q_rstd = sb("q_rstd", [P, 1])
        xnq = sb("xnq", [P, C])
        xq_t = sb("xq_t", [P, 2, P])
        q_t = sb("q_t", [P, 2, P])
        qbd = sb("qbd", [P, 2, TB, A, S])
        ctx_s = sb("ctx_s", [P, TB, 2, CC + KR])
        mask_u8 = sb("mask_u8", [P, TB, M], U8)
        mask_b = sb("mask_b", [P, 2, M], BF16)
        c_hi = sb("c_hi", [P, 2, 4, P], F16)
        c_lo = sb("c_lo", [P, 2, 2, P], F16)
        k_t = sb("k_t", [P, 2, 2, M])
        v_s = sb("v_s", [P, 2, 2, C])
        sm = sb("sm", [P, G, M])
        neg_max = sb("neg_max", [P, G])
        prob = sb("prob", [P, 2, G, M])
        sums = sb("sums", [P, TB, G])
        prob_t = sb("prob_t", [P, 2, 4, P])
        rsum = sb("rsum", [P, 2, G])
        last_pv = sb("last_pv", [P, 2, G, HD])
        o_raw = sb("o_raw", [P, 2, G, HD])
        o_c = sb("o_c", [P, TB, 64])

        o_t = sb("o_t", [64, A, TB, S])
        xr = sb("xr", [P, C])
        x1 = sb("x1", [P, C])
        stats = sb("stats", [P, 6])
        mv = sb("mv", [P, 2])
        var_eps = sb("var_eps", [P, 1])
        rstd = sb("rstd", [P, 1])
        xn = sb("xn", [P, C])
        squares = sb("squares", [P, C])
        sum_sq = sb("sum_sq", [P, 1])
        nrm = sb("nrm", [P, 1])
        nrm_c = sb("nrm_c", [P, 1])
        rnrm = sb("rnrm", [P, 1])
        xu = sb("xu", [P, C])
        x_hi = sb("x_hi", [P, 4, P], F16)
        x_lo = sb("x_lo", [P, 4, P], F16)
        gate_b = sb("gate_b", [64, A, P])
        gate_th = sb("gate_th", [64, A, P])
        gate = sb("gate", [64, A, P])
        gate_w = sb("gate_w", [64, A, P])
        gate_o = sb("gate_o", [64, A, P])
        qk_cos, qk_sin = scratch[:, 0:512], scratch[:, 512:1024]
        qk = scratch[:, 1024:1536].rearrange("p (k n) -> p k n", k=4)
        qk_t = scratch[:, 1536:2048].rearrange("p (k n) -> p k n", k=4)
        rbd = w2_n[:, 0, :].rearrange("p (m b a r) -> p m b a r", m=2, b=TB, a=A)
        vr = sb("vr", [P, C])
        vbd = w2_n[:, 1, :].rearrange("p (g b n) -> p g b n", g=G, b=TB)
        ff_g = sb("ff_g", [P, 4, P])
        st = sb("st", [P, 2, 2, P])
        y_c = sb("y_c", [P, TB, G, HD])
        y_sum = sb("y_sum", [P, TB * G])
        y_mean = sb("y_mean", [P, TB * G])
        y_ctr = sb("y_ctr", [P, TB * G, HD])
        y_sq = sb("y_sq", [P, TB * G, HD])
        y_ss = sb("y_ss", [P, TB * G])
        y_ve = sb("y_ve", [P, TB * G])
        y_rstd = sb("y_rstd", [P, TB * G])
        y_n = sb("y_n", [P, TB * G, HD])
        y_g = sb("y_g", [64, A, TB, S])
        y_t = sb("y_t", [64, A, TB, S])
        x_res = sb("x_res", [P, C])
        x_resb = sb("x_resb", [P, C])
        x2 = sb("x2", [P, C])

        f_stats = sb("f_stats", [P, 6])
        f_mv = sb("f_mv", [P, 2])
        f_ve = sb("f_ve", [P, 1])
        f_rstd = sb("f_rstd", [P, 1])
        f_xn = sb("f_xn", [P, C])
        f_hi = sb("f_hi", [P, 2, P], F16)
        f_lo = sb("f_lo", [P, 2, P], F16)
        h_g = w1_n[:, 0:4, :].rearrange("p k (i n) -> p (k i) n", i=2)
        h_hi = w1_t[:, 0:4, :].rearrange("p k (i n) -> p (k i) n", i=2)
        h_lo = w1_t[:, 4:8, :].rearrange("p k (i n) -> p (k i) n", i=2)
        x2b = sb("x2b", [P, C])
        y_out = sb("y_out", [P, C])

        p_ct = ps("p_ct", [P, 512])
        p_kv = ps("p_kv", [P, 512])
        p_s = [ps("p_s0", [P, 512]), ps("p_s1", [P, 512])]
        p_pt = ps("p_pt", [P, 512])
        p_o = ps("p_o", [P, 512])
        p_r = ps("p_r", [P, 1024])
        r0, r1 = p_r[:, 0:512], p_r[:, 512:1024]

        def ax(ap, n):
            return ap.unsqueeze(2).broadcast_to([ap.shape[0], ap.shape[1], n])

        def y_heads(a):
            return p_r[32 * a:32 * a + 32, :].rearrange("p (g b n) -> p b g n", g=G, b=TB)[:, :, :, 16 * a:16 * a + 16]

        def by_group(w, k):
            return w[:, k, :].rearrange("p (a g e) -> p g a e", g=G, a=A)

        x_rows = d["x"]
        ctx.enter_context(nc.allow_non_contiguous_dma(reason="a few vectors of up to 1024 elements go across partitions"))
        blk = ctx.enter_context(nc.Block())

        def steps(engine, step):
            for t in range(3):
                step(t)
            with engine.Fori(3, T - 1) as t:
                step(t, True)
            for t in range(T - 1, T + 2):
                step(t)

        def runs(stage, t, inside):
            if stage in ("T3", "H", "O2"):
                return (inside or 0 <= t - 2 < T), t - 2
            if stage in ("XT", "Q"):
                return (inside or t + 1 < T), t + 1
            return (inside or 0 <= t - 1 < T), t - 1

        @blk.sync
        def _(sp):
            sp.dma_start(last_n[:, :], d["ctx"][:, MF, :]).then_inc(sem("last_in"), 16)
            sp.dma_start(ident[:, :], d["ident"]).then_inc(sem("ident_in"), 16)
            for i, w in ((0, "wk"), (2, "wv")):
                sp.dma_start(wkv32[:, i, :], d[w][0:P, :]).then_inc(sem("wkv_in"), 16)
                sp.dma_start(wkv32[0:64, i + 1, :], d[w][P:CC, :]).then_inc(sem("wkv_in"), 16)
                sp.dma_start(wkv32[64:P, i + 1, :], d[w][P:CC, :]).then_inc(sem("wkv_in"), 16)
            sp.dma_start(wq[:, :, :], d["wq"].rearrange("(k p) n -> p k n", p=P)).then_inc(sem("wq_in"), 16)
            sp.dma_start(head_mask[:, :], d["head_mask"]).then_inc(sem("masks_in"), 16)
            sp.dma_start(batch_mask[:, :], d["batch_mask"]).then_inc(sem("masks_in"), 16)

            def load_batch(t, b):
                need(sp, sem("ct_done"), 4 * t + b - 3)
                need(sp, sem("mask_ready"), 4 * t + b - 3)
                n = 4 * t + b
                src = d["ctx"][bass.ds(n, 1), 0:MF, :].rearrange("o (j p) c -> p (o j) c", p=P)
                sp.dma_start(ctx_s[:, b, :, 0:CC], src).then_inc(sem(f"ctx_in{b}"), 16)
                sp.dma_start(ctx_s[:, b, :, CC:], src[:, :, P:CC]).then_inc(sem(f"ctx_in{b}"), 16)
                sp.dma_start(mask_u8[:, b, :],
                             d["mask"][bass.ds(n, 1), :].broadcast_to([P, M])).then_inc(sem(f"ctx_in{b}"), 16)

            def load_xq(t):
                need(sp, sem("xnq_ready"), t)
                sp.dma_start(xq[:, :], x_rows[bass.ds(t * P, P), :]).then_inc(sem("xq_in"), 16)

            load_xq(0)
            for b in range(TB):
                load_batch(0, b)

            sp.wait_ge(sem("v_last_ready"), 1)
            sp.dma_start(vl_dram[:, :], v_last[:, :]).then_inc(sem("vl_out"), 16)
            sp.wait_ge(sem("vl_out"), 16)
            for a in range(A):
                sp.dma_start(vl[32 * a:32 * a + 32, :, :],
                             vl_dram[:, 64 * a:64 * a + 64].unsqueeze(0).broadcast_to([S, B, 64])
                             ).then_inc(sem("vl_in"), 16)
            for g in range(G):
                sp.dma_start(wo[16 * g:16 * g + 16, :, :],
                             d["wo"][64 * g:64 * g + 64, :].rearrange("(a e) n -> e a n", a=A)
                             ).then_inc(sem("wo_in"), 16)
            sp.dma_start(rms[:, :], d["rms"].rearrange("(k p) -> p k", p=P)).then_inc(sem("w_in0"), 16)
            sp.dma_start(qkvff_n[:, :, :], d["qkvff"].rearrange("(k p) n -> p k n", p=P)).then_inc(sem("w_in0"), 16)
            sp.dma_start(gated_n[:, :, :], d["gated"].rearrange("(k p) n -> p k n", p=P)).then_inc(sem("w_in1"), 16)
            sp.dma_start(ff_n[:, :, :], d["wff"].rearrange("(k p) n -> p k n", p=P)).then_inc(sem("w_in1"), 16)
            for i in range(2):
                for a in range(A):
                    src = d["proj"][P * i:P * i + P, :].rearrange("p (g a e) -> p a g e", g=G, a=A)[:, a, :, :]
                    sp.dma_start(proj_n[:, i, 64 * a:64 * a + 64].rearrange("p (g e) -> p g e", g=G), src
                                 ).then_inc(sem("w_in1"), 16)
            sp.dma_start(w1_n[:, :, :], d["w1"].rearrange("(k p) n -> p k n", p=P)).then_inc(sem("w_in2"), 16)
            sp.dma_start(w2_n[:, :, :], d["w2"].rearrange("(k p) n -> p k n", p=P)).then_inc(sem("w_in2"), 16)
            for name, tile in (("cos_t", cos_t), ("sin_t", sin_t)):
                sp.dma_start(tile[:, :], d[name]).then_inc(sem("tab_in"), 16)
            sp.dma_start(decay[:, :, :], d["decay"].rearrange("p (h n) -> p h n", h=2)).then_inc(sem("tab_in"), 16)
            for name, tile in (("b_proj", b_proj), ("b2", b2)):
                sp.dma_start(tile[:, :], d[name].unsqueeze(0).broadcast_to([P, C])).then_inc(sem("tab_in"), 16)
            sp.dma_start(b1[:, :], d["b1"].rearrange("(k p) -> p k", p=P)).then_inc(sem("tab_in"), 16)
            for name, tile in (("b_gate", b_gate), ("gn_w", gn_w), ("gn_b", gn_b)):
                for g in range(G):
                    sp.dma_start(tile[16 * g:16 * g + 16, :],
                                 d[name][64 * g:64 * g + 64].rearrange("(a e) -> e a", a=A)
                                 ).then_inc(sem("vec_in"), 16)
            load_xq(1)

            def step(t, inside=False):
                for b in range(TB):
                    if inside or t + 1 < T:
                        load_batch(t + 1, b)
                    if b == 0 and (inside or 0 <= t - 1 < T):
                        need(sp, sem("x1_ready"), t - 1)
                        sp.dma_start(xr[:, :], x_rows[bass.ds((t - 1) * P, P), :]).then_inc(sem("xr_in"), 16)
                    if b == 1 and (inside or t + 2 < T):
                        load_xq(t + 2)
                    if b == 2 and (inside or 0 <= t - 2 < T):
                        sp.wait_ge(sem("y_ready"), t - 1)
                        sp.dma_start(out[bass.ds((t - 2) * P, P), :], y_out[:, :]).then_inc(sem("stored"), 16)

            for t in range(3):
                step(t)
            with sp.Fori(3, T - 2) as t:
                step(t, True)
            for t in range(T - 2, T + 2):
                step(t)
            sp.wait_ge(sem("stored"), 16 * T)

        @blk.tensor
        def _(pe):
            PASSED[pe] = sem("pe_passed")
            mm = nc.tensor.matmul

            pe.wait_ge(sem("ident_in"), 16)
            pe.wait_ge(sem("last_in"), 16)
            nc.tensor.transpose(r0[:, 0:B], last_n[:, 0:P], ident[0:B, 0:B])
            nc.tensor.transpose(r0[0:KR, B:2 * B], last_n[:, P:CC], ident[0:B, 0:B]).then_inc(sem("last_tr"), 1)
            pe.wait_ge(sem("wkv_in"), 96)
            pe.wait_ge(sem("last_t_ready"), 2)
            for m in range(2):
                mm(r1[:, B * m:B * m + B], wkv32[:, 0, P * m:P * m + P], last_t[:, 0, :], start=True, stop=False)
                mm(r1[:, B * m:B * m + B], wkv32[0:64, 1, P * m:P * m + P], last_t[0:64, 1, :], start=False, stop=True)
            mm(r1[0:B, 256:512], last_t[:, 0, :], wkv32[:, 2, :], start=True, stop=False)
            mm(r1[0:B, 256:512], last_t[0:64, 1, :], wkv32[0:64, 3, :], start=False, stop=True).then_inc(sem("last_kv"), 1)

            def context_transposed(t, b):
                n = 4 * t + b
                pe.wait_ge(sem(f"ctx_in{b}"), 48 * (t + 1))
                need(pe, sem("hi_done"), n)
                need(pe, sem("lo_done"), 2 * n)
                for j in range(2):
                    nc.tensor.transpose(p_ct[:, P * j:P * j + P], ctx_s[:, b, j, 0:P], ident[:, :])
                for j in range(2):
                    last = nc.tensor.transpose(p_ct[:, 256 + P * j:256 + P * j + P], ctx_s[:, b, j, P:], ident[:, :])
                last.then_inc(sem("ct_done"), 1)

            def keys(t, b):
                n, par = 4 * t + b, b % 2
                pe.wait_ge(sem("hi_done"), n + 1)
                pe.wait_ge(sem("lo_done"), 2 * n + 2)
                if isinstance(t, int) and n == 0:
                    pe.wait_ge(sem("wkv_split"), 2)
                need(pe, sem("v_ready"), n)
                for m in range(2):
                    o = p_kv[:, 256 * m:256 * m + 256]
                    c = slice(P * m, P * m + P)
                    mm(o, wkv_hi[:, 0, c], c_hi[:, par, 0:2, :], start=True, stop=False)
                    mm(o, wkv_lo[:, 0, c], c_hi[:, par, 0:2, :], start=False, stop=False)
                    mm(o, wkv_hi[:, 0, c], c_lo[:, par, :, :], start=False, stop=False)
                    mm(o, wkv_hi[:, 1, c], c_hi[:, par, 2:4, :], start=False, stop=False)
                    last = mm(o, wkv_lo[0:64, 1, c], c_hi[0:64, par, 2:4, :], start=False, stop=True)
                last.then_inc(sem("k_done"), 1)

            def values(t, b):
                n, par = 4 * t + b, b % 2
                pe.wait_ge(sem("kt_ready"), n + 1)
                for j in range(2):
                    o = p_kv[:, 256 * j:256 * j + 256]
                    mm(o, c_hi[:, par, j, :], wkv_hi[:, 2, :], start=True, stop=False)
                    mm(o, c_hi[:, par, j, :], wkv_lo[:, 2, :], start=False, stop=False)
                    mm(o, c_lo[:, par, j, :], wkv_hi[:, 2, :], start=False, stop=False)
                    mm(o, c_hi[:, par, 2 + j, :], wkv_hi[:, 3, :], start=False, stop=False)
                    last = mm(o, c_hi[0:64, par, 2 + j, :], wkv_lo[0:64, 3, :], start=False, stop=True)
                last.then_inc(sem("v_done"), 1)

            def scores(t, b, g):
                n, par, m, half = 4 * t + b, b % 2, g // 2, g % 2
                if g == 0:
                    pe.wait_ge(sem("qbd_ready"), n + 1)
                    pe.wait_ge(sem("kt_ready"), n + 1)
                    pe.wait_ge(sem("klast_ready"), n + 1)
                need(pe, sem("masked"), 4 * n + g - 1)
                rows = slice(64 * half, 64 * half + 64)
                mm(p_s[half][:, 0:M], qbd[rows, m, b, :, :], k_t[rows, par, m, :],
                   start=True, stop=True).then_inc(sem("s_done"), 1)

            def probs_transposed(t, b, pair):
                n, par = 4 * t + b, b % 2
                pe.wait_ge(sem("exp_done"), 4 * n + 2 * pair + 2)
                if pair == 0:
                    need(pe, sem("pt1_ready"), n)
                else:
                    pe.wait_ge(sem("pt0_ready"), n + 1)
                for i in range(2):
                    for j in range(2):
                        at = P * (2 * i + j)
                        last = nc.tensor.transpose(p_pt[:, at:at + P], prob[:, par, 2 * pair + i, P * j:P * j + P],
                                                   ident[:, :])
                last.then_inc(sem("pt_done"), 1)

            def attend(t, b, pair):
                n, par = 4 * t + b, b % 2
                pe.wait_ge(sem(f"pt{pair}_ready"), n + 1)
                if pair == 0:
                    pe.wait_ge(sem("v_ready"), n + 1)
                    if par == 0:
                        need(pe, sem("o_taken"), 4 * (2 * t + b // 2))
                for i in range(2):
                    g = 2 * pair + i
                    for j in range(2):
                        last = mm(p_o[:, 256 * par + 64 * g:256 * par + 64 * g + 64], prob_t[:, pair, 2 * i + j, :],
                                  v_s[:, par, j, 64 * g:64 * g + 64], start=(j == 0), stop=(j == 1))
                last.then_inc(sem("pv_done"), 1)

            def OT(u):
                if isinstance(u, int) and u == 0:
                    pe.wait_ge(sem("q_t_ready"), 2)
                apart(pe, (sem("oc_ready"), 2 * u + 2))
                for b in range(TB):
                    last = nc.tensor.transpose(r0[0:64, P * b:P * b + P], o_c[:, b, :], ident[:, :])
                last.then_inc(sem("ot_done"), 1)

            def WO(u):
                if isinstance(u, int) and u == 0:
                    pe.wait_ge(sem("wo_in"), 64)
                pe.wait_ge(sem("ot_ready"), u + 1)
                need(pe, sem("x2_ready"), u)
                for a in range(A):
                    last = mm(r1[:, 0:C], o_t[:, a, :, :], wo[:, a, :], start=(a == 0), stop=(a == A - 1))
                last.then_inc(sem("wo_done"), 1)

            def T3(u):
                pe.wait_ge(sem("f_xn_ready"), u + 1)
                for k in range(2):
                    last = nc.tensor.transpose(r0[:, P * k:P * k + P], f_xn[:, P * k:P * k + P], ident[:, :])
                last.then_inc(sem("t3_done"), 1)

            def XT(u):
                pe.wait_ge(sem("xnq_ready"), u + 1)
                need(pe, sem("x1_ready"), u - 1)
                for k in range(2):
                    last = nc.tensor.transpose(r1[:, P * k:P * k + P], xnq[:, P * k:P * k + P], ident[:, :])
                last.then_inc(sem("xt_done"), 1)

            def Q(u):
                pe.wait_ge(sem("xq_t_ready"), u + 1)
                need(pe, sem("f_lo_ready"), u - 2)
                need(pe, sem("f_hi_ready"), u - 2)
                for m in range(2):
                    for k in range(2):
                        last = mm(r0[:, P * m:P * m + P], wq[:, k, P * m:P * m + P], xq_t[:, k, :],
                                  start=(k == 0), stop=(k == 1))
                last.then_inc(sem("q_done"), 1)

            def H1(u, more):
                pe.wait_ge(sem("f_hi_ready"), u + 1)
                pe.wait_ge(sem("f_lo_ready"), u + 1)
                if more:
                    pe.wait_ge(sem("q_t_ready"), u + 4)
                elif u + 1 < T:
                    pe.wait_ge(sem("x1_ready"), u + 2)
                for m in range(8):
                    o = p_r[:, P * m:P * m + P]
                    for k in range(2):
                        mm(o, w1[:, k, P * m:P * m + P], f_hi[:, k, :], start=(k == 0), stop=False)
                        last = mm(o, w1[:, k, P * m:P * m + P], f_lo[:, k, :], start=False, stop=(k == 1))
                    if m % 4 == 3:
                        last.then_inc(sem("h_done"), 1)

            def TR(u):
                pe.wait_ge(sem("xn_ready"), u + 1)
                pe.wait_ge(sem("xu_ready"), u + 1)
                need(pe, sem("h_g_ready"), 8 * u)
                if isinstance(u, int) and u == 0:
                    pe.wait_ge(sem("q_t_ready"), 3)
                for k in range(2):
                    nc.tensor.transpose(r0[:, P * k:P * k + P], xn[:, P * k:P * k + P], ident[:, :])
                for k in range(2):
                    last = nc.tensor.transpose(r0[:, 256 + P * k:256 + P * k + P], xu[:, P * k:P * k + P], ident[:, :])
                last.then_inc(sem("tr_done"), 1)

            def GA(u):
                pe.wait_ge(sem("x_hi_ready"), u + 1)
                pe.wait_ge(sem("x_lo_ready"), u + 1)
                for a in range(A):
                    o = r1[0:64, P * a:P * a + P]
                    for k in range(2):
                        w_hi, w_lo = gated_hi[:, k, 64 * a:64 * a + 64], gated_lo[:, k, 64 * a:64 * a + 64]
                        mm(o, w_hi, x_hi[:, k, :], start=(k == 0), stop=False)
                        mm(o, w_lo, x_hi[:, k, :], start=False, stop=False)
                        last = mm(o, w_hi, x_lo[:, k, :], start=False, stop=(k == 1))
                last.then_inc(sem("g_done"), 1)

            def three(o, cols):
                for k in range(2):
                    mm(o, x_hi[:, 2 + k, :], qkvff_hi[:, k, cols], start=(k == 0), stop=False)
                    mm(o, x_hi[:, 2 + k, :], qkvff_lo[:, k, cols], start=False, stop=False)
                    last = mm(o, x_lo[:, 2 + k, :], qkvff_hi[:, k, cols], start=False, stop=(k == 1))
                return last

            def QK(u):
                three(r0[:, :], slice(0, 2 * C)).then_inc(sem("qk_done"), 1)

            def VR(u):
                pe.wait_ge(sem("gate_b_ready"), u + 1)
                three(r1[:, 0:C], slice(2 * C, 3 * C)).then_inc(sem("vr_done"), 1)

            def O2(u):
                pe.wait_ge(sem("h_hi_ready"), u + 1)
                pe.wait_ge(sem("h_lo_ready"), u + 1)
                need_next = u + 2
                if not (isinstance(u, int) and u == T - 1):
                    pe.wait_ge(sem("qk_taken"), 3 * need_next)
                for f in range(8):
                    mm(r0[:, 0:C], h_hi[:, f, :], w2[:, f, :], start=(f == 0), stop=False)
                    last = mm(r0[:, 0:C], h_lo[:, f, :], w2[:, f, :], start=False, stop=(f == 7))
                last.then_inc(sem("o2_done"), 1)

            def FFN(u):
                pe.wait_ge(sem("vr_ready"), u + 1)
                for e in range(4):
                    o = r1[:, P * e:P * e + P]
                    c = slice(3 * C + P * e, 3 * C + P * e + P)
                    for k in range(2):
                        mm(o, qkvff_hi[:, k, c], x_hi[:, 2 + k, :], start=(k == 0), stop=False)
                        mm(o, qkvff_lo[:, k, c], x_hi[:, 2 + k, :], start=False, stop=False)
                        last = mm(o, qkvff_hi[:, k, c], x_lo[:, 2 + k, :], start=False, stop=(k == 1))
                last.then_inc(sem("ff_done"), 1)

            def T2(u):
                pe.wait_ge(sem("qk_ready"), u + 1)
                need(pe, sem("y_ready"), u)
                pe.wait_ge(sem("qk_taken"), 3 * (u + 1))
                for i in range(4):
                    last = nc.tensor.transpose(r0[:, P * i:P * i + P], qk[:, i, :], ident[:, :])
                last.then_inc(sem("t2_done"), 1)

            def ST(u):
                apart(pe, (sem("rbd_ready"), u + 1), (sem("ff_g_ready"), u + 1))
                for half in range(2):
                    rows = slice(64 * half, 64 * half + 64)
                    for b in range(TB):
                        for m in range(2):
                            last = mm(p_r[32 * b:32 * b + 32, 512 * half + P * m:512 * half + P * m + P],
                                      qk_t[rows, 2 + m, 32 * b:32 * b + 32], rbd[rows, m, b, :, :],
                                      start=True, stop=True)
                last.then_inc(sem("st_done"), 1)

            def Y(u):
                pe.wait_ge(sem("st_ready"), 2 * (u + 1))
                pe.wait_ge(sem("vbd_ready"), u + 1)
                for g in range(G):
                    m, half = g // 2, g % 2
                    last = mm(p_r[:, 256 * g:256 * g + 256], st[:, half, m, :], vbd[:, g, :, :],
                              start=True, stop=True)
                last.then_inc(sem("y_done"), 1)

            def YT(u):
                apart(pe, (sem("y_n_ready"), u + 1))
                for b in range(TB):
                    last = nc.tensor.transpose(r0[0:64, P * b:P * b + P], y_n[:, 4 * b:4 * b + 4, :], ident[:, :])
                last.then_inc(sem("yt_done"), 1)

            def ACC(u):
                for e in range(4):
                    mm(r1[:, 0:C], ff_g[:, e, :], wff[:, e, :], start=(e == 0), stop=False)
                pe.wait_ge(sem("y_t_ready"), u + 1)
                for a in range(A):
                    last = mm(r1[:, 0:C], y_t[:, a, :, :], wproj[:, a, :], start=False, stop=(a == A - 1))
                last.then_inc(sem("acc_done"), 1)

            def weights(job):
                if job == 0:
                    pe.wait_ge(sem("w_in0"), 32)
                    pe.wait_ge(sem("q_t_ready"), 1)
                    pe.wait_ge(sem("k_last_ready"), 1)
                    pe.wait_ge(sem("v_last_ready"), 1)
                need(pe, sem("job_hi"), job - (job > 9))
                need(pe, sem("job_lo"), job)
                if job < 6:
                    k, lot = job // 3, job % 3
                    for i in range(4 if lot < 2 else 2):
                        last = nc.tensor.transpose(r0[:, P * i:P * i + P], qkvff_n[:, 4 * lot + i, P * k:P * k + P],
                                                   ident[:, :])
                elif job == 6:
                    pe.wait_ge(sem("w_in1"), 160)
                    for k in range(2):
                        for i in range(2):
                            last = nc.tensor.transpose(r0[:, 256 * k + P * i:256 * k + P * i + P],
                                                       gated_n[:, i, P * k:P * k + P], ident[:, :])
                elif job == 7:
                    for e in range(4):
                        for i in range(2):
                            last = nc.tensor.transpose(p_r[:, 256 * e + P * i:256 * e + P * i + P],
                                                       ff_n[:, i, P * e:P * e + P], ident[:, :])
                elif job == 8:
                    for a in range(A):
                        for i in range(2):
                            last = nc.tensor.transpose(p_r[0:64, 256 * a + P * i:256 * a + P * i + P],
                                                       proj_n[:, i, 64 * a:64 * a + 64], ident[:, :])
                elif job == 9:
                    pe.wait_ge(sem("abs_ready"), 2)
                    pe.wait_ge(sem("ones_ready"), 1)
                    last = mm(r0[:, 0:2], ones[:, :], abs_sum[:, :], start=True, stop=True)
                elif job < 12:
                    k = job - 10
                    pe.wait_ge(sem("ident16_ready"), 1)
                    o = r0.bitcast(F16)
                    for i in range(8):
                        last = nc.tensor.transpose(o[:, P * i:P * i + P], w1_t[:, i, P * k:P * k + P], ident16[:, :])
                else:
                    k = job - 12
                    o = r0.bitcast(F16)
                    for f in range(4):
                        for i in range(2):
                            at = 256 * f + P * i
                            last = nc.tensor.transpose(o[:, at:at + P],
                                                       w2_t[:, i, P * (4 * k + f):P * (4 * k + f) + P], ident16[:, :])
                last.then_inc(sem("job_done"), 1)

            stages = {"OT": OT, "WO": WO, "T3": T3, "XT": XT, "Q": Q, "T": TR, "G": GA, "QK": QK, "VR": VR,
                      "O2": O2, "FF": FFN, "T2": T2, "ST": ST, "Y": Y, "YT": YT, "ACC": ACC}

            pe.wait_ge(sem("k_last_ready"), 1)
            XT(0)
            Q(0)
            context_transposed(0, 0)
            keys(0, 0)
            values(0, 0)
            context_transposed(0, 1)

            def step(t, inside=False):
                has_x = inside or t < T

                def after(b, k):
                    later = (t, b + k) if b + k < TB else (t + 1, b + k - TB)
                    return later if inside or later[0] < T else None

                for slot in range(TB * SLOTS):
                    b, part = slot // SLOTS, slot % SLOTS
                    if has_x:
                        if part == 0:
                            scores(t, b, 0)
                            scores(t, b, 1)
                        elif part == 1 and after(b, 1):
                            keys(*after(b, 1))
                        elif part == 2:
                            scores(t, b, 2)
                            scores(t, b, 3)
                        elif part == 3:
                            probs_transposed(t, b, 0)
                            if after(b, 1):
                                values(*after(b, 1))
                        elif part == 4:
                            attend(t, b, 0)
                            probs_transposed(t, b, 1)
                            if after(b, 2):
                                context_transposed(*after(b, 2))
                            attend(t, b, 1)
                    if not inside and t == 0 and 1 <= slot < 15:
                        weights(slot - 1)
                    name = PE_PLAN.get(slot)
                    if not inside and t == 0 and name in ("XT", "Q"):
                        continue
                    if name:
                        on, u = runs(name, t, inside)
                        if on and name == "H":
                            H1(u, inside or t + 1 < T)
                        elif on:
                            stages[name](u)
                if not inside and t == 0:
                    pe.wait_ge(sem("job_hi"), 13)
                    pe.wait_ge(sem("job_lo"), 14)
                    XT(1)
                    Q(1)

            steps(pe, step)

        @blk.scalar
        def _(act):
            def copy(o, i):
                return nc.scalar.activation(o, i, ACT.Copy)

            def context_high(t, b):
                n, par = 4 * t + b, b % 2
                act.wait_ge(sem("ct_done"), n + 1)
                need(act, sem("v_done"), n - 1)
                copy(c_hi[:, par, :, :], p_ct[:, :].rearrange("p (j n) -> p j n", j=4)).then_inc(sem("hi_done"), 1)

            def keys_out(t, b):
                n, par = 4 * t + b, b % 2
                act.wait_ge(sem("k_done"), n + 1)
                need(act, sem("s_done"), 4 * (n - 1))
                copy(k_t[:, par, :, 0:MF], p_kv[:, :].rearrange("p (m n) -> p m n", m=2)).then_inc(sem("kt_ready"), 1)

            def exps(t, b, g):
                n, par = 4 * t + b, b % 2
                act.wait_ge(sem("masked"), 4 * n + g + 1)
                if g == 0:
                    need(act, sem("pt_done"), 2 * (n - 1))
                    need(act, sem("last_pv_ready"), n - 1)
                    if par == 0:
                        need(act, sem("rsum_ready"), 2 * t + b // 2 - 1)
                nc.scalar.activation(prob[:, par, g, :], sm[:, g, :], ACT.Exp, bias=neg_max[:, g:g + 1], scale=-1.0,
                                     accum_out=sums[:, b, g:g + 1]).then_inc(sem("exp_done"), 1)

            def probs_out(t, b):
                n = 4 * t + b
                act.wait_ge(sem("pt_done"), 2 * n + 2)
                need(act, sem("pv_done"), 2 * n)
                copy(prob_t[:, 1, :, :], p_pt[:, :].rearrange("p (j n) -> p j n", j=4)).then_inc(sem("pt1_ready"), 1)

            def XT(u):
                act.wait_ge(sem("xt_done"), u + 1)
                need(act, sem("q_done"), u)
                copy(xq_t[:, :, :], r1[:, 0:C].rearrange("p (k n) -> p k n", k=2)).then_inc(sem("xq_t_ready"), 1)

            def Q(u):
                act.wait_ge(sem("q_done"), u + 1)
                need(act, sem("qbd_ready"), 4 * u)
                copy(q_t[:, :, :], r0[:, 0:C].rearrange("p (k n) -> p k n", k=2)).then_inc(sem("q_t_ready"), 1)

            def T3(u):
                act.wait_ge(sem("t3_done"), u + 1)
                need(act, sem("h_done"), 2 * u)
                copy(f_hi[:, :, :], r0[:, 0:C].rearrange("p (k n) -> p k n", k=2)).then_inc(sem("f_hi_ready"), 1)

            def H1(u):
                need(act, sem("h_hi_ready"), u)
                need(act, sem("h_lo_ready"), u)
                for m in range(8):
                    if m % 4 == 0:
                        act.wait_ge(sem("h_done"), 2 * u + 1 + m // 4)
                    nc.scalar.activation(h_g[:, m, :], p_r[:, P * m:P * m + P], ACT.Gelu,
                                         bias=b1[:, m:m + 1]).then_inc(sem("h_g_ready"), 1)

            def squares_sum(u):
                act.wait_ge(sem("xn_ready"), u + 1)
                need(act, sem("nrm_ready"), u)
                nc.scalar.activation(squares[:, :], xn[:, :], ACT.Square,
                                     accum_out=sum_sq[:, :]).then_inc(sem("ss_ready"), 1)

            def TR(u):
                act.wait_ge(sem("tr_done"), u + 1)
                need(act, sem("ff_done"), u)
                copy(x_hi[:, :, :], r0[:, :].rearrange("p (k n) -> p k n", k=4)).then_inc(sem("x_hi_ready"), 1)

            def GA(u):
                act.wait_ge(sem("gate_b_ready"), u + 1)
                need(act, sem("gate_ready"), u)
                nc.scalar.activation(gate_th[:, :, :], gate_b[:, :, :], ACT.Tanh,
                                     scale=0.5).then_inc(sem("gate_th_ready"), 1)

            def VR(u):
                act.wait_ge(sem("vr_done"), u + 1)
                need(act, sem("vbd_ready"), u)
                copy(vr[:, :], r1[:, 0:C]).then_inc(sem("vr_ready"), 1)

            def FFN(u):
                act.wait_ge(sem("ff_done"), u + 1)
                need(act, sem("acc_done"), u)
                nc.scalar.activation(ff_g[:, :, :], r1[:, :].rearrange("p (k n) -> p k n", k=4),
                                     ACT.Gelu).then_inc(sem("ff_g_ready"), 1)

            def T2(u):
                act.wait_ge(sem("t2_done"), u + 1)
                need(act, sem("st_done"), u)
                need(act, sem("rbd_ready"), u)
                copy(qk_t[:, :, :], r0[:, :].rearrange("p (k n) -> p k n", k=4)).then_inc(sem("qk_t_ready"), 1)

            def Y(u):
                act.wait_ge(sem("y_done"), u + 1)
                need(act, sem("y_ctr_ready"), u)
                for a in range(2):
                    copy(y_c[32 * a:32 * a + 32, :, :, :], y_heads(a)).then_inc(sem("y_c_act"), 1)

            def y_squares(u):
                act.wait_ge(sem("y_ctr_ready"), u + 1)
                need(act, sem("y_ss_ready"), u)
                nc.scalar.activation(y_sq[:, :, :], y_ctr[:, :, :], ACT.Square).then_inc(sem("y_sq_ready"), 1)

            def weights(job):
                act.wait_ge(sem("job_done"), job + 1)
                if job < 6:
                    k, lot = job // 3, job % 3
                    w = 512 if lot < 2 else 256
                    last = nc.scalar.activation(qkvff_hi[:, k, 512 * lot:512 * lot + w], r0[:, 0:w], ACT.Copy,
                                                scale=rms[:, k:k + 1])
                elif job == 6:
                    for k in range(2):
                        last = copy(by_group(gated_hi, k), r0[:, 256 * k:256 * k + 256].rearrange("p (g a e) -> p g a e", g=G, a=A))
                elif job == 7:
                    last = copy(wff[:, 0:2, :], r0[:, :].rearrange("p (k n) -> p k n", k=2))
                elif job == 8:
                    last = copy(wproj[:, 0:2, :], r0[0:64, :].rearrange("p (k n) -> p k n", k=2))
                elif job == 9:
                    return
                elif job < 12:
                    last = copy(w1[:, job - 10, 0:512], r0.bitcast(F16)[:, 0:512])
                else:
                    last = copy(w2[:, 4 * (job - 12):4 * (job - 12) + 2, :],
                                r0.bitcast(F16)[:, 0:512].rearrange("p (k n) -> p k n", k=2))
                last.then_inc(sem("job_hi"), 1)

            act.wait_ge(sem("wkv_in"), 96)
            copy(wkv_hi[:, :, :], wkv32[:, :, :]).then_inc(sem("wkv_split"), 1)
            act.wait_ge(sem("v_last_ready"), 1)
            copy(k_last[:, :, :], r1[:, 0:2 * B].rearrange("p (m n) -> p m n", m=2)).then_inc(sem("k_last_ready"), 1)
            XT(0)
            Q(0)
            context_high(0, 0)
            keys_out(0, 0)
            context_high(0, 1)

            stages = {0: [], STAGE_SLOT["T3"]: [("T3", T3)], STAGE_SLOT["XT"]: [("XT", XT)],
                      STAGE_SLOT["Q"]: [("T", squares_sum), ("Q", Q)], STAGE_SLOT["H"]: [("H", H1)],
                      STAGE_SLOT["T"]: [("T", TR)], STAGE_SLOT["G"]: [("G", GA)], STAGE_SLOT["VR"]: [("VR", VR)],
                      STAGE_SLOT["FF"]: [("FF", FFN)], STAGE_SLOT["T2"]: [("T2", T2)],
                      STAGE_SLOT["Y"]: [("Y", Y)], STAGE_SLOT["Y"] + 1: [("Y", y_squares)]}

            def step(t, inside=False):
                has_x = inside or t < T

                def after(b, k):
                    later = (t, b + k) if b + k < TB else (t + 1, b + k - TB)
                    return later if inside or later[0] < T else None

                for slot in range(TB * SLOTS):
                    b, part = slot // SLOTS, slot % SLOTS
                    if has_x:
                        if part == 0:
                            exps(t, b, 0)
                            exps(t, b, 1)
                        elif part == 1 and after(b, 1):
                            keys_out(*after(b, 1))
                        elif part == 2:
                            exps(t, b, 2)
                            exps(t, b, 3)
                        elif part == 4:
                            probs_out(t, b)
                            if after(b, 2):
                                context_high(*after(b, 2))
                    if not inside and t == 0 and slot == 8:
                        act.wait_ge(sem("w_in2"), 32)
                        nc.scalar.activation(scratch[:, :], w1_n[:, :, :].rearrange("p k n -> p (k n)"), ACT.Abs,
                                             accum_out=abs_sum[:, 0:1]).then_inc(sem("abs_ready"), 1)
                        act.wait_ge(sem("abs_ready"), 1)
                        nc.scalar.activation(scratch[:, :], w2_n[:, :, :].rearrange("p k n -> p (k n)"), ACT.Abs,
                                             accum_out=abs_sum[:, 1:2]).then_inc(sem("abs_ready"), 1)
                    if not inside and t == 0 and 1 <= slot < 15:
                        weights(slot - 1)
                    for name, stage in stages.get(slot, []):
                        if not inside and t == 0 and name in ("XT", "Q"):
                            continue
                        on, u = runs(name, t, inside)
                        if on:
                            stage(u)
                if not inside and t == 0:
                    XT(1)
                    Q(1)

            steps(act, step)

        @blk.vector
        def _(dve):
            PASSED[dve] = sem("dve_passed")
            v = nc.vector

            def context_low(t, b):
                n, par = 4 * t + b, b % 2
                dve.wait_ge(sem("hi_done"), n + 1)
                need(dve, sem("v_done"), n - 1)
                v.tensor_tensor(c_lo[:, par, :, :], p_ct[:, 0:256].rearrange("p (j n) -> p j n", j=2),
                                c_hi[:, par, 0:2, :], ALU.subtract).then_inc(sem("lo_done"), 1)
                v.tensor_tensor(c_hi[64:P, par, 2:4, :], p_ct[64:P, 256:512].rearrange("p (j n) -> p j n", j=2),
                                c_hi[64:P, par, 2:4, :], ALU.subtract).then_inc(sem("lo_done"), 1)

            def values_out(t, b):
                n, par = 4 * t + b, b % 2
                dve.wait_ge(sem("v_done"), n + 1)
                need(dve, sem("pv_done"), 2 * (n - 1))
                v.tensor_copy(v_s[:, par, :, :], p_kv[:, :].rearrange("p (j n) -> p j n", j=2)
                              ).then_inc(sem("v_ready"), 1)

            def mask_scores(t, b, g):
                n, par, half = 4 * t + b, b % 2, g % 2
                apart(dve, (sem("s_done"), 4 * n + g + 1), (sem("mask_ready"), n + 1),
                      (sem("exp_done"), 4 * (n - 1) + g + 1))
                v.tensor_tensor_reduce(sm[:, g, :], p_s[half][:, 0:M], mask_b[:, par, :], -(HD ** -0.5), HUGE,
                                       ALU.add, ALU.min, neg_max[:, g:g + 1]).then_inc(sem("masked"), 1)

            def probs_out(t, b):
                n = 4 * t + b
                dve.wait_ge(sem("pt_done"), 2 * n + 1)
                need(dve, sem("pv_done"), 2 * n - 1)
                v.tensor_copy(prob_t[:, 0, :, :], p_pt[:, :].rearrange("p (j n) -> p j n", j=4)
                              ).then_inc(sem("pt0_ready"), 1)

            def output_taken(t, b):
                n, pair = 4 * t + b, 2 * t + b // 2
                dve.wait_ge(sem("exp_done"), 4 * n + 4)
                need(dve, sem("oc_ready"), pair)
                v.reciprocal(rsum[:, :, :], sums[:, b - 1:b + 1, :]).then_inc(sem("rsum_ready"), 1)
                dve.wait_ge(sem("last_pv_ready"), n + 1)
                dve.wait_ge(sem("pv_done"), 2 * n + 2)
                for a in range(A):
                    rows = slice(32 * a, 32 * a + 32)
                    own = p_o[rows, :].rearrange("p (b g n) -> p b g n", b=2, g=G)[:, :, :, 16 * a:16 * a + 16]
                    v.tensor_tensor(o_raw[rows, :, :, :], own, last_pv[rows, :, :, :], ALU.add
                                    ).then_inc(sem("o_taken"), 1)

            def statistics(u, x, st_, mv_, stats_sem, mv_sem, used_sem):
                need(dve, used_sem, u)
                v.bn_stats(st_[:, :], x[:, :]).then_inc(stats_sem, 1)
                apart(dve, (stats_sem, u + 1))
                v.bn_aggr(mv_[:, :], st_[:, :]).then_inc(mv_sem, 1)

            def q_stats_(u):
                dve.wait_ge(sem("xq_in"), 16 * (u + 1))
                statistics(u, xq, q_stats, q_mv, sem("q_stats_ready"), sem("q_mv_ready"), sem("xnq_ready"))

            def q_norm(u):
                dve.wait_ge(sem("q_rstd_ready"), u + 1)
                need(dve, sem("xt_done"), u)
                v.tensor_scalar(xnq[:, :], xq[:, :], q_mv[:, 0:1], q_rstd[:, 0:1], ALU.subtract, ALU.mult
                                ).then_inc(sem("xnq_ready"), 1)

            def OT(u):
                dve.wait_ge(sem("ot_done"), u + 1)
                need(dve, sem("wo_done"), u)
                v.tensor_copy(o_t[:, :, :, :], r0[0:64, :].rearrange("p (b a r) -> p a b r", b=TB, a=A)
                              ).then_inc(sem("ot_ready"), 1)

            def WO(u):
                dve.wait_ge(sem("wo_done"), u + 1)
                dve.wait_ge(sem("xr_in"), 16 * (u + 1))
                need(dve, sem("xres_ready"), 2 * u)
                v.tensor_tensor(x1[:, :], r1[:, 0:C], xr[:, :], ALU.add).then_inc(sem("x1_ready"), 1)
                dve.wait_ge(sem("x1_ready"), u + 1)
                statistics(u, x1, stats, mv, sem("stats_ready"), sem("mv_ready"), sem("xn_ready"))

            def T3(u):
                dve.wait_ge(sem("f_hi_ready"), u + 1)
                need(dve, sem("h_done"), 2 * u)
                v.tensor_tensor(f_lo[:, :, :], r0[:, 0:C].rearrange("p (k n) -> p k n", k=2), f_hi[:, :, :],
                                ALU.subtract).then_inc(sem("f_lo_ready"), 1)

            def norm(u):
                dve.wait_ge(sem("rstd_ready"), u + 1)
                need(dve, sem("tr_done"), u)
                need(dve, sem("xres_ready"), 2 * u)
                v.tensor_scalar(xn[:, :], x1[:, :], mv[:, 0:1], rstd[:, 0:1], ALU.subtract, ALU.mult
                                ).then_inc(sem("xn_ready"), 1)

            def rms_norm(u):
                dve.wait_ge(sem("nrm_ready"), u + 1)
                v.tensor_scalar(nrm_c[:, :], nrm[:, :], C ** -0.5, 1e-8, ALU.mult, ALU.max
                                ).then_inc(sem("nrm_c_ready"), 1)
                dve.wait_ge(sem("nrm_c_ready"), u + 1)
                v.reciprocal(rnrm[:, :], nrm_c[:, :]).then_inc(sem("rnrm_ready"), 1)
                dve.wait_ge(sem("rnrm_ready"), u + 1)
                v.tensor_scalar(xu[:, :], xn[:, :], rnrm[:, 0:1], None, ALU.mult).then_inc(sem("xu_ready"), 1)

            def H1(u):
                dve.wait_ge(sem("h_g_ready"), 8 * (u + 1))
                need(dve, sem("o2_done"), u)
                v.tensor_copy(h_hi[:, :, :], h_g[:, :, :]).then_inc(sem("h_hi_ready"), 1)

            def TR(u):
                dve.wait_ge(sem("x_hi_ready"), u + 1)
                need(dve, sem("ff_done"), u)
                v.tensor_tensor(x_lo[:, :, :], r0[:, :].rearrange("p (k n) -> p k n", k=4), x_hi[:, :, :],
                                ALU.subtract).then_inc(sem("x_lo_ready"), 1)

            def GA(u):
                dve.wait_ge(sem("g_done"), u + 1)
                need(dve, sem("gate_ready"), u)
                v.tensor_tensor(gate_b[:, :, :], r1[0:64, :].rearrange("p (a n) -> p a n", a=A), ax(b_gate[:, :], P),
                                ALU.add).then_inc(sem("gate_b_ready"), 1)

            def QK(u):
                dve.wait_ge(sem("qk_done"), u + 1)
                need(dve, sem("qk_ready"), u)
                v.tensor_tensor(qk_cos[:, :], r0[:, :], cos_t[:, :], ALU.mult).then_inc(sem("qk_taken"), 1)
                v.tensor_tensor(qk_sin[:, 0::2], r0[:, 1::2], sin_t[:, 0::2], ALU.mult).then_inc(sem("qk_taken"), 1)
                v.tensor_tensor(qk_sin[:, 1::2], r0[:, 0::2], sin_t[:, 1::2], ALU.mult).then_inc(sem("qk_taken"), 1)

            def gate_out(u):
                dve.wait_ge(sem("gate_th_ready"), u + 1)
                need(dve, sem("gate_w_ready"), u)
                need(dve, sem("gate_o_ready"), u)
                v.scalar_tensor_tensor(out=gate[:, :, :], in0=gate_th[:, :, :], scalar=1.0, in1=gate_b[:, :, :],
                                       op0=ALU.add, op1=ALU.mult).then_inc(sem("gate_ready"), 1)

            def O2(u):
                dve.wait_ge(sem("o2_done"), u + 1)
                dve.wait_ge(sem("x2b_ready"), u + 1)
                need(dve, sem("stored"), 16 * u)
                v.tensor_tensor(y_out[:, :], r0[:, 0:C], x2b[:, :], ALU.add).then_inc(sem("y_ready"), 1)

            def ST(u):
                dve.wait_ge(sem("st_done"), u + 1)
                need(dve, sem("y_done"), u)
                for half in range(2):
                    v.tensor_tensor(st[:, half, :, :].rearrange("p m n -> p (m n)"),
                                    p_r[:, 512 * half:512 * half + 256], decay[:, half, :], ALU.mult
                                    ).then_inc(sem("st_ready"), 1)

            def Y(u):
                dve.wait_ge(sem("y_done"), u + 1)
                for a in (2, 3):
                    v.tensor_copy(y_c[32 * a:32 * a + 32, :, :, :], y_heads(a)).then_inc(sem("y_c_dve"), 1)
                dve.wait_ge(sem("y_c_dve"), 2 * (u + 1))
                dve.wait_ge(sem("y_c_act"), 2 * (u + 1))
                grouped = y_c[:, :, :, :].rearrange("p b g n -> p (b g) n")
                v.tensor_reduce(y_sum[:, :], grouped, AX_X, ALU.add).then_inc(sem("y_sum_ready"), 1)
                dve.wait_ge(sem("y_sum_ready"), u + 1)
                v.tensor_scalar(y_mean[:, :], y_sum[:, :], 1.0 / HD, None, ALU.mult).then_inc(sem("y_mean_ready"), 1)
                dve.wait_ge(sem("y_mean_ready"), u + 1)
                need(dve, sem("y_sq_ready"), u)
                v.tensor_tensor(y_ctr[:, :, :], grouped, ax(y_mean[:, :], HD), ALU.subtract
                                ).then_inc(sem("y_ctr_ready"), 1)

            def y_variance(u):
                dve.wait_ge(sem("y_sq_ready"), u + 1)
                need(dve, sem("y_ve_ready"), u)
                v.tensor_reduce(y_ss[:, :], y_sq[:, :, :], AX_X, ALU.add).then_inc(sem("y_ss_ready"), 1)

            def y_norm(u):
                dve.wait_ge(sem("y_rstd_ready"), u + 1)
                need(dve, sem("yt_done"), u)
                v.tensor_tensor(y_n[:, :, :], y_ctr[:, :, :], ax(y_rstd[:, :], HD), ALU.mult
                                ).then_inc(sem("y_n_ready"), 1)

            def YT(u):
                dve.wait_ge(sem("yt_done"), u + 1)
                dve.wait_ge(sem("gate_w_ready"), u + 1)
                need(dve, sem("acc_done"), u)
                for a in range(A):
                    v.tensor_tensor(y_g[:, a, :, :], r0[0:64, :].rearrange("p (b a r) -> p a b r", b=TB, a=A)[:, a, :, :],
                                    gate_w[:, a, :].rearrange("p (b r) -> p b r", b=TB), ALU.mult
                                    ).then_inc(sem("y_g_ready"), 1)
                dve.wait_ge(sem("y_g_ready"), 4 * (u + 1))
                dve.wait_ge(sem("gate_o_ready"), u + 1)
                v.tensor_tensor(y_t[:, :, :, :].rearrange("p a b r -> p a (b r)"),
                                y_g[:, :, :, :].rearrange("p a b r -> p a (b r)"), gate_o[:, :, :], ALU.add
                                ).then_inc(sem("y_t_ready"), 1)

            def ACC(u):
                dve.wait_ge(sem("acc_done"), u + 1)
                dve.wait_ge(sem("xres_ready"), 2 * (u + 1))
                need(dve, sem("x2b_ready"), u)
                v.tensor_tensor(x2[:, :], r1[:, 0:C], x_resb[:, :], ALU.add).then_inc(sem("x2_ready"), 1)
                dve.wait_ge(sem("x2_ready"), u + 1)
                statistics(u, x2, f_stats, f_mv, sem("f_stats_ready"), sem("f_mv_ready"), sem("f_xn_ready"))

            def ffn_norm(u):
                dve.wait_ge(sem("f_rstd_ready"), u + 1)
                need(dve, sem("t3_done"), u)
                v.tensor_scalar(f_xn[:, :], x2[:, :], f_mv[:, 0:1], f_rstd[:, 0:1], ALU.subtract, ALU.mult
                                ).then_inc(sem("f_xn_ready"), 1)

            def weights(job):
                dve.wait_ge(sem("job_done"), job + 1)
                if job < 6:
                    k, lot = job // 3, job % 3
                    w = 512 if lot < 2 else 256
                    cols = slice(512 * lot, 512 * lot + w)
                    dve.wait_ge(sem("job_hi"), job + 1)
                    last = v.scalar_tensor_tensor(out=qkvff_lo[:, k, cols], in0=r0[:, 0:w], scalar=rms[:, k:k + 1],
                                           in1=qkvff_hi[:, k, cols], op0=ALU.mult, op1=ALU.subtract
                                           )
                elif job == 6:
                    dve.wait_ge(sem("job_hi"), job + 1)
                    for k in range(2):
                        last = v.tensor_tensor(by_group(gated_lo, k),
                                               r0[:, 256 * k:256 * k + 256].rearrange("p (g a e) -> p g a e", g=G, a=A),
                                               by_group(gated_hi, k), ALU.subtract)
                elif job == 7:
                    last = v.tensor_copy(wff[:, 2:4, :], r1[:, :].rearrange("p (k n) -> p k n", k=2))
                elif job == 8:
                    last = v.tensor_copy(wproj[:, 2:4, :], r1[0:64, :].rearrange("p (k n) -> p k n", k=2))
                elif job == 9:
                    v.tensor_scalar(mean_abs[:, :], r0[:, 0:2], 1.0 / (FF * C), 1e-8, ALU.mult, ALU.max
                                    ).then_inc(sem("mean_abs_ready"), 1)
                    dve.wait_ge(sem("mean_abs_ready"), 1)
                    v.tensor_scalar(thr_up[:, :], mean_abs[:, :], 0.5, None, ALU.mult).then_inc(sem("thr_ready"), 1)
                    v.tensor_scalar(thr_down[:, :], mean_abs[:, :], -0.5, None, ALU.mult).then_inc(sem("thr_ready"), 1)
                    dve.wait_ge(sem("thr_ready"), 2)
                    for i, (w, tern) in enumerate(((w1_n, w1_t), (w2_n, w2_t))):
                        flat = w[:, :, :].rearrange("p k n -> p (k n)")
                        v.tensor_scalar(below[:, :], flat, thr_down[:, i:i + 1], None, ALU.is_lt
                                        ).then_inc(sem("below_ready"), 1)
                        dve.wait_ge(sem("below_ready"), 2 * i + 1)
                        last = v.scalar_tensor_tensor(out=tern[:, :, :].rearrange("p k n -> p (k n)"), in0=flat,
                                               scalar=thr_up[:, i:i + 1], in1=below[:, :], op0=ALU.is_gt,
                                               op1=ALU.subtract)
                        if i == 0:
                            last.then_inc(sem("below_ready"), 1)
                            dve.wait_ge(sem("below_ready"), 2)
                elif job < 12:
                    dve.wait_ge(sem("job_hi"), job)
                    last = v.tensor_copy(w1[:, job - 10, 512:1024], r0.bitcast(F16)[:, 512:1024])
                else:
                    k = 4 * (job - 12)
                    dve.wait_ge(sem("job_hi"), job)
                    last = v.tensor_copy(w2[:, k + 2:k + 4, :],
                                         r0.bitcast(F16)[:, 512:1024].rearrange("p (k n) -> p k n", k=2))
                last.then_inc(sem("job_lo"), 1)

            dve.wait_ge(sem("last_tr"), 1)
            v.tensor_copy(last_t[:, 0, :], r0[:, 0:B]).then_inc(sem("last_t_ready"), 1)
            v.tensor_copy(last_t[0:64, 1, :], r0[0:64, B:2 * B]).then_inc(sem("last_t_ready"), 1)
            q_stats_(0)
            dve.wait_ge(sem("wkv_split"), 1)
            v.tensor_tensor(wkv_lo[:, :, :], wkv32[:, :, :], wkv_hi[:, :, :], ALU.subtract
                            ).then_inc(sem("wkv_split"), 1)
            q_norm(0)
            dve.wait_ge(sem("last_kv"), 1)
            for a in range(A):
                last = v.tensor_copy(v_last[:, 64 * a:64 * a + 64].rearrange("p (g n) -> p g n", g=G),
                                     r1[0:B, 256:512].rearrange("p (g a n) -> p a g n", g=G, a=A)[:, a, :, :])
            last.then_inc(sem("v_last_ready"), 1)
            dve.wait_ge(sem("ident_in"), 16)
            v.tensor_copy(ident16[:, :], ident[:, :]).then_inc(sem("ident16_ready"), 1)
            context_low(0, 0)
            values_out(0, 0)
            context_low(0, 1)

            at = STAGE_SLOT
            stages = {at["OT"]: [("OT", OT)], at["WO"]: [("WO", WO)],
                      at["WO"] + 1: [("T3", T3)], at["WO"] + 2: [("OT", norm)],
                      at["H"]: [("OT", rms_norm)], at["T"]: [("H", H1), ("T", TR)],
                      at["G"]: [("G", GA)], at["QK"]: [("QK", QK)], at["QK"] + 1: [("G", gate_out)],
                      at["O2"]: [("O2", O2)], at["FF"]: [("Q2", q_stats_)], at["FF"] + 1: [("Q2", q_norm)],
                      at["ST"]: [("ST", ST)],
                      at["Y"]: [("Y", Y)], at["Y"] + 1: [("Y", y_variance)], at["Y"] + 2: [("Y", y_norm)],
                      at["YT"]: [("YT", YT)], at["ACC"]: [("ACC", ACC)]}

            def step(t, inside=False):
                has_x = inside or t < T

                def after(b, k):
                    later = (t, b + k) if b + k < TB else (t + 1, b + k - TB)
                    return later if inside or later[0] < T else None

                if inside or 0 <= t - 2 < T:
                    ffn_norm(t - 2)
                for slot in range(TB * SLOTS):
                    b, part = slot // SLOTS, slot % SLOTS
                    if has_x:
                        if part == 0:
                            mask_scores(t, b, 0)
                            mask_scores(t, b, 1)
                        elif part == 2:
                            mask_scores(t, b, 2)
                            mask_scores(t, b, 3)
                        elif part == 3:
                            probs_out(t, b)
                            if after(b, 1):
                                values_out(*after(b, 1))
                        elif part == 4:
                            if after(b, 2):
                                context_low(*after(b, 2))
                            if b % 2 == 1:
                                output_taken(t, b)
                    if not inside and t == 0 and 1 <= slot < 15:
                        weights(slot - 1)
                    for name, stage in stages.get(slot, []):
                        if name == "Q2":
                            if inside or 0 < t < T - 2:
                                stage(t + 2)
                            continue
                        on, u = runs(name, t, inside)
                        if on:
                            stage(u)
                if not inside and t == 0:
                    q_stats_(2)
                    q_norm(2)

            q_stats_(1)
            q_norm(1)
            for t in range(3):
                step(t)
            with dve.Fori(3, T - 2) as t:
                step(t, True)
            for t in range(T - 2, T + 2):
                step(t)

        @blk.gpsimd
        def _(pool):
            PASSED[pool] = sem("pool_passed")
            g_ = nc.gpsimd

            def rstd_of(u, mv_, ve, rs, mv_sem, used_sem, ve_sem, rs_sem):
                apart(pool, (mv_sem, u + 1), (used_sem, u))
                g_.tensor_scalar(ve[:, :], mv_[:, 1:2], EPS, None, ALU.add).then_inc(ve_sem, 1)
                pool.wait_ge(ve_sem, u + 1)
                g_.tensor_tensor(rs[:, :], ve[:, :], halves[:, 0, 0:1], ALU.pow).then_inc(rs_sem, 1)

            def mask_bias(t, b):
                n, par = 4 * t + b, b % 2
                apart(pool, (sem(f"ctx_in{b}"), 48 * (t + 1)), (sem("masked"), 4 * (n - 1)))
                g_.tensor_scalar(mask_b[:, par, :], mask_u8[:, b, :], 1.0, BIG, ALU.subtract, ALU.mult
                                 ).then_inc(sem("mask_ready"), 1)

            def last_key(t, b):
                n, par = 4 * t + b, b % 2
                need(pool, sem("s_done"), 4 * (n - 1))
                g_.tensor_copy(k_t[:, par, :, MF:M], k_last[:, :, bass.ds(n, 1)]).then_inc(sem("klast_ready"), 1)

            def last_value(t, b):
                n, par = 4 * t + b, b % 2
                pool.wait_ge(sem("exp_done"), 4 * n + 4)
                need(pool, sem("o_taken"), 4 * (2 * t + b // 2))
                g_.tensor_tensor(last_pv[:, par, :, :], vl[:, bass.ds(n, 1), :].rearrange("p o (g n) -> p (o g) n", g=G),
                                 prob[:, par, :, MF:M].broadcast_to([P, G, HD]), ALU.mult
                                 ).then_inc(sem("last_pv_ready"), 1)

            def output_scaled(t, b):
                pair = 2 * t + b // 2
                pool.wait_ge(sem("rsum_ready"), pair + 1)
                pool.wait_ge(sem("o_taken"), 4 * (pair + 1))
                need(pool, sem("ot_done"), t)
                g_.tensor_tensor(o_c[:, b - 1:b + 1, :].rearrange("p b (g n) -> p (b g) n", g=G),
                                 o_raw[:, :, :, :].rearrange("p b g n -> p (b g) n"),
                                 ax(rsum[:, :, :].rearrange("p b g -> p (b g)"), HD), ALU.mult
                                 ).then_inc(sem("oc_ready"), 1)

            def queries(u, b):
                n = 4 * u + b
                if b == 0:
                    pool.wait_ge(sem("q_t_ready"), u + 1)
                need(pool, sem("s_done"), 4 * (n - 4) + 4)
                for m in range(2):
                    src = q_t[:, m, S * b:S * b + S].unsqueeze(1).broadcast_to([P, A, S])
                    last = g_.tensor_tensor(qbd[:, m, b, :, :], src, ax(head_mask[:, :], S), ALU.mult)
                last.then_inc(sem("qbd_ready"), 1)

            def norm(u):
                rstd_of(u, mv, var_eps, rstd, sem("mv_ready"), sem("xn_ready"), sem("var_eps_ready"), sem("rstd_ready"))

            def nrm_(u):
                pool.wait_ge(sem("ss_ready"), u + 1)
                need(pool, sem("nrm_c_ready"), u)
                g_.tensor_tensor(nrm[:, :], sum_sq[:, :], halves[:, 1, 0:1], ALU.pow).then_inc(sem("nrm_ready"), 1)

            def low_hidden(u):
                pool.wait_ge(sem("h_hi_ready"), u + 1)
                need(pool, sem("o2_done"), u)
                g_.tensor_tensor(h_lo[:, :, :], h_g[:, :, :], h_hi[:, :, :], ALU.subtract
                                 ).then_inc(sem("h_lo_ready"), 1)

            def q_norm(u):
                rstd_of(u, q_mv, q_ve, q_rstd, sem("q_mv_ready"), sem("xnq_ready"), sem("q_ve_ready"), sem("q_rstd_ready"))

            def residual(u):
                pool.wait_ge(sem("xn_ready"), u + 1)
                need(pool, sem("x2_ready"), u)
                g_.tensor_tensor(x_res[:, :], x1[:, :], xn[:, :], ALU.add).then_inc(sem("xres_ready"), 1)
                pool.wait_ge(sem("xres_ready"), 2 * u + 1)
                g_.tensor_tensor(x_resb[:, :], x_res[:, :], b_proj[:, :], ALU.add).then_inc(sem("xres_ready"), 1)

            def qk_sum(u):
                pool.wait_ge(sem("qk_taken"), 3 * (u + 1))
                need(pool, sem("t2_done"), u)
                g_.tensor_tensor(qk[:, :, :].rearrange("p k n -> p (k n)"), qk_cos[:, :], qk_sin[:, :], ALU.add
                                 ).then_inc(sem("qk_ready"), 1)

            def v_blocks(u):
                pool.wait_ge(sem("vr_ready"), u + 1)
                need(pool, sem("y_done"), u)
                for g in range(G):
                    last = g_.tensor_tensor(vbd[:, g, :, :], vr[:, 64 * g:64 * g + 64].unsqueeze(1).broadcast_to([P, TB, 64]),
                                            ax(batch_mask[:, :], 64), ALU.mult)
                last.then_inc(sem("vbd_ready"), 1)

            def gates(u):
                pool.wait_ge(sem("gate_ready"), u + 1)
                need(pool, sem("y_t_ready"), u)
                g_.tensor_tensor(gate_w[:, :, :], gate[:, :, :], ax(gn_w2[:, :], P), ALU.mult
                                 ).then_inc(sem("gate_w_ready"), 1)
                g_.tensor_tensor(gate_o[:, :, :], gate[:, :, :], ax(gn_b2[:, :], P), ALU.mult
                                 ).then_inc(sem("gate_o_ready"), 1)

            def r_queries(u):
                pool.wait_ge(sem("qk_t_ready"), u + 1)
                need(pool, sem("st_done"), u)
                for b in range(TB):
                    for m in range(2):
                        last = g_.tensor_tensor(rbd[:, m, b, :, :], qk_t[:, m, S * b:S * b + S].unsqueeze(1).broadcast_to([P, A, S]),
                                                ax(head_mask[:, :], S), ALU.mult)
                last.then_inc(sem("rbd_ready"), 1)

            def y_rstd_(u):
                apart(pool, (sem("y_ss_ready"), u + 1), (sem("y_n_ready"), u))
                g_.tensor_scalar(y_ve[:, :], y_ss[:, :], 1.0 / HD, EPS, ALU.mult, ALU.add).then_inc(sem("y_ve_ready"), 1)
                pool.wait_ge(sem("y_ve_ready"), u + 1)
                g_.tensor_tensor(y_rstd[:, :], y_ve[:, :], halves[:, 0, :], ALU.pow).then_inc(sem("y_rstd_ready"), 1)

            def ffn_norm(u):
                rstd_of(u, f_mv, f_ve, f_rstd, sem("f_mv_ready"), sem("f_xn_ready"), sem("f_ve_ready"), sem("f_rstd_ready"))

            def out_bias(u):
                pool.wait_ge(sem("x2_ready"), u + 1)
                need(pool, sem("y_ready"), u)
                g_.tensor_tensor(x2b[:, :], x2[:, :], b2[:, :], ALU.add).then_inc(sem("x2b_ready"), 1)

            g_.memset(halves[:, 0, :], -0.5).then_inc(sem("halves_ready"), 1)
            g_.memset(halves[:, 1, :], 0.5).then_inc(sem("halves_ready"), 1)
            g_.memset(ones[:, :], 1.0).then_inc(sem("ones_ready"), 1)
            pool.wait_ge(sem("halves_ready"), 2)
            q_norm(0)
            mask_bias(0, 0)
            pool.wait_ge(sem("k_last_ready"), 1)
            last_key(0, 0)
            pool.wait_ge(sem("masks_in"), 32)
            for b in range(TB):
                queries(0, b)

            at = STAGE_SLOT
            stages = {at["WO"]: [("WO", norm)], at["WO"] + 2: [("WO", residual)], at["Q"]: [("T", nrm_)],
                      at["T"]: [("H", low_hidden)],
                      at["QK"]: [("QK", qk_sum)], at["QK"] + 1: [("G", gates)], at["VR"] + 1: [("VR", v_blocks)],
                      at["FF"]: [("Q2", q_norm)], at["T2"]: [("T2", r_queries)],
                      at["Y"] + 1: [("Y", y_rstd_)], at["ACC"]: [("ACC", ffn_norm), ("ACC", out_bias)]}

            def step(t, inside=False):
                has_x = inside or t < T

                def after(b, k):
                    later = (t, b + k) if b + k < TB else (t + 1, b + k - TB)
                    return later if inside or later[0] < T else None

                if not inside and t == 0:
                    q_norm(1)
                for slot in range(TB * SLOTS):
                    b, part = slot // SLOTS, slot % SLOTS
                    if has_x:
                        if part == 0 and after(b, 1):
                            last_key(*after(b, 1))
                            mask_bias(*after(b, 1))
                        elif part == 3:
                            if not inside and t == 0 and b == 0:
                                pool.wait_ge(sem("vl_in"), 64)
                            last_value(t, b)
                        elif part == 4 and b % 2 == 1:
                            output_scaled(t, b)
                    if part == 4 and (inside or (0 < t and t + 1 < T)) and b >= 1:
                        queries(t + 1, b - 1)
                        if b == TB - 1:
                            queries(t + 1, b)
                    if not inside and t == 0 and slot == 15:
                        pool.wait_ge(sem("vec_in"), 192)
                        g_.tensor_scalar(gn_w2[:, :], gn_w[:, :], 0.5, None, ALU.mult).then_inc(sem("gn_ready"), 1)
                        g_.tensor_scalar(gn_b2[:, :], gn_b[:, :], 0.5, None, ALU.mult).then_inc(sem("gn_ready"), 1)
                        pool.wait_ge(sem("gn_ready"), 2)
                    for name, stage in stages.get(slot, []):
                        if name == "Q2":
                            if inside or 0 < t < T - 2:
                                stage(t + 2)
                            continue
                        on, u = runs(name, t, inside)
                        if on:
                            stage(u)
                if not inside and t == 0:
                    for b in range(TB):
                        queries(1, b)
                    q_norm(2)

            for t in range(3):
                step(t)
            with pool.Fori(3, T - 2) as t:
                step(t, True)
            for t in range(T - 2, T + 2):
                step(t)


def tables():
    f = np.float32
    p = np.arange(P)
    t = {"ident": np.eye(P, dtype=f)}
    t["head_mask"] = ((p[:, None] % 64) // HD == np.arange(A)[None, :]).astype(f)
    t["batch_mask"] = (p[:, None] // S == np.arange(TB)[None, :]).astype(f)
    half = C // 2
    pos = np.arange(S, dtype=f)
    angle = pos[:, None] * (f(1.0) / f(10000.0) ** (np.arange(half, dtype=f) / f(half)))[None, :]
    base = (np.arange(0, C, 2, dtype=f) + f(0.4 * C)) / f(1.4 * C)
    scale = base[None, :] ** ((pos - f(S // 2)) / f(128))[:, None]
    cos = np.repeat(np.concatenate([np.cos(angle) * scale, np.cos(angle) / scale], 1), 2, axis=1)
    sin = np.repeat(np.concatenate([np.sin(angle) * scale, np.sin(angle) / scale], 1), 2, axis=1)
    sin = sin * np.tile(np.array([-1.0, 1.0], f), C)[None, :]
    t["cos_t"] = np.tile(cos, (TB, 1)).astype(f)
    t["sin_t"] = np.tile(sin, (TB, 1)).astype(f)
    gamma = f(1.0) - f(2.0) ** (f(-5.0) - np.arange(H, dtype=f))
    diff = np.arange(S)[None, :] - np.arange(S)[:, None]
    by_head = np.where(diff[None] >= 0, gamma[:, None, None] ** np.maximum(diff, 0)[None].astype(f), 0) * HD ** -0.5
    by_head = by_head.reshape(2, 2, A, S, S).transpose(3, 1, 0, 2, 4).reshape(S, 2 * 2 * A * S)
    t["decay"] = np.tile(by_head, (TB, 1)).astype(f)
    return t


def kernel(**inputs):
    import concourse.bacc as bacc
    from concourse.bass_utils import run_bass_kernel_spmd as run

    nc = bacc.Bacc("TRN2", target_bir_lowering=False, num_devices=1)
    names = {"x": "x", "ctx": "ctx_768", "mask": "mask_BxS2_bf1", "wq": "L0_xattn_Wq", "wk": "L0_xattn_Wk",
             "wv": "L0_xattn_Wv", "wo": "L0_xattn_Wo", "qkvff": "L0_attn_w_qkvff", "gated": "L0_attn_w_gated",
             "b_gate": "L0_attn_b_gated", "proj": "L0_attn_w_proj", "b_proj": "L0_attn_b_proj",
             "gn_w": "L0_attn_gn_w", "gn_b": "L0_attn_gn_b", "wff": "L0_attn_w_ff", "rms": "L0_attn_rms_w",
             "w1": "L0_ffn_W1", "b1": "L0_ffn_b1", "w2": "L0_ffn_W2", "b2": "L0_ffn_b2"}
    host = {k: np.ascontiguousarray(inputs[v]) for k, v in names.items()}
    host["x"] = host["x"].reshape(B * S, C)
    host["mask"] = host["mask"].view(np.uint8)
    host.update(tables())
    arrays, d = {}, {}
    for k, a in host.items():
        arrays[f"in_{k}"] = a
        d[k] = nc.dram_tensor(f"in_{k}", a.shape, mybir.dt.from_np(a.dtype), kind="ExternalInput").ap()
    out = nc.dram_tensor("out", (B * S, C), F32, kind="ExternalOutput").ap()
    vl_dram = nc.dram_tensor("vl_dram", (B, C), F32, kind="Internal").ap()
    block_kernel(nc, d, out, vl_dram)
    r = run(nc, [arrays], core_ids=[0])
    return r.results[0]["out"].reshape(B, S, C)
```

```python
from contextlib import ExitStack

import numpy as np

import concourse.bass as bass
from concourse import mybir

F32, F16, BF16, U8 = mybir.dt.float32, mybir.dt.float16, mybir.dt.bfloat16, mybir.dt.uint8
ALU = mybir.AluOpType
ACT = mybir.ActivationFunctionType
AX_X = mybir.AxisListType.X

B, S, C = 32, 32, 256
M, CC = 257, 192
H, HD = 16, 16
G, A = 4, 4
MF = 256
TB = 4
T = B // TB
P = 128
KR = CC - P
FF = 1024
BIG = 2.0 ** 126
HUGE = 3.0e38
EPS = 1e-5
SLOTS = 5
PASSED = {}

PE_PLAN = {2: [("ST", 2)], 3: [("Y", 2)], 5: [("XT", -1), ("O2", 3)], 6: [("Q", -1)], 8: [("YT", 2), ("OT", 1)],
           9: [("WO", 1)], 10: [("ACC", 2)], 12: [("T3", 2)], 13: [("T", 1)], 14: [("QK", 1)], 15: [("G", 1)],
           16: [("VR", 1)], 17: [("FF", 1)], 18: [("H", 2)], 19: [("T2", 1)]}
ACT_PLAN = {4: [("y_squares", 2)], 5: [("XT", -1)], 6: [("Q", -1)], 11: [("squares_sum", 1)], 12: [("T3", 2)],
            13: [("T", 1)], 16: [("G", 1), ("VR", 1)], 18: [("FF", 1), ("H", 2)], 19: [("T2", 1)]}
DVE_PLAN = {0: [("H", 3)], 2: [("ST", 2)], 3: [("q_stats", -1), ("Y", 2)], 4: [("q_norm", -1)],
            5: [("y_variance", 2), ("O2", 3)], 7: [("y_norm", 2)], 8: [("YT", 2), ("OT", 1)], 9: [("WO", 1)],
            10: [("ACC", 2), ("norm", 1)], 11: [("ffn_norm", 2)], 12: [("rms_norm", 1), ("T3", 2)],
            13: [("T", 1)], 14: [("QK", 1)], 15: [("G", 1)], 17: [("gate", 1)]}
POOL_PLAN = {0: [("r_queries", 2)], 1: [("low_hidden", 3)], 3: [("q_norm", -1)], 5: [("y_rstd", 2)],
             9: [("norm", 1)], 10: [("ffn_norm", 2)], 11: [("nrm", 1)], 12: [("out_bias", 2), ("residual", 1)],
             15: [("qk_sum", 1)], 17: [("gates", 1)], 18: [("v_blocks", 1)]}
FIRST_STEP = {15: "XT", 16: "Q"}


def placed(t, b, later, inside):
    tile, place = t + (b + later) // TB, (b + later) % TB
    return (tile, place) if inside or 0 <= tile < T else None


def due(plan, slot, t, inside):
    first = not inside and t == 0
    if first and FIRST_STEP.get(slot) in [name for stages in plan.values() for name, _ in stages]:
        yield FIRST_STEP[slot], 1
    for name, lag in plan.get(slot, []):
        if first and name in FIRST_STEP.values():
            continue
        if inside or 0 <= t - lag < T:
            yield name, t - lag


def run_steps(engine, step):
    for t in range(3):
        step(t)
    with engine.Fori(3, T - 1) as t:
        step(t, True)
    for t in range(T - 1, T + 3):
        step(t)


def need(engine, semaphore, value):
    if isinstance(value, int) and value <= 0:
        return
    engine.wait_ge(semaphore, value)


def apart(engine, *waits):
    waits = [w for w in waits if not (isinstance(w[1], int) and w[1] <= 0)]
    for semaphore, value in waits:
        engine.wait_ge(semaphore, value)
    if any(not isinstance(value, int) for _, value in waits):
        engine.sem_inc(PASSED[engine], 1)


def block_kernel(nc, d, out, vl_dram, mask_dram):
    with ExitStack() as ctx:
        def sb(name, shape, dt=F32):
            return ctx.enter_context(nc.sbuf_tensor(name, shape, dt))

        def ps(name, shape):
            return ctx.enter_context(nc.psum_tensor(name, shape, F32))

        sems = {}

        def sem(name):
            if name not in sems:
                sems[name] = ctx.enter_context(nc.semaphore(name))
            return sems[name]

        ident = sb("ident", [P, P])
        ident16 = sb("ident16", [P, P], F16)
        ones = sb("ones", [P, P])
        halves = sb("halves", [P, 2, G * TB])
        cos_t = sb("cos_t", [P, 2 * C])
        sin_t = sb("sin_t", [P, 2 * C])
        decay = sb("decay", [P, 2, 2 * P])
        head_mask = sb("head_mask", [P, A])
        batch_mask = sb("batch_mask", [P, TB])
        wq = sb("wq", [P, 2, C])
        wkv32 = sb("wkv32", [P, 4, C])
        wkv_hi = sb("wkv_hi", [P, 4, C], F16)
        wkv_lo = sb("wkv_lo", [P, 4, C], F16)
        wo = sb("wo", [64, A, C])
        qkvff_n = sb("qkvff_n", [P, 10, C])
        gated_n = sb("gated_n", [P, 2, C])
        proj_n = sb("proj_n", [P, 2, C])
        ff_n = sb("ff_n", [P, 2, 2 * C])
        w1_n = sb("w1_n", [P, 8, C])
        w2_n = sb("w2_n", [P, 2, FF])
        rms = sb("rms", [P, 2])
        b_gate = sb("b_gate", [64, A])
        gn_w = sb("gn_w", [64, A])
        gn_b = sb("gn_b", [64, A])
        gn_w2 = sb("gn_w2", [64, A])
        gn_b2 = sb("gn_b2", [64, A])
        b1 = sb("b1", [P, 8])
        b_proj = sb("b_proj", [P, C])
        b2 = sb("b2", [P, C])
        qkvff_hi = sb("qkvff_hi", [P, 2, 5 * C], F16)
        qkvff_lo = sb("qkvff_lo", [P, 2, 5 * C], F16)
        gated_hi = sb("gated_hi", [P, 2, C], F16)
        gated_lo = sb("gated_lo", [P, 2, C], F16)
        wff = sb("wff", [P, 4, C])
        wproj = sb("wproj", [64, A, C])
        w1_t = sb("w1_t", [P, 8, C], F16)
        w2_t = sb("w2_t", [P, 2, FF], F16)
        below = sb("below", [P, 2 * FF], F16)
        scratch = sb("scratch", [P, 2 * FF])
        w1 = sb("w1", [P, 2, FF], F16)
        w2 = sb("w2", [P, 8, C], F16)
        abs_sum = sb("abs_sum", [P, 2])
        mean_abs = sb("mean_abs", [P, 2])
        thr_up = sb("thr_up", [P, 2])
        thr_down = sb("thr_down", [P, 2])

        last_n = sb("last_n", [B, CC])
        last_t = sb("last_t", [P, 2, B])
        k_last = sb("k_last", [P, 2, B])
        v_last = sb("v_last", [B, C])
        vl = sb("vl", [P, B, 64])

        xq = sb("xq", [P, C])
        q_stats = sb("q_stats", [P, 6])
        q_mv = sb("q_mv", [P, 2])
        q_ve = sb("q_ve", [P, 1])
        q_rstd = sb("q_rstd", [P, 1])
        xnq = sb("xnq", [P, C])
        xq_t = sb("xq_t", [P, 2, P])
        q_t = sb("q_t", [P, 2, P])
        qbd = sb("qbd", [P, 2, TB, A, S])
        ctx_s = sb("ctx_s", [P, TB, 2, CC + KR])
        mask_u8 = sb("mask_u8", [B, M], U8)
        mask_all = sb("mask_all", [B, M], BF16)
        mask_b = sb("mask_b", [P, TB, M], BF16)
        c_hi = sb("c_hi", [P, 2, 4, P], F16)
        c_lo = sb("c_lo", [P, 2, 2, P], F16)
        k_t = sb("k_t", [P, 2, 2, M])
        v_s = sb("v_s", [P, TB, 2, C])
        sm = sb("sm", [P, G, M])
        neg_max = sb("neg_max", [P, G])
        prob = sb("prob", [P, 2, G, M])
        sums = sb("sums", [P, TB, G])
        prob_t = sb("prob_t", [P, 2, 4, P])
        rsum = sb("rsum", [P, 2, G])
        last_pv = sb("last_pv", [P, TB, G, HD])
        o_raw = sb("o_raw", [P, 2, G, HD])
        o_c = sb("o_c", [P, TB, 64])

        o_t = sb("o_t", [64, A, TB, S])
        xr = sb("xr", [P, C])
        x1 = sb("x1", [P, C])
        stats = sb("stats", [P, 6])
        mv = sb("mv", [P, 2])
        var_eps = sb("var_eps", [P, 1])
        rstd = sb("rstd", [P, 1])
        xn = sb("xn", [P, C])
        squares = sb("squares", [P, C])
        sum_sq = sb("sum_sq", [P, 1])
        nrm = sb("nrm", [P, 1])
        nrm_c = sb("nrm_c", [P, 1])
        rnrm = sb("rnrm", [P, 1])
        xu = sb("xu", [P, C])
        x_hi = sb("x_hi", [P, 4, P], F16)
        x_lo = sb("x_lo", [P, 4, P], F16)
        gate_b = sb("gate_b", [64, A, P])
        gate_th = sb("gate_th", [64, A, P])
        gate = sb("gate", [64, A, P])
        gate_w = sb("gate_w", [64, A, P])
        gate_o = sb("gate_o", [64, A, P])
        qk_cos, qk_sin = scratch[:, 0:512], scratch[:, 512:1024]
        qk = scratch[:, 1024:1536].rearrange("p (k n) -> p k n", k=4)
        qk_t = scratch[:, 1536:2048].rearrange("p (k n) -> p k n", k=4)
        rbd = w2_n[:, 0, :].rearrange("p (m b a r) -> p m b a r", m=2, b=TB, a=A)
        vr = sb("vr", [P, C])
        vbd = w2_n[:, 1, :].rearrange("p (g b n) -> p g b n", g=G, b=TB)
        ff_g = sb("ff_g", [P, 4, P])
        st = sb("st", [P, 2, 2, P])
        y_sum = sb("y_sum", [P, TB * G])
        y_mean = sb("y_mean", [P, TB * G])
        y_ctr = sb("y_ctr", [P, TB * G, HD])
        y_sq = sb("y_sq", [P, TB * G, HD])
        y_ss = sb("y_ss", [P, TB * G])
        y_ve = sb("y_ve", [P, TB * G])
        y_rstd = sb("y_rstd", [P, TB * G])
        y_n = sb("y_n", [P, TB, G, HD])
        y_g = sb("y_g", [64, A, TB, S])
        y_t = sb("y_t", [64, A, TB, S])
        x_res = sb("x_res", [P, C])
        x_resb = sb("x_resb", [P, C])
        x2 = sb("x2", [P, C])

        f_stats = sb("f_stats", [P, 6])
        f_mv = sb("f_mv", [P, 2])
        f_ve = sb("f_ve", [P, 1])
        f_rstd = sb("f_rstd", [P, 1])
        f_xn = sb("f_xn", [P, C])
        f_hi = sb("f_hi", [P, 2, P], F16)
        f_lo = sb("f_lo", [P, 2, P], F16)
        h_g = w1_n[:, 0:4, :].rearrange("p k (i n) -> p (k i) n", i=2)
        h_hi = w1_t[:, 0:4, :].rearrange("p k (i n) -> p (k i) n", i=2)
        h_lo = w1_t[:, 4:8, :].rearrange("p k (i n) -> p (k i) n", i=2)
        x2b = sb("x2b", [P, C])
        y_out = sb("y_out", [P, C])

        p_ct = ps("p_ct", [P, 512])
        p_kv = ps("p_kv", [P, 512])
        p_s = [ps("p_s0", [P, 512]), ps("p_s1", [P, 512])]
        p_pt = ps("p_pt", [P, 512])
        p_o = ps("p_o", [P, 512])
        p_r = ps("p_r", [P, 1024])
        r0, r1 = p_r[:, 0:512], p_r[:, 512:1024]

        def ax(ap, n):
            return ap.unsqueeze(2).broadcast_to([ap.shape[0], ap.shape[1], n])

        def by_group(w, k):
            return w[:, k, :].rearrange("p (a g e) -> p g a e", g=G, a=A)

        x_rows = d["x"]
        ctx.enter_context(nc.allow_non_contiguous_dma(reason="a few vectors of up to 1024 elements go across partitions"))
        blk = ctx.enter_context(nc.Block())

        @blk.sync
        def _(sp):
            sp.dma_start(last_n[:, :], d["ctx"][:, MF, :]).then_inc(sem("last_in"), 16)
            sp.dma_start(mask_u8[:, :], d["mask"]).then_inc(sem("mask_u8_in"), 16)
            sp.dma_start(ident[:, :], d["ident"]).then_inc(sem("ident_in"), 16)
            for i, w in ((0, "wk"), (2, "wv")):
                sp.dma_start(wkv32[:, i, :], d[w][0:P, :]).then_inc(sem("wkv_in"), 16)
                sp.dma_start(wkv32[0:64, i + 1, :], d[w][P:CC, :]).then_inc(sem("wkv_in"), 16)
                sp.dma_start(wkv32[64:P, i + 1, :], d[w][P:CC, :]).then_inc(sem("wkv_in"), 16)
            sp.dma_start(wq[:, :, :], d["wq"].rearrange("(k p) n -> p k n", p=P)).then_inc(sem("wq_in"), 16)
            sp.dma_start(head_mask[:, :], d["head_mask"]).then_inc(sem("masks_in"), 16)
            sp.dma_start(batch_mask[:, :], d["batch_mask"]).then_inc(sem("masks_in"), 16)

            def load_context(t, b):
                n = 4 * t + b
                need(sp, sem("ct_done"), n - 3)
                src = d["ctx"][bass.ds(n, 1), 0:MF, :].rearrange("o (j p) c -> p (o j) c", p=P)
                sp.dma_start(ctx_s[:, b, :, 0:CC], src).then_inc(sem(f"ctx_in{b}"), 16)
                sp.dma_start(ctx_s[:, b, :, CC:], src[:, :, P:CC]).then_inc(sem(f"ctx_in{b}"), 16)

            def load_mask(t, b):
                n = 4 * t + b
                need(sp, sem("masked"), 4 * (n - 3))
                sp.dma_start(mask_b[:, b, :], mask_dram[bass.ds(n, 1), :].broadcast_to([P, M])
                             ).then_inc(sem(f"mask_in{b}"), 16)

            def load_xq(t):
                need(sp, sem("xnq_ready"), t)
                sp.dma_start(xq[:, :], x_rows[bass.ds(t * P, P), :]).then_inc(sem("xq_in"), 16)

            load_xq(0)
            for b in range(TB):
                load_context(0, b)
            sp.wait_ge(sem("mask_ready"), 1)
            sp.dma_start(mask_dram[:, :], mask_all[:, :]).then_inc(sem("mask_out"), 16)
            sp.wait_ge(sem("mask_out"), 16)
            for b in range(TB):
                load_mask(0, b)

            sp.wait_ge(sem("v_last_ready"), 1)
            sp.dma_start(vl_dram[:, :], v_last[:, :]).then_inc(sem("vl_out"), 16)
            sp.wait_ge(sem("vl_out"), 16)
            for a in range(A):
                sp.dma_start(vl[32 * a:32 * a + 32, :, :],
                             vl_dram[:, 64 * a:64 * a + 64].unsqueeze(0).broadcast_to([S, B, 64])
                             ).then_inc(sem("vl_in"), 16)
            for g in range(G):
                sp.dma_start(wo[16 * g:16 * g + 16, :, :],
                             d["wo"][64 * g:64 * g + 64, :].rearrange("(a e) n -> e a n", a=A)
                             ).then_inc(sem("wo_in"), 16)
            sp.dma_start(rms[:, :], d["rms"].rearrange("(k p) -> p k", p=P)).then_inc(sem("w_in0"), 16)
            sp.dma_start(qkvff_n[:, :, :], d["qkvff"].rearrange("(k p) n -> p k n", p=P)).then_inc(sem("w_in0"), 16)
            sp.dma_start(gated_n[:, :, :], d["gated"].rearrange("(k p) n -> p k n", p=P)).then_inc(sem("w_in1"), 16)
            sp.dma_start(ff_n[:, :, :], d["wff"].rearrange("(k p) n -> p k n", p=P)).then_inc(sem("w_in1"), 16)
            for i in range(2):
                for a in range(A):
                    src = d["proj"][P * i:P * i + P, :].rearrange("p (g a e) -> p a g e", g=G, a=A)[:, a, :, :]
                    sp.dma_start(proj_n[:, i, 64 * a:64 * a + 64].rearrange("p (g e) -> p g e", g=G), src
                                 ).then_inc(sem("w_in1"), 16)
            sp.dma_start(w1_n[:, :, :], d["w1"].rearrange("(k p) n -> p k n", p=P)).then_inc(sem("w_in2"), 16)
            sp.dma_start(w2_n[:, :, :], d["w2"].rearrange("(k p) n -> p k n", p=P)).then_inc(sem("w_in2"), 16)
            for name, tile in (("cos_t", cos_t), ("sin_t", sin_t)):
                sp.dma_start(tile[:, :], d[name]).then_inc(sem("tab_in"), 16)
            sp.dma_start(decay[:, :, :], d["decay"].rearrange("p (h n) -> p h n", h=2)).then_inc(sem("tab_in"), 16)
            for name, tile in (("b_proj", b_proj), ("b2", b2)):
                sp.dma_start(tile[:, :], d[name].unsqueeze(0).broadcast_to([P, C])).then_inc(sem("tab_in"), 16)
            sp.dma_start(b1[:, :], d["b1"].rearrange("(k p) -> p k", p=P)).then_inc(sem("tab_in"), 16)
            for name, tile in (("b_gate", b_gate), ("gn_w", gn_w), ("gn_b", gn_b)):
                for g in range(G):
                    sp.dma_start(tile[16 * g:16 * g + 16, :],
                                 d[name][64 * g:64 * g + 64].rearrange("(a e) -> e a", a=A)
                                 ).then_inc(sem("vec_in"), 16)
            sp.sem_inc(sem("out_free"), 16)

            def step(t, inside=False):
                for b in range(TB):
                    if b == 0 and (inside or t + 1 < T):
                        load_xq(t + 1)
                    if b == 0 and (inside or 0 <= t - 1 < T):
                        need(sp, sem("x1_ready"), t - 1)
                        sp.dma_start(xr[:, :], x_rows[bass.ds((t - 1) * P, P), :]).then_inc(sem("xr_in"), 16)
                    if inside or t + 1 < T:
                        load_context(t + 1, b)
                        load_mask(t + 1, b)
                    if b == 2 and (inside or 0 <= t - 3 < T):
                        sp.wait_ge(sem("y_ready"), t - 2)
                        sp.dma_start(out[bass.ds((t - 3) * P, P), :], y_out[:, :]).then_inc(sem("out_free"), 16)

            run_steps(sp, step)
            sp.wait_ge(sem("out_free"), 16 * (T + 1))

        @blk.tensor
        def _(pe):
            PASSED[pe] = sem("pe_passed")
            mm = nc.tensor.matmul

            pe.wait_ge(sem("ident_in"), 16)
            pe.wait_ge(sem("last_in"), 16)
            nc.tensor.transpose(r0[:, 0:B], last_n[:, 0:P], ident[0:B, 0:B])
            nc.tensor.transpose(r0[0:KR, B:2 * B], last_n[:, P:CC], ident[0:B, 0:B]).then_inc(sem("last_tr"), 1)
            pe.wait_ge(sem("wkv_in"), 96)
            pe.wait_ge(sem("last_t_ready"), 2)
            for m in range(2):
                mm(r1[:, B * m:B * m + B], wkv32[:, 0, P * m:P * m + P], last_t[:, 0, :], start=True, stop=False)
                mm(r1[:, B * m:B * m + B], wkv32[0:64, 1, P * m:P * m + P], last_t[0:64, 1, :], start=False, stop=True)
            mm(r1[0:B, 256:512], last_t[:, 0, :], wkv32[:, 2, :], start=True, stop=False)
            mm(r1[0:B, 256:512], last_t[0:64, 1, :], wkv32[0:64, 3, :], start=False, stop=True).then_inc(sem("last_kv"), 1)

            def context_transposed(t, b):
                n = 4 * t + b
                pe.wait_ge(sem(f"ctx_in{b}"), 32 * (t + 1))
                need(pe, sem("hi_done"), n)
                need(pe, sem("lo_done"), 2 * n)
                for j in range(2):
                    nc.tensor.transpose(p_ct[:, P * j:P * j + P], ctx_s[:, b, j, 0:P], ident[:, :])
                for j in range(2):
                    last = nc.tensor.transpose(p_ct[:, 256 + P * j:256 + P * j + P], ctx_s[:, b, j, P:], ident[:, :])
                last.then_inc(sem("ct_done"), 1)

            def keys(t, b):
                n, par = 4 * t + b, b % 2
                pe.wait_ge(sem("hi_done"), n + 1)
                pe.wait_ge(sem("lo_done"), 2 * n + 2)
                if isinstance(t, int) and n == 0:
                    pe.wait_ge(sem("wkv_split"), 2)
                need(pe, sem("v_ready"), n)
                for m in range(2):
                    o = p_kv[:, 256 * m:256 * m + 256]
                    c = slice(P * m, P * m + P)
                    mm(o, wkv_hi[:, 0, c], c_hi[:, par, 0:2, :], start=True, stop=False)
                    mm(o, wkv_lo[:, 0, c], c_hi[:, par, 0:2, :], start=False, stop=False)
                    mm(o, wkv_hi[:, 0, c], c_lo[:, par, :, :], start=False, stop=False)
                    mm(o, wkv_hi[:, 1, c], c_hi[:, par, 2:4, :], start=False, stop=False)
                    last = mm(o, wkv_lo[0:64, 1, c], c_hi[0:64, par, 2:4, :], start=False, stop=True)
                last.then_inc(sem("k_done"), 1)

            def values(t, b):
                n, par = 4 * t + b, b % 2
                pe.wait_ge(sem("kt_ready"), n + 1)
                for j in range(2):
                    o = p_kv[:, 256 * j:256 * j + 256]
                    mm(o, c_hi[:, par, j, :], wkv_hi[:, 2, :], start=True, stop=False)
                    mm(o, c_hi[:, par, j, :], wkv_lo[:, 2, :], start=False, stop=False)
                    mm(o, c_lo[:, par, j, :], wkv_hi[:, 2, :], start=False, stop=False)
                    mm(o, c_hi[:, par, 2 + j, :], wkv_hi[:, 3, :], start=False, stop=False)
                    last = mm(o, c_hi[0:64, par, 2 + j, :], wkv_lo[0:64, 3, :], start=False, stop=True)
                last.then_inc(sem("v_done"), 1)

            def scores(t, b, g):
                n, par, m, half = 4 * t + b, b % 2, g // 2, g % 2
                if g == 0:
                    pe.wait_ge(sem("qbd_ready"), n + 1)
                    pe.wait_ge(sem("kt_ready"), n + 1)
                    pe.wait_ge(sem("klast_ready"), n + 1)
                need(pe, sem("masked"), 4 * n + g - 1)
                rows = slice(64 * half, 64 * half + 64)
                mm(p_s[half][:, 0:M], qbd[rows, m, b, :, :], k_t[rows, par, m, :],
                   start=True, stop=True).then_inc(sem("s_done"), 1)

            def probs_transposed(t, b, pair):
                n, par = 4 * t + b, b % 2
                pe.wait_ge(sem("exp_done"), 4 * n + 2 * pair + 2)
                if pair == 0:
                    need(pe, sem("pt1_ready"), n)
                else:
                    pe.wait_ge(sem("pt0_ready"), n + 1)
                for i in range(2):
                    for j in range(2):
                        at = P * (2 * i + j)
                        last = nc.tensor.transpose(p_pt[:, at:at + P], prob[:, par, 2 * pair + i, P * j:P * j + P],
                                                   ident[:, :])
                last.then_inc(sem("pt_done"), 1)

            def attend(t, b, pair):
                n, par = 4 * t + b, b % 2
                pe.wait_ge(sem(f"pt{pair}_ready"), n + 1)
                if pair == 0:
                    pe.wait_ge(sem("v_ready"), n + 1)
                    if par == 0:
                        need(pe, sem("o_taken"), 4 * (2 * t + b // 2))
                for i in range(2):
                    g = 2 * pair + i
                    for j in range(2):
                        last = mm(p_o[:, 256 * par + 64 * g:256 * par + 64 * g + 64], prob_t[:, pair, 2 * i + j, :],
                                  v_s[:, b, j, 64 * g:64 * g + 64], start=(j == 0), stop=(j == 1))
                last.then_inc(sem("pv_done"), 1)

            def OT(u):
                apart(pe, (sem("oc_ready"), 2 * u + 2), (sem("y_ready"), u - 1))
                for b in range(TB):
                    last = nc.tensor.transpose(r1[0:64, P * b:P * b + P], o_c[:, b, :], ident[:, :])
                last.then_inc(sem("ot_done"), 1)

            def WO(u):
                if isinstance(u, int) and u == 0:
                    pe.wait_ge(sem("wo_in"), 64)
                pe.wait_ge(sem("ot_ready"), u + 1)
                for a in range(A):
                    last = mm(r1[:, 0:C], o_t[:, a, :, :], wo[:, a, :], start=(a == 0), stop=(a == A - 1))
                last.then_inc(sem("wo_done"), 1)

            def T3(u):
                pe.wait_ge(sem("f_xn_ready"), u + 1)
                if isinstance(u, int) and u + 1 == T:
                    pe.wait_ge(sem("y_ready"), u)
                else:
                    pe.wait_ge(sem("x1_ready"), u + 2)
                for k in range(2):
                    last = nc.tensor.transpose(r1[:, P * k:P * k + P], f_xn[:, P * k:P * k + P], ident[:, :])
                last.then_inc(sem("t3_done"), 1)

            def XT(u):
                pe.wait_ge(sem("xnq_ready"), u + 1)
                need(pe, sem("q_t_ready"), u)
                need(pe, sem("y_ctr_ready"), u - 2)
                for k in range(2):
                    last = nc.tensor.transpose(r0[:, P * k:P * k + P], xnq[:, P * k:P * k + P], ident[:, :])
                last.then_inc(sem("xt_done"), 1)

            def Q(u):
                pe.wait_ge(sem("xq_t_ready"), u + 1)
                for m in range(2):
                    for k in range(2):
                        last = mm(r0[:, P * m:P * m + P], wq[:, k, P * m:P * m + P], xq_t[:, k, :],
                                  start=(k == 0), stop=(k == 1))
                last.then_inc(sem("q_done"), 1)

            def H1(u):
                pe.wait_ge(sem("f_hi_ready"), u + 1)
                pe.wait_ge(sem("f_lo_ready"), u + 1)
                another = not (isinstance(u, int) and u + 1 == T)
                if another:
                    pe.wait_ge(sem("vr_ready"), u + 2)
                for m in range(8):
                    if m == 4 and another:
                        pe.wait_ge(sem("ff_g_ready"), u + 2)
                    o = (r1 if m < 4 else r0)[:, P * (m % 4):P * (m % 4) + P]
                    for k in range(2):
                        mm(o, w1[:, k, P * m:P * m + P], f_hi[:, k, :], start=(k == 0), stop=False)
                        last = mm(o, w1[:, k, P * m:P * m + P], f_lo[:, k, :], start=False, stop=(k == 1))
                    if m % 4 == 3:
                        last.then_inc(sem("h_done"), 1)

            def TR(u):
                pe.wait_ge(sem("xn_ready"), u + 1)
                pe.wait_ge(sem("xu_ready"), u + 1)
                need(pe, sem("x2_ready"), u)
                if isinstance(u, int) and u == 0:
                    pe.wait_ge(sem("q_t_ready"), 3)
                for k in range(2):
                    nc.tensor.transpose(r0[:, P * k:P * k + P], xn[:, P * k:P * k + P], ident[:, :])
                for k in range(2):
                    last = nc.tensor.transpose(r0[:, 256 + P * k:256 + P * k + P], xu[:, P * k:P * k + P], ident[:, :])
                last.then_inc(sem("tr_done"), 1)

            def three(o, cols):
                for k in range(2):
                    mm(o, x_hi[:, 2 + k, :], qkvff_hi[:, k, cols], start=(k == 0), stop=False)
                    mm(o, x_hi[:, 2 + k, :], qkvff_lo[:, k, cols], start=False, stop=False)
                    last = mm(o, x_lo[:, 2 + k, :], qkvff_hi[:, k, cols], start=False, stop=(k == 1))
                return last

            def QK(u):
                pe.wait_ge(sem("x_hi_ready"), u + 1)
                pe.wait_ge(sem("x_lo_ready"), u + 1)
                need(pe, sem("f_lo_ready"), u)
                three(r1[:, :], slice(0, 2 * C)).then_inc(sem("qk_done"), 1)

            def GA(u):
                for a in range(A):
                    o = r0[0:64, P * a:P * a + P]
                    for k in range(2):
                        w_hi, w_lo = gated_hi[:, k, 64 * a:64 * a + 64], gated_lo[:, k, 64 * a:64 * a + 64]
                        mm(o, w_hi, x_hi[:, k, :], start=(k == 0), stop=False)
                        mm(o, w_lo, x_hi[:, k, :], start=False, stop=False)
                        last = mm(o, w_hi, x_lo[:, k, :], start=False, stop=(k == 1))
                last.then_inc(sem("g_done"), 1)

            def VR(u):
                pe.wait_ge(sem("qk_taken"), 3 * (u + 1))
                three(r1[:, 0:C], slice(2 * C, 3 * C)).then_inc(sem("vr_done"), 1)

            def O2(u):
                pe.wait_ge(sem("h_hi_ready"), u + 1)
                pe.wait_ge(sem("h_lo_ready"), u + 1)
                for f in range(8):
                    mm(r1[:, 0:C], h_hi[:, f, :], w2[:, f, :], start=(f == 0), stop=False)
                    last = mm(r1[:, 0:C], h_lo[:, f, :], w2[:, f, :], start=False, stop=(f == 7))
                last.then_inc(sem("o2_done"), 1)

            def FFN(u):
                pe.wait_ge(sem("gate_b_ready"), u + 1)
                for e in range(4):
                    o = r0[:, P * e:P * e + P]
                    c = slice(3 * C + P * e, 3 * C + P * e + P)
                    for k in range(2):
                        mm(o, qkvff_hi[:, k, c], x_hi[:, 2 + k, :], start=(k == 0), stop=False)
                        mm(o, qkvff_lo[:, k, c], x_hi[:, 2 + k, :], start=False, stop=False)
                        last = mm(o, qkvff_hi[:, k, c], x_lo[:, 2 + k, :], start=False, stop=(k == 1))
                last.then_inc(sem("ff_done"), 1)

            def T2(u):
                pe.wait_ge(sem("qk_ready"), u + 1)
                if isinstance(u, int) and u == 0:
                    pe.wait_ge(sem("vr_ready"), 1)
                need(pe, sem("h_g_ready"), 8 * u - 4)
                for i in range(4):
                    last = nc.tensor.transpose(r1[:, P * i:P * i + P], qk[:, i, :], ident[:, :])
                last.then_inc(sem("t2_done"), 1)

            def ST(u):
                apart(pe, (sem("rbd_ready"), u + 1), (sem("ff_g_ready"), u + 1), (sem("h_g_ready"), 8 * u))
                for half in range(2):
                    rows = slice(64 * half, 64 * half + 64)
                    for m in range(2):
                        for b in range(TB):
                            last = mm(p_r[32 * b:32 * b + 32, 512 * half + P * m:512 * half + P * m + P],
                                      qk_t[rows, 2 + m, 32 * b:32 * b + 32], rbd[rows, m, b, :, :],
                                      start=True, stop=True)
                last.then_inc(sem("st_done"), 1)

            def Y(u):
                apart(pe, (sem("st_ready"), 2 * (u + 1)), (sem("vbd_ready"), u + 1))
                for g in range(G):
                    m, half = g // 2, g % 2
                    for a in range(A):
                        last = mm(r0[32 * a:32 * a + 32, 64 * g:64 * g + 64], st[:, half, m, 32 * a:32 * a + 32],
                                  vbd[:, g, :, 16 * a:16 * a + 16], start=True, stop=True)
                last.then_inc(sem("y_done"), 1)

            def YT(u):
                more = not isinstance(u, int) or u + 3 < T
                apart(pe, (sem("y_n_ready"), u + 1), (sem("q_t_ready"), u + 4 if more else 0))
                for b in range(TB):
                    last = nc.tensor.transpose(r0[0:64, P * b:P * b + P], y_n[:, b, :, :], ident[:, :])
                last.then_inc(sem("yt_done"), 1)

            def ACC(u):
                pe.wait_ge(sem("y_t_ready"), u + 1)
                for e in range(4):
                    mm(r0[:, 0:C], ff_g[:, e, :], wff[:, e, :], start=(e == 0), stop=False)
                for a in range(A):
                    last = mm(r0[:, 0:C], y_t[:, a, :, :], wproj[:, a, :], start=False, stop=(a == A - 1))
                last.then_inc(sem("acc_done"), 1)

            def weights(job):
                if job == 0:
                    pe.wait_ge(sem("w_in0"), 32)
                    pe.wait_ge(sem("q_t_ready"), 1)
                    pe.wait_ge(sem("k_last_ready"), 1)
                    pe.wait_ge(sem("v_last_ready"), 1)
                need(pe, sem("job_hi"), job - (job > 9))
                need(pe, sem("job_lo"), job)
                if job < 6:
                    k, lot = job // 3, job % 3
                    for i in range(4 if lot < 2 else 2):
                        last = nc.tensor.transpose(r0[:, P * i:P * i + P], qkvff_n[:, 4 * lot + i, P * k:P * k + P],
                                                   ident[:, :])
                elif job == 6:
                    pe.wait_ge(sem("w_in1"), 160)
                    for k in range(2):
                        for i in range(2):
                            last = nc.tensor.transpose(r0[:, 256 * k + P * i:256 * k + P * i + P],
                                                       gated_n[:, i, P * k:P * k + P], ident[:, :])
                elif job == 7:
                    for e in range(4):
                        for i in range(2):
                            last = nc.tensor.transpose(p_r[:, 256 * e + P * i:256 * e + P * i + P],
                                                       ff_n[:, i, P * e:P * e + P], ident[:, :])
                elif job == 8:
                    for a in range(A):
                        for i in range(2):
                            last = nc.tensor.transpose(p_r[0:64, 256 * a + P * i:256 * a + P * i + P],
                                                       proj_n[:, i, 64 * a:64 * a + 64], ident[:, :])
                elif job == 9:
                    pe.wait_ge(sem("abs_ready"), 2)
                    pe.wait_ge(sem("ones_ready"), 1)
                    last = mm(r0[:, 0:2], ones[:, :], abs_sum[:, :], start=True, stop=True)
                elif job < 12:
                    k = job - 10
                    pe.wait_ge(sem("ident16_ready"), 1)
                    o = r0.bitcast(F16)
                    for i in range(8):
                        last = nc.tensor.transpose(o[:, P * i:P * i + P], w1_t[:, i, P * k:P * k + P], ident16[:, :])
                else:
                    k = job - 12
                    o = r0.bitcast(F16)
                    for f in range(4):
                        for i in range(2):
                            at = 256 * f + P * i
                            last = nc.tensor.transpose(o[:, at:at + P],
                                                       w2_t[:, i, P * (4 * k + f):P * (4 * k + f) + P], ident16[:, :])
                last.then_inc(sem("job_done"), 1)

            stages = {"OT": OT, "WO": WO, "T3": T3, "XT": XT, "Q": Q, "T": TR, "G": GA, "QK": QK, "VR": VR, "H": H1,
                      "O2": O2, "FF": FFN, "T2": T2, "ST": ST, "Y": Y, "YT": YT, "ACC": ACC}

            XT(0)
            Q(0)
            context_transposed(0, 0)
            keys(0, 0)
            values(0, 0)
            context_transposed(0, 1)

            def step(t, inside=False):
                for slot in range(TB * SLOTS):
                    b, part = slot // SLOTS, slot % SLOTS
                    now, before, next1, next2 = (placed(t, b, k, inside) for k in (0, -1, 1, 2))
                    if part == 0 and now:
                        scores(t, b, 0)
                        scores(t, b, 1)
                    if part == 1 and before:
                        probs_transposed(*before, 0)
                    if part == 1 and next1:
                        keys(*next1)
                    if part == 2 and now:
                        scores(t, b, 2)
                        scores(t, b, 3)
                    if part == 2 and before:
                        attend(*before, 0)
                    if part == 3 and before:
                        probs_transposed(*before, 1)
                    if part == 3 and next1:
                        values(*next1)
                    if part == 4 and next2:
                        context_transposed(*next2)
                    if part == 4 and before:
                        attend(*before, 1)
                    if not inside and t == 0 and 1 <= slot < 15:
                        weights(slot - 1)
                    if not inside and t == 0 and slot == 15:
                        pe.wait_ge(sem("job_hi"), 13)
                        pe.wait_ge(sem("job_lo"), 14)
                    for name, u in due(PE_PLAN, slot, t, inside):
                        stages[name](u)

            run_steps(pe, step)

        @blk.scalar
        def _(act):
            def copy(o, i):
                return nc.scalar.activation(o, i, ACT.Copy)

            def context_high(t, b):
                n, par = 4 * t + b, b % 2
                act.wait_ge(sem("ct_done"), n + 1)
                need(act, sem("v_done"), n - 1)
                copy(c_hi[:, par, :, :], p_ct[:, :].rearrange("p (j n) -> p j n", j=4)).then_inc(sem("hi_done"), 1)

            def keys_out(t, b):
                n, par = 4 * t + b, b % 2
                act.wait_ge(sem("k_done"), n + 1)
                need(act, sem("s_done"), 4 * (n - 1))
                copy(k_t[:, par, :, 0:MF], p_kv[:, :].rearrange("p (m n) -> p m n", m=2)).then_inc(sem("kt_ready"), 1)

            def exps(t, b, g):
                n, par = 4 * t + b, b % 2
                act.wait_ge(sem("masked"), 4 * n + g + 1)
                if g == 0:
                    need(act, sem("pt_done"), 2 * (n - 1))
                    need(act, sem("last_pv_ready"), n - 1)
                    if par == 0:
                        need(act, sem("rsum_ready"), 2 * t + b // 2 - 1)
                nc.scalar.activation(prob[:, par, g, :], sm[:, g, :], ACT.Exp, bias=neg_max[:, g:g + 1], scale=-1.0,
                                     accum_out=sums[:, b, g:g + 1]).then_inc(sem("exp_done"), 1)

            def probs_out(t, b):
                n = 4 * t + b
                act.wait_ge(sem("pt_done"), 2 * n + 2)
                need(act, sem("pv_done"), 2 * n)
                copy(prob_t[:, 1, :, :], p_pt[:, :].rearrange("p (j n) -> p j n", j=4)).then_inc(sem("pt1_ready"), 1)

            def XT(u):
                act.wait_ge(sem("xt_done"), u + 1)
                need(act, sem("q_done"), u)
                copy(xq_t[:, :, :], r0[:, 0:C].rearrange("p (k n) -> p k n", k=2)).then_inc(sem("xq_t_ready"), 1)

            def Q(u):
                act.wait_ge(sem("q_done"), u + 1)
                need(act, sem("qbd_ready"), 4 * u)
                copy(q_t[:, :, :], r0[:, 0:C].rearrange("p (k n) -> p k n", k=2)).then_inc(sem("q_t_ready"), 1)

            def T3(u):
                act.wait_ge(sem("t3_done"), u + 1)
                need(act, sem("h_done"), 2 * u)
                copy(f_hi[:, :, :], r1[:, 0:C].rearrange("p (k n) -> p k n", k=2)).then_inc(sem("f_hi_ready"), 1)

            def H1(u):
                need(act, sem("h_hi_ready"), u)
                need(act, sem("h_lo_ready"), u)
                for m in range(8):
                    if m % 4 == 0:
                        act.wait_ge(sem("h_done"), 2 * u + 1 + m // 4)
                    bank = r1 if m < 4 else r0
                    nc.scalar.activation(h_g[:, m, :], bank[:, P * (m % 4):P * (m % 4) + P], ACT.Gelu,
                                         bias=b1[:, m:m + 1]).then_inc(sem("h_g_ready"), 1)

            def squares_sum(u):
                act.wait_ge(sem("xn_ready"), u + 1)
                need(act, sem("nrm_ready"), u)
                nc.scalar.activation(squares[:, :], xn[:, :], ACT.Square,
                                     accum_out=sum_sq[:, :]).then_inc(sem("ss_ready"), 1)

            def TR(u):
                act.wait_ge(sem("tr_done"), u + 1)
                need(act, sem("ff_done"), u)
                copy(x_hi[:, :, :], r0[:, :].rearrange("p (k n) -> p k n", k=4)).then_inc(sem("x_hi_ready"), 1)

            def GA(u):
                act.wait_ge(sem("gate_b_ready"), u + 1)
                need(act, sem("gate_ready"), u)
                nc.scalar.activation(gate_th[:, :, :], gate_b[:, :, :], ACT.Tanh,
                                     scale=0.5).then_inc(sem("gate_th_ready"), 1)

            def VR(u):
                act.wait_ge(sem("vr_done"), u + 1)
                need(act, sem("vbd_ready"), u)
                copy(vr[:, :], r1[:, 0:C]).then_inc(sem("vr_ready"), 1)

            def FFN(u):
                act.wait_ge(sem("ff_done"), u + 1)
                need(act, sem("acc_done"), u)
                nc.scalar.activation(ff_g[:, :, :], r0[:, :].rearrange("p (k n) -> p k n", k=4),
                                     ACT.Gelu).then_inc(sem("ff_g_ready"), 1)

            def T2(u):
                act.wait_ge(sem("t2_done"), u + 1)
                need(act, sem("st_done"), u)
                need(act, sem("rbd_ready"), u)
                copy(qk_t[:, :, :], r1[:, :].rearrange("p (k n) -> p k n", k=4)).then_inc(sem("qk_t_ready"), 1)

            def y_squares(u):
                act.wait_ge(sem("y_ctr_ready"), u + 1)
                need(act, sem("y_ss_ready"), u)
                nc.scalar.activation(y_sq[:, :, :], y_ctr[:, :, :], ACT.Square).then_inc(sem("y_sq_ready"), 1)

            def weights(job):
                act.wait_ge(sem("job_done"), job + 1)
                if job < 6:
                    k, lot = job // 3, job % 3
                    w = 512 if lot < 2 else 256
                    last = nc.scalar.activation(qkvff_hi[:, k, 512 * lot:512 * lot + w], r0[:, 0:w], ACT.Copy,
                                                scale=rms[:, k:k + 1])
                elif job == 6:
                    for k in range(2):
                        last = copy(by_group(gated_hi, k), r0[:, 256 * k:256 * k + 256].rearrange("p (g a e) -> p g a e", g=G, a=A))
                elif job == 7:
                    last = copy(wff[:, 0:2, :], r0[:, :].rearrange("p (k n) -> p k n", k=2))
                elif job == 8:
                    last = copy(wproj[:, 0:2, :], r0[0:64, :].rearrange("p (k n) -> p k n", k=2))
                elif job == 9:
                    return
                elif job < 12:
                    last = copy(w1[:, job - 10, 0:512], r0.bitcast(F16)[:, 0:512])
                else:
                    last = copy(w2[:, 4 * (job - 12):4 * (job - 12) + 2, :],
                                r0.bitcast(F16)[:, 0:512].rearrange("p (k n) -> p k n", k=2))
                last.then_inc(sem("job_hi"), 1)

            act.wait_ge(sem("wkv_in"), 96)
            copy(wkv_hi[:, :, :], wkv32[:, :, :]).then_inc(sem("wkv_split"), 1)
            act.wait_ge(sem("v_last_ready"), 1)
            copy(k_last[:, :, :], r1[:, 0:2 * B].rearrange("p (m n) -> p m n", m=2)).then_inc(sem("k_last_ready"), 1)
            XT(0)
            Q(0)
            context_high(0, 0)
            keys_out(0, 0)
            context_high(0, 1)

            stages = {"T3": T3, "XT": XT, "squares_sum": squares_sum, "Q": Q, "H": H1, "T": TR, "G": GA, "VR": VR,
                      "FF": FFN, "T2": T2, "y_squares": y_squares}

            def step(t, inside=False):
                for slot in range(TB * SLOTS):
                    b, part = slot // SLOTS, slot % SLOTS
                    now, before, next1, next2 = (placed(t, b, k, inside) for k in (0, -1, 1, 2))
                    if part == 1 and now:
                        exps(t, b, 0)
                        exps(t, b, 1)
                    if part == 2 and next1:
                        keys_out(*next1)
                    if part == 3 and before:
                        probs_out(*before)
                    if part == 3 and now:
                        exps(t, b, 2)
                        exps(t, b, 3)
                    if part == 4 and next2:
                        context_high(*next2)
                    if not inside and t == 0 and slot == 8:
                        act.wait_ge(sem("w_in2"), 32)
                        nc.scalar.activation(scratch[:, :], w1_n[:, :, :].rearrange("p k n -> p (k n)"), ACT.Abs,
                                             accum_out=abs_sum[:, 0:1]).then_inc(sem("abs_ready"), 1)
                        act.wait_ge(sem("abs_ready"), 1)
                        nc.scalar.activation(scratch[:, :], w2_n[:, :, :].rearrange("p k n -> p (k n)"), ACT.Abs,
                                             accum_out=abs_sum[:, 1:2]).then_inc(sem("abs_ready"), 1)
                    if not inside and t == 0 and 1 <= slot < 15:
                        weights(slot - 1)
                    for name, u in due(ACT_PLAN, slot, t, inside):
                        stages[name](u)

            run_steps(act, step)

        @blk.vector
        def _(dve):
            PASSED[dve] = sem("dve_passed")
            v = nc.vector

            def context_low(t, b):
                n, par = 4 * t + b, b % 2
                dve.wait_ge(sem("hi_done"), n + 1)
                need(dve, sem("v_done"), n - 1)
                v.tensor_tensor(c_lo[:, par, :, :], p_ct[:, 0:256].rearrange("p (j n) -> p j n", j=2),
                                c_hi[:, par, 0:2, :], ALU.subtract).then_inc(sem("lo_done"), 1)
                v.tensor_tensor(c_hi[64:P, par, 2:4, :], p_ct[64:P, 256:512].rearrange("p (j n) -> p j n", j=2),
                                c_hi[64:P, par, 2:4, :], ALU.subtract).then_inc(sem("lo_done"), 1)

            def values_out(t, b):
                n, par = 4 * t + b, b % 2
                dve.wait_ge(sem("v_done"), n + 1)
                need(dve, sem("pv_done"), 2 * (n - 3))
                v.tensor_copy(v_s[:, b, :, :], p_kv[:, :].rearrange("p (j n) -> p j n", j=2)
                              ).then_inc(sem("v_ready"), 1)

            def mask_scores(t, b, g):
                n, par, half = 4 * t + b, b % 2, g % 2
                apart(dve, (sem("s_done"), 4 * n + g + 1), (sem(f"mask_in{b}"), 16 * (t + 1)),
                      (sem("exp_done"), 4 * (n - 1) + g + 1))
                v.tensor_tensor_reduce(sm[:, g, :], p_s[half][:, 0:M], mask_b[:, b, :], -(HD ** -0.5), HUGE,
                                       ALU.add, ALU.min, neg_max[:, g:g + 1]).then_inc(sem("masked"), 1)

            def probs_out(t, b):
                n = 4 * t + b
                dve.wait_ge(sem("pt_done"), 2 * n + 1)
                need(dve, sem("pv_done"), 2 * n - 1)
                v.tensor_copy(prob_t[:, 0, :, :], p_pt[:, :].rearrange("p (j n) -> p j n", j=4)
                              ).then_inc(sem("pt0_ready"), 1)

            def output_taken(t, b):
                n, pair = 4 * t + b, 2 * t + b // 2
                dve.wait_ge(sem("exp_done"), 4 * n + 4)
                need(dve, sem("oc_ready"), pair)
                v.reciprocal(rsum[:, :, :], sums[:, b - 1:b + 1, :]).then_inc(sem("rsum_ready"), 1)
                dve.wait_ge(sem("last_pv_ready"), n + 1)
                dve.wait_ge(sem("pv_done"), 2 * n + 2)
                for a in range(A):
                    rows = slice(32 * a, 32 * a + 32)
                    own = p_o[rows, :].rearrange("p (b g n) -> p b g n", b=2, g=G)[:, :, :, 16 * a:16 * a + 16]
                    v.tensor_tensor(o_raw[rows, :, :, :], own, last_pv[rows, b - 1:b + 1, :, :], ALU.add
                                    ).then_inc(sem("o_taken"), 1)

            def statistics(u, x, st_, mv_, stats_sem, mv_sem, used_sem):
                need(dve, used_sem, u)
                v.bn_stats(st_[:, :], x[:, :]).then_inc(stats_sem, 1)
                apart(dve, (stats_sem, u + 1))
                v.bn_aggr(mv_[:, :], st_[:, :]).then_inc(mv_sem, 1)

            def q_stats_(u):
                dve.wait_ge(sem("xq_in"), 16 * (u + 1))
                statistics(u, xq, q_stats, q_mv, sem("q_stats_ready"), sem("q_mv_ready"), sem("xnq_ready"))

            def q_norm(u):
                dve.wait_ge(sem("q_rstd_ready"), u + 1)
                need(dve, sem("xt_done"), u)
                v.tensor_scalar(xnq[:, :], xq[:, :], q_mv[:, 0:1], q_rstd[:, 0:1], ALU.subtract, ALU.mult
                                ).then_inc(sem("xnq_ready"), 1)

            def OT(u):
                dve.wait_ge(sem("ot_done"), u + 1)
                need(dve, sem("wo_done"), u)
                v.tensor_copy(o_t[:, :, :, :], r1[0:64, :].rearrange("p (b a r) -> p a b r", b=TB, a=A)
                              ).then_inc(sem("ot_ready"), 1)

            def WO(u):
                dve.wait_ge(sem("wo_done"), u + 1)
                dve.wait_ge(sem("xr_in"), 16 * (u + 1))
                need(dve, sem("xres_ready"), 2 * u)
                v.tensor_tensor(x1[:, :], r1[:, 0:C], xr[:, :], ALU.add).then_inc(sem("x1_ready"), 1)
                dve.wait_ge(sem("x1_ready"), u + 1)
                statistics(u, x1, stats, mv, sem("stats_ready"), sem("mv_ready"), sem("xn_ready"))

            def T3(u):
                dve.wait_ge(sem("f_hi_ready"), u + 1)
                need(dve, sem("h_done"), 2 * u)
                v.tensor_tensor(f_lo[:, :, :], r1[:, 0:C].rearrange("p (k n) -> p k n", k=2), f_hi[:, :, :],
                                ALU.subtract).then_inc(sem("f_lo_ready"), 1)

            def norm(u):
                dve.wait_ge(sem("rstd_ready"), u + 1)
                need(dve, sem("tr_done"), u)
                need(dve, sem("xres_ready"), 2 * u)
                v.tensor_scalar(xn[:, :], x1[:, :], mv[:, 0:1], rstd[:, 0:1], ALU.subtract, ALU.mult
                                ).then_inc(sem("xn_ready"), 1)

            def rms_norm(u):
                dve.wait_ge(sem("nrm_ready"), u + 1)
                v.tensor_scalar(nrm_c[:, :], nrm[:, :], C ** -0.5, 1e-8, ALU.mult, ALU.max
                                ).then_inc(sem("nrm_c_ready"), 1)
                dve.wait_ge(sem("nrm_c_ready"), u + 1)
                v.reciprocal(rnrm[:, :], nrm_c[:, :]).then_inc(sem("rnrm_ready"), 1)
                dve.wait_ge(sem("rnrm_ready"), u + 1)
                v.tensor_scalar(xu[:, :], xn[:, :], rnrm[:, 0:1], None, ALU.mult).then_inc(sem("xu_ready"), 1)

            def H1(u):
                dve.wait_ge(sem("h_g_ready"), 8 * (u + 1))
                need(dve, sem("o2_done"), u)
                v.tensor_copy(h_hi[:, :, :], h_g[:, :, :]).then_inc(sem("h_hi_ready"), 1)

            def TR(u):
                dve.wait_ge(sem("x_hi_ready"), u + 1)
                need(dve, sem("ff_done"), u)
                v.tensor_tensor(x_lo[:, :, :], r0[:, :].rearrange("p (k n) -> p k n", k=4), x_hi[:, :, :],
                                ALU.subtract).then_inc(sem("x_lo_ready"), 1)

            def GA(u):
                dve.wait_ge(sem("g_done"), u + 1)
                need(dve, sem("gate_ready"), u)
                v.tensor_tensor(gate_b[:, :, :], r0[0:64, :].rearrange("p (a n) -> p a n", a=A), ax(b_gate[:, :], P),
                                ALU.add).then_inc(sem("gate_b_ready"), 1)

            def QK(u):
                dve.wait_ge(sem("qk_done"), u + 1)
                need(dve, sem("qk_ready"), u)
                v.tensor_tensor(qk_cos[:, :], r1[:, :], cos_t[:, :], ALU.mult).then_inc(sem("qk_taken"), 1)
                v.tensor_tensor(qk_sin[:, 0::2], r1[:, 1::2], sin_t[:, 0::2], ALU.mult).then_inc(sem("qk_taken"), 1)
                v.tensor_tensor(qk_sin[:, 1::2], r1[:, 0::2], sin_t[:, 1::2], ALU.mult).then_inc(sem("qk_taken"), 1)

            def gate_out(u):
                dve.wait_ge(sem("gate_th_ready"), u + 1)
                need(dve, sem("gate_w_ready"), u)
                need(dve, sem("gate_o_ready"), u)
                v.scalar_tensor_tensor(out=gate[:, :, :], in0=gate_th[:, :, :], scalar=1.0, in1=gate_b[:, :, :],
                                       op0=ALU.add, op1=ALU.mult).then_inc(sem("gate_ready"), 1)

            def O2(u):
                dve.wait_ge(sem("o2_done"), u + 1)
                dve.wait_ge(sem("x2b_ready"), u + 1)
                dve.wait_ge(sem("out_free"), 16 * (u + 1))
                v.tensor_tensor(y_out[:, :], r1[:, 0:C], x2b[:, :], ALU.add).then_inc(sem("y_ready"), 1)

            def ST(u):
                dve.wait_ge(sem("st_done"), u + 1)
                need(dve, sem("y_done"), u)
                for half in range(2):
                    v.tensor_tensor(st[:, half, :, :].rearrange("p m n -> p (m n)"),
                                    p_r[:, 512 * half:512 * half + 256], decay[:, half, :], ALU.mult
                                    ).then_inc(sem("st_ready"), 1)

            def Y(u):
                dve.wait_ge(sem("y_done"), u + 1)
                grouped = r0[:, 0:C].rearrange("p (i n) -> p i n", n=HD)
                v.tensor_reduce(y_sum[:, :], grouped, AX_X, ALU.add).then_inc(sem("y_sum_ready"), 1)
                dve.wait_ge(sem("y_sum_ready"), u + 1)
                v.tensor_scalar(y_mean[:, :], y_sum[:, :], 1.0 / HD, None, ALU.mult).then_inc(sem("y_mean_ready"), 1)
                dve.wait_ge(sem("y_mean_ready"), u + 1)
                need(dve, sem("y_sq_ready"), u)
                v.tensor_tensor(y_ctr[:, :, :], grouped, ax(y_mean[:, :], HD), ALU.subtract
                                ).then_inc(sem("y_ctr_ready"), 1)

            def y_variance(u):
                dve.wait_ge(sem("y_sq_ready"), u + 1)
                need(dve, sem("y_ve_ready"), u)
                v.tensor_reduce(y_ss[:, :], y_sq[:, :, :], AX_X, ALU.add).then_inc(sem("y_ss_ready"), 1)

            def y_norm(u):
                dve.wait_ge(sem("y_rstd_ready"), u + 1)
                need(dve, sem("yt_done"), u)
                v.tensor_tensor(y_n[:, :, :, :].rearrange("p b g n -> p g b n"),
                                y_ctr[:, :, :].rearrange("p (g b) n -> p g b n", g=G),
                                y_rstd[:, :].rearrange("p (g b) -> p g b", g=G).unsqueeze(3).broadcast_to([P, G, TB, HD]),
                                ALU.mult
                                ).then_inc(sem("y_n_ready"), 1)

            def YT(u):
                dve.wait_ge(sem("yt_done"), u + 1)
                dve.wait_ge(sem("gate_w_ready"), u + 1)
                need(dve, sem("acc_done"), u)
                for a in range(A):
                    v.tensor_tensor(y_g[:, a, :, :], r0[0:64, :].rearrange("p (b a r) -> p a b r", b=TB, a=A)[:, a, :, :],
                                    gate_w[:, a, :].rearrange("p (b r) -> p b r", b=TB), ALU.mult
                                    ).then_inc(sem("y_g_ready"), 1)
                dve.wait_ge(sem("y_g_ready"), 4 * (u + 1))
                dve.wait_ge(sem("gate_o_ready"), u + 1)
                v.tensor_tensor(y_t[:, :, :, :].rearrange("p a b r -> p a (b r)"),
                                y_g[:, :, :, :].rearrange("p a b r -> p a (b r)"), gate_o[:, :, :], ALU.add
                                ).then_inc(sem("y_t_ready"), 1)

            def ACC(u):
                dve.wait_ge(sem("acc_done"), u + 1)
                dve.wait_ge(sem("xres_ready"), 2 * (u + 1))
                need(dve, sem("x2b_ready"), u)
                v.tensor_tensor(x2[:, :], r0[:, 0:C], x_resb[:, :], ALU.add).then_inc(sem("x2_ready"), 1)
                dve.wait_ge(sem("x2_ready"), u + 1)
                statistics(u, x2, f_stats, f_mv, sem("f_stats_ready"), sem("f_mv_ready"), sem("f_xn_ready"))

            def ffn_norm(u):
                dve.wait_ge(sem("f_rstd_ready"), u + 1)
                need(dve, sem("t3_done"), u)
                v.tensor_scalar(f_xn[:, :], x2[:, :], f_mv[:, 0:1], f_rstd[:, 0:1], ALU.subtract, ALU.mult
                                ).then_inc(sem("f_xn_ready"), 1)

            def weights(job):
                dve.wait_ge(sem("job_done"), job + 1)
                if job < 6:
                    k, lot = job // 3, job % 3
                    w = 512 if lot < 2 else 256
                    cols = slice(512 * lot, 512 * lot + w)
                    dve.wait_ge(sem("job_hi"), job + 1)
                    last = v.scalar_tensor_tensor(out=qkvff_lo[:, k, cols], in0=r0[:, 0:w], scalar=rms[:, k:k + 1],
                                           in1=qkvff_hi[:, k, cols], op0=ALU.mult, op1=ALU.subtract
                                           )
                elif job == 6:
                    dve.wait_ge(sem("job_hi"), job + 1)
                    for k in range(2):
                        last = v.tensor_tensor(by_group(gated_lo, k),
                                               r0[:, 256 * k:256 * k + 256].rearrange("p (g a e) -> p g a e", g=G, a=A),
                                               by_group(gated_hi, k), ALU.subtract)
                elif job == 7:
                    last = v.tensor_copy(wff[:, 2:4, :], r1[:, :].rearrange("p (k n) -> p k n", k=2))
                elif job == 8:
                    last = v.tensor_copy(wproj[:, 2:4, :], r1[0:64, :].rearrange("p (k n) -> p k n", k=2))
                elif job == 9:
                    v.tensor_scalar(mean_abs[:, :], r0[:, 0:2], 1.0 / (FF * C), 1e-8, ALU.mult, ALU.max
                                    ).then_inc(sem("mean_abs_ready"), 1)
                    dve.wait_ge(sem("mean_abs_ready"), 1)
                    v.tensor_scalar(thr_up[:, :], mean_abs[:, :], 0.5, None, ALU.mult).then_inc(sem("thr_ready"), 1)
                    v.tensor_scalar(thr_down[:, :], mean_abs[:, :], -0.5, None, ALU.mult).then_inc(sem("thr_ready"), 1)
                    dve.wait_ge(sem("thr_ready"), 2)
                    for i, (w, tern) in enumerate(((w1_n, w1_t), (w2_n, w2_t))):
                        flat = w[:, :, :].rearrange("p k n -> p (k n)")
                        v.tensor_scalar(below[:, :], flat, thr_down[:, i:i + 1], None, ALU.is_lt
                                        ).then_inc(sem("below_ready"), 1)
                        dve.wait_ge(sem("below_ready"), 2 * i + 1)
                        last = v.scalar_tensor_tensor(out=tern[:, :, :].rearrange("p k n -> p (k n)"), in0=flat,
                                               scalar=thr_up[:, i:i + 1], in1=below[:, :], op0=ALU.is_gt,
                                               op1=ALU.subtract)
                        if i == 0:
                            last.then_inc(sem("below_ready"), 1)
                            dve.wait_ge(sem("below_ready"), 2)
                elif job < 12:
                    dve.wait_ge(sem("job_hi"), job)
                    last = v.tensor_copy(w1[:, job - 10, 512:1024], r0.bitcast(F16)[:, 512:1024])
                else:
                    k = 4 * (job - 12)
                    dve.wait_ge(sem("job_hi"), job)
                    last = v.tensor_copy(w2[:, k + 2:k + 4, :],
                                         r0.bitcast(F16)[:, 512:1024].rearrange("p (k n) -> p k n", k=2))
                last.then_inc(sem("job_lo"), 1)

            dve.wait_ge(sem("last_tr"), 1)
            v.tensor_copy(last_t[:, 0, :], r0[:, 0:B]).then_inc(sem("last_t_ready"), 1)
            v.tensor_copy(last_t[0:64, 1, :], r0[0:64, B:2 * B]).then_inc(sem("last_t_ready"), 1)
            q_stats_(0)
            dve.wait_ge(sem("wkv_split"), 1)
            v.tensor_tensor(wkv_lo[:, :, :], wkv32[:, :, :], wkv_hi[:, :, :], ALU.subtract
                            ).then_inc(sem("wkv_split"), 1)
            q_norm(0)
            dve.wait_ge(sem("last_kv"), 1)
            for a in range(A):
                last = v.tensor_copy(v_last[:, 64 * a:64 * a + 64].rearrange("p (g n) -> p g n", g=G),
                                     r1[0:B, 256:512].rearrange("p (g a n) -> p a g n", g=G, a=A)[:, a, :, :])
            last.then_inc(sem("v_last_ready"), 1)
            dve.wait_ge(sem("ident_in"), 16)
            v.tensor_copy(ident16[:, :], ident[:, :]).then_inc(sem("ident16_ready"), 1)
            context_low(0, 0)
            values_out(0, 0)

            stages = {"OT": OT, "WO": WO, "T3": T3, "norm": norm, "rms_norm": rms_norm, "H": H1, "T": TR, "G": GA,
                      "QK": QK, "gate": gate_out, "O2": O2, "q_stats": q_stats_, "q_norm": q_norm, "ST": ST, "Y": Y,
                      "y_variance": y_variance, "y_norm": y_norm, "YT": YT, "ACC": ACC, "ffn_norm": ffn_norm}

            def step(t, inside=False):
                for slot in range(TB * SLOTS):
                    b, part = slot // SLOTS, slot % SLOTS
                    now, before, next1 = (placed(t, b, k, inside) for k in (0, -1, 1))
                    pair = placed(t, b, -2, inside) if b % 2 == 1 else None
                    if part == 0 and next1:
                        context_low(*next1)
                    if part == 0 and now:
                        mask_scores(t, b, 0)
                        mask_scores(t, b, 1)
                    if part == 0 and pair:
                        output_taken(*pair)
                    if part == 1 and before:
                        probs_out(*before)
                    if part == 2 and now:
                        mask_scores(t, b, 2)
                        mask_scores(t, b, 3)
                    if part == 4 and next1:
                        values_out(*next1)
                    if not inside and t == 0 and 1 <= slot < 15:
                        weights(slot - 1)
                    for name, u in due(DVE_PLAN, slot, t, inside):
                        stages[name](u)

            run_steps(dve, step)

        @blk.gpsimd
        def _(pool):
            PASSED[pool] = sem("pool_passed")
            g_ = nc.gpsimd

            def rstd_of(u, mv_, ve, rs, mv_sem, used_sem, ve_sem, rs_sem):
                apart(pool, (mv_sem, u + 1), (used_sem, u))
                g_.tensor_scalar(ve[:, :], mv_[:, 1:2], EPS, None, ALU.add).then_inc(ve_sem, 1)
                pool.wait_ge(ve_sem, u + 1)
                g_.tensor_tensor(rs[:, :], ve[:, :], halves[:, 0, 0:1], ALU.pow).then_inc(rs_sem, 1)

            def last_key(t, b):
                n, par = 4 * t + b, b % 2
                need(pool, sem("s_done"), 4 * (n - 1))
                g_.tensor_copy(k_t[:, par, :, MF:M], k_last[:, :, bass.ds(n, 1)]).then_inc(sem("klast_ready"), 1)

            def last_value(t, b):
                n, par = 4 * t + b, b % 2
                pool.wait_ge(sem("exp_done"), 4 * n + 4)
                need(pool, sem("o_taken"), 4 * (2 * t + b // 2 - 1))
                g_.tensor_tensor(last_pv[:, b, :, :], vl[:, bass.ds(n, 1), :].rearrange("p o (g n) -> p (o g) n", g=G),
                                 prob[:, par, :, MF:M].broadcast_to([P, G, HD]), ALU.mult
                                 ).then_inc(sem("last_pv_ready"), 1)

            def output_scaled(t, b):
                pair = 2 * t + b // 2
                pool.wait_ge(sem("rsum_ready"), pair + 1)
                pool.wait_ge(sem("o_taken"), 4 * (pair + 1))
                need(pool, sem("ot_done"), t)
                g_.tensor_tensor(o_c[:, b - 1:b + 1, :].rearrange("p b (g n) -> p (b g) n", g=G),
                                 o_raw[:, :, :, :].rearrange("p b g n -> p (b g) n"),
                                 ax(rsum[:, :, :].rearrange("p b g -> p (b g)"), HD), ALU.mult
                                 ).then_inc(sem("oc_ready"), 1)

            def queries(u, b):
                n = 4 * u + b
                if b == 0:
                    pool.wait_ge(sem("q_t_ready"), u + 1)
                need(pool, sem("s_done"), 4 * (n - 4) + 4)
                g_.tensor_tensor(qbd[:, :, b, :, :],
                                 q_t[:, :, S * b:S * b + S].unsqueeze(2).broadcast_to([P, 2, A, S]),
                                 head_mask[:, :].unsqueeze(1).unsqueeze(3).broadcast_to([P, 2, A, S]), ALU.mult
                                 ).then_inc(sem("qbd_ready"), 1)

            def norm(u):
                rstd_of(u, mv, var_eps, rstd, sem("mv_ready"), sem("xn_ready"), sem("var_eps_ready"), sem("rstd_ready"))

            def nrm_(u):
                pool.wait_ge(sem("ss_ready"), u + 1)
                need(pool, sem("nrm_c_ready"), u)
                g_.tensor_tensor(nrm[:, :], sum_sq[:, :], halves[:, 1, 0:1], ALU.pow).then_inc(sem("nrm_ready"), 1)

            def low_hidden(u):
                pool.wait_ge(sem("h_hi_ready"), u + 1)
                need(pool, sem("o2_done"), u)
                g_.tensor_tensor(h_lo[:, :, :], h_g[:, :, :], h_hi[:, :, :], ALU.subtract
                                 ).then_inc(sem("h_lo_ready"), 1)

            def q_norm(u):
                rstd_of(u, q_mv, q_ve, q_rstd, sem("q_mv_ready"), sem("xnq_ready"), sem("q_ve_ready"), sem("q_rstd_ready"))

            def residual(u):
                pool.wait_ge(sem("xn_ready"), u + 1)
                need(pool, sem("x2_ready"), u)
                g_.tensor_tensor(x_res[:, :], x1[:, :], xn[:, :], ALU.add).then_inc(sem("xres_ready"), 1)
                pool.wait_ge(sem("xres_ready"), 2 * u + 1)
                g_.tensor_tensor(x_resb[:, :], x_res[:, :], b_proj[:, :], ALU.add).then_inc(sem("xres_ready"), 1)

            def qk_sum(u):
                pool.wait_ge(sem("qk_taken"), 3 * (u + 1))
                need(pool, sem("t2_done"), u)
                g_.tensor_tensor(qk[:, :, :].rearrange("p k n -> p (k n)"), qk_cos[:, :], qk_sin[:, :], ALU.add
                                 ).then_inc(sem("qk_ready"), 1)

            def v_blocks(u):
                pool.wait_ge(sem("vr_ready"), u + 1)
                need(pool, sem("y_done"), u)
                g_.tensor_tensor(vbd[:, :, :, :],
                                 vr[:, :].rearrange("p (g n) -> p g n", g=G).unsqueeze(2).broadcast_to([P, G, TB, 64]),
                                 batch_mask[:, :].unsqueeze(1).unsqueeze(3).broadcast_to([P, G, TB, 64]), ALU.mult
                                 ).then_inc(sem("vbd_ready"), 1)

            def gates(u):
                pool.wait_ge(sem("gate_ready"), u + 1)
                need(pool, sem("y_t_ready"), u)
                g_.tensor_tensor(gate_w[:, :, :], gate[:, :, :], ax(gn_w2[:, :], P), ALU.mult
                                 ).then_inc(sem("gate_w_ready"), 1)
                g_.tensor_tensor(gate_o[:, :, :], gate[:, :, :], ax(gn_b2[:, :], P), ALU.mult
                                 ).then_inc(sem("gate_o_ready"), 1)

            def r_queries(u):
                pool.wait_ge(sem("qk_t_ready"), u + 1)
                need(pool, sem("st_done"), u)
                for m in range(2):
                    last = g_.tensor_tensor(
                        rbd[:, m, :, :, :],
                        qk_t[:, m, :].rearrange("p (b r) -> p b r", b=TB).unsqueeze(2).broadcast_to([P, TB, A, S]),
                        head_mask[:, :].unsqueeze(1).unsqueeze(3).broadcast_to([P, TB, A, S]), ALU.mult)
                last.then_inc(sem("rbd_ready"), 1)

            def y_rstd_(u):
                apart(pool, (sem("y_ss_ready"), u + 1), (sem("y_n_ready"), u))
                g_.tensor_scalar(y_ve[:, :], y_ss[:, :], 1.0 / HD, EPS, ALU.mult, ALU.add).then_inc(sem("y_ve_ready"), 1)
                pool.wait_ge(sem("y_ve_ready"), u + 1)
                g_.tensor_tensor(y_rstd[:, :], y_ve[:, :], halves[:, 0, :], ALU.pow).then_inc(sem("y_rstd_ready"), 1)

            def ffn_norm(u):
                rstd_of(u, f_mv, f_ve, f_rstd, sem("f_mv_ready"), sem("f_xn_ready"), sem("f_ve_ready"), sem("f_rstd_ready"))

            def out_bias(u):
                pool.wait_ge(sem("x2_ready"), u + 1)
                need(pool, sem("y_ready"), u)
                g_.tensor_tensor(x2b[:, :], x2[:, :], b2[:, :], ALU.add).then_inc(sem("x2b_ready"), 1)

            g_.memset(halves[:, 0, :], -0.5).then_inc(sem("halves_ready"), 1)
            g_.memset(halves[:, 1, :], 0.5).then_inc(sem("halves_ready"), 1)
            g_.memset(ones[:, :], 1.0).then_inc(sem("ones_ready"), 1)
            pool.wait_ge(sem("halves_ready"), 2)
            pool.wait_ge(sem("mask_u8_in"), 16)
            g_.tensor_scalar(mask_all[:, :], mask_u8[:, :], 1.0, BIG, ALU.subtract, ALU.mult
                             ).then_inc(sem("mask_ready"), 1)
            q_norm(0)
            pool.wait_ge(sem("k_last_ready"), 1)
            last_key(0, 0)
            pool.wait_ge(sem("masks_in"), 32)
            for b in range(TB):
                queries(0, b)

            stages = {"norm": norm, "nrm": nrm_, "low_hidden": low_hidden, "q_norm": q_norm, "residual": residual,
                      "qk_sum": qk_sum, "v_blocks": v_blocks, "gates": gates, "r_queries": r_queries,
                      "y_rstd": y_rstd_, "ffn_norm": ffn_norm, "out_bias": out_bias}
            queries_at = {8: [0, 1], 13: [2], 18: [3]}

            def step(t, inside=False):
                for slot in range(TB * SLOTS):
                    b, part = slot // SLOTS, slot % SLOTS
                    now, next1 = placed(t, b, 0, inside), placed(t, b, 1, inside)
                    pair = placed(t, b, -2, inside) if b % 2 == 1 else None
                    if part == 0 and pair:
                        output_scaled(*pair)
                    if part == 2 and next1:
                        last_key(*next1)
                    if part == 4 and now:
                        if not inside and t == 0 and b == 0:
                            pool.wait_ge(sem("vl_in"), 64)
                        last_value(t, b)
                    if inside or t + 1 < T:
                        first = not inside and t == 0
                        for place in (range(TB) if slot == 18 else []) if first else queries_at.get(slot, []):
                            queries(t + 1, place)
                    if not inside and t == 0 and slot == 15:
                        pool.wait_ge(sem("vec_in"), 192)
                        g_.tensor_scalar(gn_w2[:, :], gn_w[:, :], 0.5, None, ALU.mult).then_inc(sem("gn_ready"), 1)
                        g_.tensor_scalar(gn_b2[:, :], gn_b[:, :], 0.5, None, ALU.mult).then_inc(sem("gn_ready"), 1)
                        pool.wait_ge(sem("gn_ready"), 2)
                    for name, u in due(POOL_PLAN, slot, t, inside):
                        stages[name](u)

            run_steps(pool, step)


def tables():
    f = np.float32
    p = np.arange(P)
    t = {"ident": np.eye(P, dtype=f)}
    t["head_mask"] = ((p[:, None] % 64) // HD == np.arange(A)[None, :]).astype(f)
    t["batch_mask"] = (p[:, None] // S == np.arange(TB)[None, :]).astype(f)
    half = C // 2
    pos = np.arange(S, dtype=f)
    angle = pos[:, None] * (f(1.0) / f(10000.0) ** (np.arange(half, dtype=f) / f(half)))[None, :]
    base = (np.arange(0, C, 2, dtype=f) + f(0.4 * C)) / f(1.4 * C)
    scale = base[None, :] ** ((pos - f(S // 2)) / f(128))[:, None]
    cos = np.repeat(np.concatenate([np.cos(angle) * scale, np.cos(angle) / scale], 1), 2, axis=1)
    sin = np.repeat(np.concatenate([np.sin(angle) * scale, np.sin(angle) / scale], 1), 2, axis=1)
    sin = sin * np.tile(np.array([-1.0, 1.0], f), C)[None, :]
    t["cos_t"] = np.tile(cos, (TB, 1)).astype(f)
    t["sin_t"] = np.tile(sin, (TB, 1)).astype(f)
    gamma = f(1.0) - f(2.0) ** (f(-5.0) - np.arange(H, dtype=f))
    diff = np.arange(S)[None, :] - np.arange(S)[:, None]
    by_head = np.where(diff[None] >= 0, gamma[:, None, None] ** np.maximum(diff, 0)[None].astype(f), 0) * HD ** -0.5
    by_head = by_head.reshape(2, 2, A, S, S).transpose(3, 1, 0, 2, 4).reshape(S, 2 * 2 * A * S)
    t["decay"] = np.tile(by_head, (TB, 1)).astype(f)
    return t


def kernel(**inputs):
    import concourse.bacc as bacc
    from concourse.bass_utils import run_bass_kernel_spmd as run

    nc = bacc.Bacc("TRN2", target_bir_lowering=False, num_devices=1)
    names = {"x": "x", "ctx": "ctx_768", "mask": "mask_BxS2_bf1", "wq": "L0_xattn_Wq", "wk": "L0_xattn_Wk",
             "wv": "L0_xattn_Wv", "wo": "L0_xattn_Wo", "qkvff": "L0_attn_w_qkvff", "gated": "L0_attn_w_gated",
             "b_gate": "L0_attn_b_gated", "proj": "L0_attn_w_proj", "b_proj": "L0_attn_b_proj",
             "gn_w": "L0_attn_gn_w", "gn_b": "L0_attn_gn_b", "wff": "L0_attn_w_ff", "rms": "L0_attn_rms_w",
             "w1": "L0_ffn_W1", "b1": "L0_ffn_b1", "w2": "L0_ffn_W2", "b2": "L0_ffn_b2"}
    host = {k: np.ascontiguousarray(inputs[v]) for k, v in names.items()}
    host["x"] = host["x"].reshape(B * S, C)
    host["mask"] = host["mask"].view(np.uint8)
    host.update(tables())
    arrays, d = {}, {}
    for k, a in host.items():
        arrays[f"in_{k}"] = a
        d[k] = nc.dram_tensor(f"in_{k}", a.shape, mybir.dt.from_np(a.dtype), kind="ExternalInput").ap()
    out = nc.dram_tensor("out", (B * S, C), F32, kind="ExternalOutput").ap()
    vl_dram = nc.dram_tensor("vl_dram", (B, C), F32, kind="Internal").ap()
    mask_dram = nc.dram_tensor("mask_dram", (B, M), BF16, kind="Internal").ap()
    block_kernel(nc, d, out, vl_dram, mask_dram)
    r = run(nc, [arrays], core_ids=[0])
    return r.results[0]["out"].reshape(B, S, C)
```

```python
from contextlib import ExitStack

import numpy as np

import concourse.bass as bass
from concourse import mybir

F32, F16, BF16, U8 = mybir.dt.float32, mybir.dt.float16, mybir.dt.bfloat16, mybir.dt.uint8
ALU = mybir.AluOpType
ACT = mybir.ActivationFunctionType
AX_X = mybir.AxisListType.X

B, S, C = 32, 32, 256
M, CC = 257, 192
H, HD = 16, 16
G, A = 4, 4
MF = 256
TB = 4
T = B // TB
P = 128
KR = CC - P
FF = 1024
BIG = 2.0 ** 126
HUGE = 3.0e38
EPS = 1e-5
W_UP = 64.0
P_UP = 4096.0
SLOTS = 5
PASSED = {}

PE_PLAN = {0: [("T2", 2)], 2: [("O2", 3)], 4: [("ST", 2)], 5: [("Y", 2)], 6: [("XT", -1)], 7: [("Q", -1)],
           8: [("OT", 1)], 9: [("WO", 1)], 10: [("ACCff", 2), ("YT", 2)], 11: [("ACC", 2)], 12: [("T", 1)],
           14: [("QK", 1)], 15: [("G", 1)], 16: [("FF", 1), ("T3", 2)], 17: [("VR", 1)], 18: [("Ha", 2)], 19: [("Hb", 2)]}
ACT_PLAN = {6: [("y_squares", 2), ("XT", -1)], 7: [("Q", -1)], 10: [("squares_sum", 1)],
            12: [("T", 1)], 16: [("G", 1), ("T3", 2)], 17: [("VR", 1), ("FF", 1)], 18: [("Ha", 2)],
            19: [("Hb", 2)]}
DVE_PLAN = {0: [("Hb", 3), ("T2", 2)], 3: [("O2", 3), ("q_stats", -1)], 4: [("ST", 2)], 5: [("q_norm", -1), ("Y", 2)],
            6: [("y_variance", 2)], 7: [("Q", -1)], 8: [("OT", 1)], 9: [("WO", 1), ("y_norm", 2)], 10: [("norm", 1), ("YT", 2), ("rms_norm", 1)],
            11: [("ACC", 2)], 12: [("T", 1), ("ffn_norm", 2)],
            14: [("QK", 1)], 15: [("G", 1)], 16: [("T3", 2)], 17: [("gate", 1)], 19: [("Ha", 2)]}
POOL_PLAN = {0: [("low_b", 3), ("r_queries", 2)], 4: [("q_norm", -1)], 7: [("y_rstd", 2)],
             9: [("norm", 1)], 10: [("nrm", 1)], 11: [("ffn_norm", 2)], 12: [("out_bias", 2), ("residual", 1)],
             15: [("qk_sum", 1)], 17: [("gates", 1)], 18: [("v_blocks", 1)], 19: [("low_a", 2)]}

JOBS = {0: {3 + i: ("qkvff", i) for i in range(6)} | {9: ("gated", 0), 12: ("means", 0)},
        1: {0: ("w1", 0), 1: ("w1", 1), 2: ("w2", 0), 3: ("w2", 1), 4: ("wff", 0), 10: ("proj", 0)}}
ORDER = [(step, slot) for step in JOBS for slot in JOBS[step]]
JOB_COUNT = {place: number for number, place in enumerate(ORDER)}
TERNARY = {13: (0, 0), 14: (0, 1), 16: (1, 0), 17: (1, 1)}
FIRST_STEP = {15: "XT", 16: "Q"}


def job_of(t, slot, inside):
    if not inside and (t, slot) in JOB_COUNT:
        return JOB_COUNT[t, slot], *JOBS[t][slot]
    return None


def placed(t, b, later, inside):
    tile, place = t + (b + later) // TB, (b + later) % TB
    return (tile, place) if inside or 0 <= tile < T else None


def due(plan, slot, t, inside):
    first = not inside and t == 0
    if first and FIRST_STEP.get(slot) in [name for stages in plan.values() for name, _ in stages]:
        yield FIRST_STEP[slot], 1
    for name, lag in plan.get(slot, []):
        if first and name in FIRST_STEP.values():
            continue
        if inside or 0 <= t - lag < T:
            yield name, t - lag


def run_steps(engine, step):
    for t in range(3):
        step(t)
    with engine.Fori(3, T - 1) as t:
        step(t, True)
    for t in range(T - 1, T + 3):
        step(t)


def need(engine, semaphore, value):
    if isinstance(value, int) and value <= 0:
        return
    engine.wait_ge(semaphore, value)


def apart(engine, *waits):
    waits = [w for w in waits if not (isinstance(w[1], int) and w[1] <= 0)]
    for semaphore, value in waits:
        engine.wait_ge(semaphore, value)
    if any(not isinstance(value, int) for _, value in waits):
        engine.sem_inc(PASSED[engine], 1)


def block_kernel(nc, d, out, vl_dram, mask_dram):
    with ExitStack() as ctx:
        def sb(name, shape, dt=F32):
            return ctx.enter_context(nc.sbuf_tensor(name, shape, dt))

        def ps(name, shape):
            return ctx.enter_context(nc.psum_tensor(name, shape, F32))

        sems = {}

        def sem(name):
            if name not in sems:
                sems[name] = ctx.enter_context(nc.semaphore(name))
            return sems[name]

        ident = sb("ident", [P, P])
        ident16 = sb("ident16", [P, P], F16)
        ones = sb("ones", [P, P])
        halves = sb("halves", [P, 2, G * TB])
        cos_t = sb("cos_t", [P, 2 * C])
        sin_t = sb("sin_t", [P, 2 * C])
        decay = sb("decay", [P, 2, 2 * P])
        head_mask = sb("head_mask", [P, A])
        batch_mask = sb("batch_mask", [P, TB])
        wq = sb("wq", [P, 2, C])
        wkv32 = sb("wkv32", [P, 4, C])
        wkv_hi = sb("wkv_hi", [P, 4, C], F16)
        wkv_lo = sb("wkv_lo", [P, 4, C], F16)
        wo = sb("wo", [P, 2, C])
        qkvff_n = sb("qkvff_n", [P, 10, C])
        gated_n = sb("gated_n", [P, 2, C])
        proj_n = sb("proj_n", [P, 2, C])
        ff_n = sb("ff_n", [P, 2, 2 * C])
        w1_n = sb("w1_n", [P, 8, C])
        w2_n = sb("w2_n", [P, 2, FF])
        rms = sb("rms", [P, 2])
        rms_up = sb("rms_up", [P, 2])
        b_gate = sb("b_gate", [P, 2])
        gn_w = sb("gn_w", [P, 2])
        gn_b = sb("gn_b", [P, 2])
        gn_w2 = sb("gn_w2", [P, 2])
        gn_b2 = sb("gn_b2", [P, 2])
        b1 = sb("b1", [P, 8])
        b_proj = sb("b_proj", [P, C])
        b2 = sb("b2", [P, C])
        qkvff_hi = sb("qkvff_hi", [P, 2, 5 * C], F16)
        qkvff_lo = sb("qkvff_lo", [P, 2, 5 * C], F16)
        gated_hi = sb("gated_hi", [P, 2, C], F16)
        gated_lo = sb("gated_lo", [P, 2, C], F16)
        wff = sb("wff", [P, 4, C])
        wproj = sb("wproj", [P, 2, C])
        w1_t = sb("w1_t", [P, 8, C], F16)
        w2_t = sb("w2_t", [P, 2, FF], F16)
        below = sb("below", [P, 2 * FF], F16)
        scratch = sb("scratch", [P, 2 * FF])
        w1 = sb("w1", [P, 2, FF], F16)
        w2 = sb("w2", [P, 8, C], F16)
        abs_sum = sb("abs_sum", [P, 2])
        mean_abs = sb("mean_abs", [P, 2])
        thr_up = sb("thr_up", [P, 2])
        thr_down = sb("thr_down", [P, 2])

        last_n = sb("last_n", [B, CC])
        last_t = sb("last_t", [P, 2, B])
        kl_hi = sb("kl_hi", [P, 2, B], F16)
        kl_lo = sb("kl_lo", [P, 2, B], F16)
        v_last = sb("v_last", [B, C])
        vl = sb("vl", [P, B, 64])

        xq = sb("xq", [P, C])
        q_stats = sb("q_stats", [P, 6])
        q_mv = sb("q_mv", [P, 2])
        q_ve = sb("q_ve", [P, 1])
        q_rstd = sb("q_rstd", [P, 1])
        xnq = sb("xnq", [P, C])
        xq_t = sb("xq_t", [P, 2, P])
        q_hi = sb("q_hi", [P, 2, P], F16)
        q_lo = sb("q_lo", [P, 2, P], F16)
        qbd_hi = sb("qbd_hi", [P, 2, TB, A, S], F16)
        qbd_lo = sb("qbd_lo", [P, 2, TB, A, S], F16)
        ctx_s = sb("ctx_s", [P, TB, 2, CC + KR])
        mask_u8 = sb("mask_u8", [B, M], U8)
        mask_all = sb("mask_all", [B, M], BF16)
        mask_b = sb("mask_b", [P, TB, M], BF16)
        c_hi = sb("c_hi", [P, 2, 4, P], F16)
        c_lo = sb("c_lo", [P, 2, 2, P], F16)
        k_hi = sb("k_hi", [P, 2, 2, M], F16)
        k_lo = sb("k_lo", [P, 2, 2, M], F16)
        v_s = sb("v_s", [P, TB, 2, G, 2, 64], F16)
        sm = sb("sm", [P, G, M])
        neg_max = sb("neg_max", [P, G])
        prob = sb("prob", [P, 2, G, M])
        sums = sb("sums", [P, TB, G])
        p_hi = sb("p_hi", [P, 2, 4, P], F16)
        p_lo = sb("p_lo", [P, 2, 4, P], F16)
        rsum = sb("rsum", [P, 2, G])
        last_pv = sb("last_pv", [P, TB, G, HD])
        o_raw = sb("o_raw", [P, 2, G, HD])
        o_sum = sb("o_sum", [P, 2, G, HD])
        o_c = sb("o_c", [P, TB, 64])

        o_t = sb("o_t", [P, 2, TB, S])
        xr = sb("xr", [P, C])
        x1 = sb("x1", [P, C])
        stats = sb("stats", [P, 6])
        mv = sb("mv", [P, 2])
        var_eps = sb("var_eps", [P, 1])
        rstd = sb("rstd", [P, 1])
        xn = sb("xn", [P, C])
        squares = sb("squares", [P, C])
        sum_sq = sb("sum_sq", [P, 1])
        nrm = sb("nrm", [P, 1])
        nrm_c = sb("nrm_c", [P, 1])
        rnrm = sb("rnrm", [P, 1])
        xu = sb("xu", [P, C])
        x_hi = sb("x_hi", [P, 4, P], F16)
        x_lo = sb("x_lo", [P, 4, P], F16)
        gate_b = sb("gate_b", [P, 2, P])
        gate_th = sb("gate_th", [P, 2, P])
        gate = sb("gate", [P, 2, P])
        gate_w = sb("gate_w", [P, 2, P])
        gate_o = sb("gate_o", [P, 2, P])
        below2 = scratch.bitcast(F16)[:, 0:2 * FF]
        qk_cos, qk_sin = scratch[:, 0:512], scratch[:, 512:1024]
        qk = scratch[:, 1024:1536].rearrange("p (k n) -> p k n", k=4)
        qk_t = scratch[:, 1536:2048].rearrange("p (k n) -> p k n", k=4)
        rbd = w2_n[:, 0, :].rearrange("p (m b a r) -> p m b a r", m=2, b=TB, a=A)
        vr = sb("vr", [P, C])
        vbd = w2_n[:, 1, :].rearrange("p (g b n) -> p g b n", g=G, b=TB)
        ff_g = sb("ff_g", [P, 4, P])
        st = sb("st", [P, 2, 2, P])
        y_sum = sb("y_sum", [P, TB * G])
        y_mean = sb("y_mean", [P, TB * G])
        y_ctr = sb("y_ctr", [P, TB * G, HD])
        y_sq = sb("y_sq", [P, TB * G, HD])
        y_ss = sb("y_ss", [P, TB * G])
        y_ve = sb("y_ve", [P, TB * G])
        y_rstd = sb("y_rstd", [P, TB * G])
        y_n = sb("y_n", [P, TB, G, HD])
        y_g = sb("y_g", [P, 2, TB, S])
        y_t = sb("y_t", [P, 2, TB, S])
        x_res = sb("x_res", [P, C])
        x_resb = sb("x_resb", [P, C])
        x2 = sb("x2", [P, C])

        f_stats = sb("f_stats", [P, 6])
        f_mv = sb("f_mv", [P, 2])
        f_ve = sb("f_ve", [P, 1])
        f_rstd = sb("f_rstd", [P, 1])
        f_xn = sb("f_xn", [P, C])
        f_hi = sb("f_hi", [P, 2, P], F16)
        f_lo = sb("f_lo", [P, 2, P], F16)
        h_g = w1_n[:, 0:4, :].rearrange("p k (i n) -> p (k i) n", i=2)
        h_hi = w1_t[:, 0:4, :].rearrange("p k (i n) -> p (k i) n", i=2)
        h_lo = w1_t[:, 4:8, :].rearrange("p k (i n) -> p (k i) n", i=2)
        x2b = sb("x2b", [P, C])
        y_out = sb("y_out", [P, C])

        p_ct = ps("p_ct", [P, 512])
        p_kv = ps("p_kv", [P, 512])
        p_s = [ps("p_s0", [P, 512]), ps("p_s1", [P, 512])]
        p_pt = ps("p_pt", [P, 512])
        p_o = ps("p_o", [P, 512])
        p_r = ps("p_r", [P, 1024])
        r0, r1 = p_r[:, 0:512], p_r[:, 512:1024]

        def ax(ap, n):
            return ap.unsqueeze(2).broadcast_to([ap.shape[0], ap.shape[1], n])

        def by_group(w, k):
            return [w[:, k, P * h + 64 * pair:P * h + 64 * pair + 64].rearrange("p (g e) -> p g e", g=G)
                    for pair in range(2) for h in range(2)]

        def load_kv_weights(engine, w, i):
            engine.dma_start(wkv32[:, i, :], d[w][0:P, :]).then_inc(sem(f"{w}_in"), 16)
            engine.dma_start(wkv32[0:64, i + 1, :], d[w][P:CC, :]).then_inc(sem(f"{w}_in"), 16)
            engine.dma_start(wkv32[64:P, i + 1, :], d[w][P:CC, :]).then_inc(sem(f"{w}_in"), 16)

        def bank_of(job):
            return r1 if job % 2 == 1 and job < 12 else r0

        def by_head(w):
            return [w.rearrange("p (g a e) -> p a g e", g=G, a=A)[:, a, :, :] for a in range(A)]

        x_rows = d["x"]
        ctx.enter_context(nc.allow_non_contiguous_dma(reason="a few vectors of up to 1024 elements go across partitions"))
        blk = ctx.enter_context(nc.Block())

        @blk.sync
        def _(sp):
            def load_context(t, b):
                n = 4 * t + b
                need(sp, sem("ct_done"), n - 3)
                src = d["ctx"][bass.ds(n, 1), 0:MF, :].rearrange("o (j p) c -> p (o j) c", p=P)
                sp.dma_start(ctx_s[:, b, :, 0:CC], src).then_inc(sem(f"ctx_in{b}"), 16)
                sp.dma_start(ctx_s[:, b, :, CC:], src[:, :, P:CC]).then_inc(sem(f"ctx_in{b}"), 16)

            def load_mask(t, b):
                n = 4 * t + b
                need(sp, sem("masked"), 4 * (n - 3))
                sp.dma_start(mask_b[:, b, :], mask_dram[bass.ds(n, 1), :].broadcast_to([P, M])
                             ).then_inc(sem(f"mask_in{b}"), 16)

            def load_xq(t):
                need(sp, sem("xnq_ready"), t)
                sp.dma_start(xq[:, :], x_rows[bass.ds(t * P, P), :]).then_inc(sem("xq_in"), 16)

            sp.dma_start(ident[:, :], d["ident"]).then_inc(sem("ident_in"), 16)
            load_context(0, 0)
            load_kv_weights(sp, "wv", 2)
            sp.dma_start(last_n[:, :], d["ctx"][:, MF, :]).then_inc(sem("last_in"), 16)
            load_xq(0)
            sp.dma_start(mask_u8[:, :], d["mask"]).then_inc(sem("mask_u8_in"), 16)
            sp.dma_start(wq[:, :, :], d["wq"].rearrange("(k p) n -> p k n", p=P)).then_inc(sem("wq_in"), 16)
            load_context(0, 1)
            sp.dma_start(head_mask[:, :], d["head_mask"]).then_inc(sem("masks_in"), 16)
            sp.dma_start(batch_mask[:, :], d["batch_mask"]).then_inc(sem("masks_in"), 16)
            for b in range(2, TB):
                load_context(0, b)
            sp.wait_ge(sem("mask_ready"), 1)
            sp.dma_start(mask_dram[:, :], mask_all[:, :]).then_inc(sem("mask_out"), 16)
            sp.wait_ge(sem("mask_out"), 16)
            for b in range(TB):
                load_mask(0, b)

            sp.wait_ge(sem("v_last_ready"), 1)
            sp.dma_start(vl_dram[:, :], v_last[:, :]).then_inc(sem("vl_out"), 16)
            sp.wait_ge(sem("vl_out"), 16)

            def load_last_values(first, last, loaded):
                for a in range(A):
                    sp.dma_start(vl[32 * a:32 * a + 32, first:last, :],
                                 vl_dram[first:last, 64 * a:64 * a + 64].unsqueeze(0).broadcast_to([S, last - first, 64])
                                 ).then_inc(sem(loaded), 16)

            load_last_values(0, TB, "vl_in")
            load_xq(1)
            sp.dma_start(rms[:, :], d["rms"].rearrange("(k p) -> p k", p=P)).then_inc(sem("w_in0"), 16)
            sp.dma_start(qkvff_n[:, :, :], d["qkvff"].rearrange("(k p) n -> p k n", p=P)).then_inc(sem("w_in0"), 16)
            load_context(1, 0)
            load_context(1, 1)
            sp.dma_start(gated_n[:, :, :], d["gated"].rearrange("(k p) n -> p k n", p=P)).then_inc(sem("w_in1"), 16)
            sp.dma_start(w1_n[:, :, :], d["w1"].rearrange("(k p) n -> p k n", p=P)).then_inc(sem("w_in2"), 16)
            sp.dma_start(w2_n[:, :, :], d["w2"].rearrange("(k p) n -> p k n", p=P)).then_inc(sem("w_in2"), 16)
            for a in range(A):
                sp.dma_start(wo[64 * (a // 2):64 * (a // 2) + 64, a % 2, :],
                             d["wo"].rearrange("(g a e) n -> g a e n", g=G, a=A)[:, a, :, :]
                             ).then_inc(sem("wo_in"), 16)
            sp.dma_start(ff_n[:, :, :], d["wff"].rearrange("(k p) n -> p k n", p=P)).then_inc(sem("w_in3"), 16)
            for i in range(2):
                for a in range(A):
                    at = P * (a % 2) + 64 * (a // 2)
                    src = d["proj"][P * i:P * i + P, :].rearrange("p (g a e) -> p a g e", g=G, a=A)[:, a, :, :]
                    sp.dma_start(proj_n[:, i, at:at + 64].rearrange("p (g e) -> p g e", g=G), src
                                 ).then_inc(sem("w_in3"), 16)
            for name, tile in (("cos_t", cos_t), ("sin_t", sin_t)):
                sp.dma_start(tile[:, :], d[name]).then_inc(sem("tab_in"), 16)
            sp.dma_start(decay[:, :, :], d["decay"].rearrange("p (h n) -> p h n", h=2)).then_inc(sem("tab_in"), 16)
            for name, tile in (("b_proj", b_proj), ("b2", b2)):
                sp.dma_start(tile[:, :], d[name].unsqueeze(0).broadcast_to([P, C])).then_inc(sem("tab_in"), 16)
            sp.dma_start(b1[:, :], d["b1"].rearrange("(k p) -> p k", p=P)).then_inc(sem("tab_in"), 16)
            for name, tile in (("b_gate", b_gate), ("gn_w", gn_w), ("gn_b", gn_b)):
                for a in range(A):
                    sp.dma_start(tile[64 * (a // 2):64 * (a // 2) + 64, a % 2:a % 2 + 1],
                                 d[name].rearrange("(g a e) -> g a e", g=G, a=A)[:, a, :].unsqueeze(2)
                                 ).then_inc(sem("vec_in"), 16)
            load_last_values(TB, B, "vl_rest_in")
            sp.sem_inc(sem("out_free"), 16)

            def step(t, inside=False):
                for b in range(TB):
                    if b == 0 and (inside or 0 < t < T - 1):
                        load_xq(t + 1)
                    if b == 0 and (inside or 0 <= t - 1 < T):
                        need(sp, sem("x1_ready"), t - 1)
                        sp.dma_start(xr[:, :], x_rows[bass.ds((t - 1) * P, P), :]).then_inc(sem("xr_in"), 16)
                    if inside or t + 1 < T:
                        if inside or t > 0 or b > 1:
                            load_context(t + 1, b)
                        load_mask(t + 1, b)
                    if b == 2 and (inside or 0 <= t - 3 < T):
                        sp.wait_ge(sem("y_ready"), t - 2)
                        sp.dma_start(out[bass.ds((t - 3) * P, P), :], y_out[:, :]).then_inc(sem("out_free"), 16)

            run_steps(sp, step)
            sp.wait_ge(sem("out_free"), 16 * (T + 1))

        @blk.tensor
        def _(pe):
            PASSED[pe] = sem("pe_passed")
            mm = nc.tensor.matmul

            def context_transposed(t, b):
                n = 4 * t + b
                pe.wait_ge(sem(f"ctx_in{b}"), 32 * (t + 1))
                need(pe, sem("hi_done"), n)
                need(pe, sem("lo_done"), 2 * n)
                for j in range(2):
                    nc.tensor.transpose(p_ct[:, P * j:P * j + P], ctx_s[:, b, j, 0:P], ident[:, :])
                for j in range(2):
                    last = nc.tensor.transpose(p_ct[:, 256 + P * j:256 + P * j + P], ctx_s[:, b, j, P:], ident[:, :])
                last.then_inc(sem("ct_done"), 1)

            def keys(t, b):
                n, par = 4 * t + b, b % 2
                pe.wait_ge(sem("hi_done"), n + 1)
                pe.wait_ge(sem("lo_done"), 2 * n + 2)
                if isinstance(t, int) and n == 0:
                    pe.wait_ge(sem("wkv_split"), 2)
                need(pe, sem("v_lo_ready"), n)
                for m in range(2):
                    o = p_kv[:, 256 * m:256 * m + 256]
                    c = slice(P * m, P * m + P)
                    mm(o, wkv_hi[:, 0, c], c_hi[:, par, 0:2, :], start=True, stop=False)
                    mm(o, wkv_lo[:, 0, c], c_hi[:, par, 0:2, :], start=False, stop=False)
                    mm(o, wkv_hi[:, 0, c], c_lo[:, par, :, :], start=False, stop=False)
                    mm(o, wkv_hi[:, 1, c], c_hi[:, par, 2:4, :], start=False, stop=False)
                    last = mm(o, wkv_lo[0:64, 1, c], c_hi[0:64, par, 2:4, :], start=False, stop=True)
                last.then_inc(sem("k_done"), 1)

            def values(t, b):
                n, par = 4 * t + b, b % 2
                pe.wait_ge(sem("k_lo_ready"), n + 1)
                for j in range(2):
                    o = p_kv[:, 256 * j:256 * j + 256]
                    mm(o, c_hi[:, par, j, :], wkv_hi[:, 2, :], start=True, stop=False)
                    mm(o, c_hi[:, par, j, :], wkv_lo[:, 2, :], start=False, stop=False)
                    mm(o, c_lo[:, par, j, :], wkv_hi[:, 2, :], start=False, stop=False)
                    mm(o, c_hi[:, par, 2 + j, :], wkv_hi[:, 3, :], start=False, stop=False)
                    last = mm(o, c_hi[0:64, par, 2 + j, :], wkv_lo[0:64, 3, :], start=False, stop=True)
                last.then_inc(sem("v_done"), 1)

            def scores(t, b, g):
                n, par, m, half = 4 * t + b, b % 2, g // 2, g % 2
                if g == 0:
                    pe.wait_ge(sem("qbd_ready"), n + 1)
                    pe.wait_ge(sem("k_lo_ready"), n + 1)
                    pe.wait_ge(sem("klast_ready"), n + 1)
                need(pe, sem("masked"), 4 * n + g - 1)
                rows = slice(64 * half, 64 * half + 64)
                o = p_s[half][:, 0:M]
                mm(o, qbd_hi[rows, m, b, :, :], k_hi[rows, par, m, :], start=True, stop=False)
                mm(o, qbd_hi[rows, m, b, :, :], k_lo[rows, par, m, :], start=False, stop=False)
                mm(o, qbd_lo[rows, m, b, :, :], k_hi[rows, par, m, :], start=False, stop=True
                   ).then_inc(sem("s_done"), 1)

            def probs_transposed(t, b, pair):
                n, par = 4 * t + b, b % 2
                pe.wait_ge(sem("exp_done"), 4 * n + 2 * pair + 2)
                if pair == 0:
                    need(pe, sem("p_lo1_ready"), n)
                else:
                    pe.wait_ge(sem("p_lo0_ready"), n + 1)
                for i in range(2):
                    for j in range(2):
                        at = P * (2 * i + j)
                        last = nc.tensor.transpose(p_pt[:, at:at + P], prob[:, par, 2 * pair + i, P * j:P * j + P],
                                                   ident[:, :])
                last.then_inc(sem("pt_done"), 1)

            def attend(t, b, pair):
                n, par = 4 * t + b, b % 2
                pe.wait_ge(sem(f"p_hi{pair}_ready"), n + 1)
                pe.wait_ge(sem(f"p_lo{pair}_ready"), n + 1)
                if pair == 0:
                    pe.wait_ge(sem("v_hi_ready"), n + 1)
                    pe.wait_ge(sem("v_lo_ready"), n + 1)
                    need(pe, sem("o_taken"), 4 * n)
                for i in range(2):
                    g = 2 * pair + i
                    for j in range(2):
                        mm(p_o[:, P * g:P * g + P], p_hi[:, pair, 2 * i + j, :], v_s[:, b, j, g, :, :],
                           start=(j == 0), stop=False)
                        last = mm(p_o[:, P * g:P * g + 64], p_lo[:, pair, 2 * i + j, :], v_s[:, b, j, g, 0, :],
                                  start=False, stop=(j == 1))
                last.then_inc(sem("pv_done"), 1)

            def heads_transposed(o, rows):
                for b in range(TB):
                    for pair in range(2):
                        half = slice(64 * pair, 64 * pair + 64)
                        last = mm(o[half, 64 * b:64 * b + 64], rows[b], ident[:, half], start=True, stop=True)
                return last

            def OT(u):
                apart(pe, (sem("oc_ready"), 2 * u + 2))
                last = heads_transposed(r1, [o_c[:, b, :] for b in range(TB)])
                last.then_inc(sem("ot_done"), 1)

            def WO(u):
                if isinstance(u, int) and u == 0:
                    pe.wait_ge(sem("wo_ready"), 1)
                pe.wait_ge(sem("ot_ready"), u + 1)
                for h in range(2):
                    last = mm(r1[:, 0:C], o_t[:, h, :, :], wo[:, h, :], start=(h == 0), stop=(h == 1))
                last.then_inc(sem("wo_done"), 1)

            def T3(u):
                pe.wait_ge(sem("f_xn_ready"), u + 1)
                if not (isinstance(u, int) and u + 1 == T):
                    pe.wait_ge(sem("qk_taken"), 3 * (u + 2))
                for k in range(2):
                    last = nc.tensor.transpose(r1[:, P * k:P * k + P], f_xn[:, P * k:P * k + P], ident[:, :])
                last.then_inc(sem("t3_done"), 1)

            def XT(u):
                pe.wait_ge(sem("xnq_ready"), u + 1)
                need(pe, sem("q_lo_ready"), u)
                need(pe, sem("y_ctr_ready"), u - 2)
                for k in range(2):
                    last = nc.tensor.transpose(r0[:, P * k:P * k + P], xnq[:, P * k:P * k + P], ident[:, :])
                last.then_inc(sem("xt_done"), 1)

            def Q(u):
                pe.wait_ge(sem("xq_t_ready"), u + 1)
                for m in range(2):
                    for k in range(2):
                        last = mm(r0[:, P * m:P * m + P], wq[:, k, P * m:P * m + P], xq_t[:, k, :],
                                  start=(k == 0), stop=(k == 1))
                last.then_inc(sem("q_done"), 1)

            def hidden(u, bank, first):
                for m in range(4):
                    o, c = bank[:, P * m:P * m + P], slice(P * (first + m), P * (first + m) + P)
                    for k in range(2):
                        mm(o, w1[:, k, c], f_hi[:, k, :], start=(k == 0), stop=False)
                        last = mm(o, w1[:, k, c], f_lo[:, k, :], start=False, stop=(k == 1))
                last.then_inc(sem("h_done"), 1)

            def Ha(u):
                pe.wait_ge(sem("f_hi_ready"), u + 1)
                pe.wait_ge(sem("f_lo_ready"), u + 1)
                if not (isinstance(u, int) and u + 1 == T):
                    pe.wait_ge(sem("vr_ready"), u + 2)
                hidden(u, r1, 0)

            def Hb(u):
                if not (isinstance(u, int) and u + 1 == T):
                    pe.wait_ge(sem("ff_g_ready"), u + 2)
                hidden(u, r0, 4)

            def TR(u):
                pe.wait_ge(sem("xn_ready"), u + 1)
                pe.wait_ge(sem("xu_ready"), u + 1)
                need(pe, sem("x2_ready"), u)
                if isinstance(u, int) and u == 0:
                    pe.wait_ge(sem("q_lo_ready"), 3)
                for k in range(2):
                    nc.tensor.transpose(r0[:, P * k:P * k + P], xn[:, P * k:P * k + P], ident[:, :])
                for k in range(2):
                    last = nc.tensor.transpose(r0[:, 256 + P * k:256 + P * k + P], xu[:, P * k:P * k + P], ident[:, :])
                last.then_inc(sem("tr_done"), 1)

            def three(o, cols):
                for k in range(2):
                    mm(o, x_hi[:, 2 + k, :], qkvff_hi[:, k, cols], start=(k == 0), stop=False)
                    mm(o, x_hi[:, 2 + k, :], qkvff_lo[:, k, cols], start=False, stop=False)
                    last = mm(o, x_lo[:, 2 + k, :], qkvff_hi[:, k, cols], start=False, stop=(k == 1))
                return last

            def QK(u):
                pe.wait_ge(sem("x_hi_ready"), u + 1)
                pe.wait_ge(sem("x_lo_ready"), u + 1)
                three(r1[:, :], slice(0, 2 * C)).then_inc(sem("qk_done"), 1)

            def GA(u):
                for h in range(2):
                    o = r0[:, P * h:P * h + P]
                    for k in range(2):
                        w_hi, w_lo = gated_hi[:, k, P * h:P * h + P], gated_lo[:, k, P * h:P * h + P]
                        mm(o, w_hi, x_hi[:, k, :], start=(k == 0), stop=False)
                        mm(o, w_lo, x_hi[:, k, :], start=False, stop=False)
                        last = mm(o, w_hi, x_lo[:, k, :], start=False, stop=(k == 1))
                last.then_inc(sem("g_done"), 1)

            def VR(u):
                pe.wait_ge(sem("qk_taken"), 3 * (u + 1))
                need(pe, sem("f_lo_ready"), u)
                three(r1[:, 0:C], slice(2 * C, 3 * C)).then_inc(sem("vr_done"), 1)

            def O2(u):
                if not (isinstance(u, int) and u + 1 == T):
                    pe.wait_ge(sem("qk_t_ready"), u + 2)
                for f in range(8):
                    if f % 4 == 0:
                        pe.wait_ge(sem("h_lo_ready"), 2 * u + 1 + f // 4)
                    mm(r1[:, 0:C], h_hi[:, f, :], w2[:, f, :], start=(f == 0), stop=False)
                    last = mm(r1[:, 0:C], h_lo[:, f, :], w2[:, f, :], start=False, stop=(f == 7))
                last.then_inc(sem("o2_done"), 1)

            def FFN(u):
                pe.wait_ge(sem("gate_b_ready"), u + 1)
                for e in range(4):
                    o = r0[:, P * e:P * e + P]
                    c = slice(3 * C + P * e, 3 * C + P * e + P)
                    for k in range(2):
                        mm(o, qkvff_hi[:, k, c], x_hi[:, 2 + k, :], start=(k == 0), stop=False)
                        mm(o, qkvff_lo[:, k, c], x_hi[:, 2 + k, :], start=False, stop=False)
                        last = mm(o, qkvff_hi[:, k, c], x_lo[:, 2 + k, :], start=False, stop=(k == 1))
                last.then_inc(sem("ff_done"), 1)

            def T2(u):
                pe.wait_ge(sem("qk_ready"), u + 1)
                if isinstance(u, int) and u == 0:
                    pe.wait_ge(sem("vr_ready"), 1)
                need(pe, sem("h_g_ready"), 8 * u - 4)
                for i in range(4):
                    last = nc.tensor.transpose(r1[:, P * i:P * i + P], qk[:, i, :], ident[:, :])
                last.then_inc(sem("t2_done"), 1)

            def ST(u):
                apart(pe, (sem("rbd_ready"), u + 1), (sem("ff_g_ready"), u + 1), (sem("h_g_ready"), 8 * u),
                      (sem("y_ready"), u))
                for half in range(2):
                    rows = slice(64 * half, 64 * half + 64)
                    for m in range(2):
                        for b in range(TB):
                            last = mm(p_r[32 * b:32 * b + 32, 512 * half + P * m:512 * half + P * m + P],
                                      qk_t[rows, 2 + m, 32 * b:32 * b + 32], rbd[rows, m, b, :, :],
                                      start=True, stop=True)
                last.then_inc(sem("st_done"), 1)

            def Y(u):
                apart(pe, (sem("st_ready"), 2 * (u + 1)), (sem("vbd_ready"), u + 1))
                for g in range(G):
                    m, half = g // 2, g % 2
                    for a in range(A):
                        last = mm(r0[32 * a:32 * a + 32, 64 * g:64 * g + 64], st[:, half, m, 32 * a:32 * a + 32],
                                  vbd[:, g, :, 16 * a:16 * a + 16], start=True, stop=True)
                last.then_inc(sem("y_done"), 1)

            def ACCff(u):
                pe.wait_ge(sem("y_ctr_ready"), u + 1)
                if not isinstance(u, int) or u + 3 < T:
                    pe.wait_ge(sem("q_lo_ready"), u + 4)
                for e in range(4):
                    mm(r0[:, 0:C], ff_g[:, e, :], wff[:, e, :], start=(e == 0), stop=False)

            def YT(u):
                more = not isinstance(u, int) or u + 1 < T
                apart(pe, (sem("y_n_ready"), u + 1), (sem("x1_ready"), u + 2 if more else 0))
                heads_transposed(r1, [y_n[:, b, :, :] for b in range(TB)]).then_inc(sem("yt_done"), 1)

            def ACC(u):
                pe.wait_ge(sem("y_t_ready"), u + 1)
                for h in range(2):
                    last = mm(r0[:, 0:C], y_t[:, h, :, :], wproj[:, h, :], start=False, stop=(h == 1))
                last.then_inc(sem("acc_done"), 1)

            def weights(job, name, part):
                if job == 0:
                    pe.wait_ge(sem("w_in0"), 32)
                    pe.wait_ge(sem("q_lo_ready"), 1)
                    pe.wait_ge(sem("k_last_ready"), 1)
                    pe.wait_ge(sem("v_last_ready"), 1)
                before = job if name in ("wff", "proj") else job - 1
                need(pe, sem("job_hi"), before)
                need(pe, sem("job_lo"), before)
                bank = bank_of(job)
                if name == "qkvff":
                    k, lot = part // 3, part % 3
                    for i in range(4 if lot < 2 else 2):
                        last = nc.tensor.transpose(bank[:, P * i:P * i + P], qkvff_n[:, 4 * lot + i, P * k:P * k + P],
                                                   ident[:, :])
                elif name == "gated":
                    pe.wait_ge(sem("w_in1"), 16)
                    for k in range(2):
                        for i in range(2):
                            last = nc.tensor.transpose(bank[:, 256 * k + P * i:256 * k + P * i + P],
                                                       gated_n[:, i, P * k:P * k + P], ident[:, :])
                elif name == "means":
                    pe.wait_ge(sem("abs_ready"), 2)
                    pe.wait_ge(sem("ones_ready"), 1)
                    last = mm(bank[:, 0:2], ones[:, :], abs_sum[:, :], start=True, stop=True)
                elif name == "w1":
                    if part == 0:
                        pe.wait_ge(sem("q_lo_ready"), 2)
                        pe.wait_ge(sem("ternary_ready"), 4)
                        pe.wait_ge(sem("ident16_ready"), 1)
                    o = bank.bitcast(F16)
                    for i in range(8):
                        last = nc.tensor.transpose(o[:, P * i:P * i + P], w1_t[:, i, P * part:P * part + P],
                                                   ident16[:, :])
                elif name == "w2":
                    o = bank.bitcast(F16)
                    for f in range(4):
                        for i in range(2):
                            at, col = 256 * f + P * i, P * (4 * part + f)
                            last = nc.tensor.transpose(o[:, at:at + P], w2_t[:, i, col:col + P], ident16[:, :])
                elif name == "wff":
                    pe.wait_ge(sem("w_in3"), 16 * 9)
                    for e in range(4):
                        for i in range(2):
                            last = nc.tensor.transpose(p_r[:, 256 * e + P * i:256 * e + P * i + P],
                                                       ff_n[:, i, P * e:P * e + P], ident[:, :])
                else:
                    pe.wait_ge(sem("q_lo_ready"), 3)
                    for h in range(2):
                        for i in range(2):
                            last = nc.tensor.transpose(bank[:, 256 * h + P * i:256 * h + P * i + P],
                                                       proj_n[:, i, P * h:P * h + P], ident[:, :])
                last.then_inc(sem("job_done"), 1)

            stages = {"OT": OT, "WO": WO, "T3": T3, "XT": XT, "Q": Q, "T": TR, "G": GA, "QK": QK, "VR": VR,
                      "Ha": Ha, "Hb": Hb,
                      "O2": O2, "FF": FFN, "T2": T2, "ST": ST, "Y": Y, "YT": YT, "ACC": ACC, "ACCff": ACCff}

            pe.wait_ge(sem("ident_in"), 16)
            context_transposed(0, 0)
            pe.wait_ge(sem("last_in"), 16)
            nc.tensor.transpose(r0[:, 0:B], last_n[:, 0:P], ident[0:B, 0:B])
            nc.tensor.transpose(r0[0:KR, B:2 * B], last_n[:, P:CC], ident[0:B, 0:B]).then_inc(sem("last_tr"), 1)
            keys(0, 0)
            pe.wait_ge(sem("last_t_ready"), 2)
            for m in range(2):
                mm(r1[:, B * m:B * m + B], wkv32[:, 0, P * m:P * m + P], last_t[:, 0, :], start=True, stop=False)
                mm(r1[:, B * m:B * m + B], wkv32[0:64, 1, P * m:P * m + P], last_t[0:64, 1, :], start=False, stop=True)
            mm(r1[0:B, 256:512], last_t[:, 0, :], wkv32[:, 2, :], start=True, stop=False)
            mm(r1[0:B, 256:512], last_t[0:64, 1, :], wkv32[0:64, 3, :], start=False, stop=True).then_inc(sem("last_kv"), 1)
            XT(0)
            values(0, 0)
            pe.wait_ge(sem("wq_in"), 16)
            Q(0)
            context_transposed(0, 1)

            def step(t, inside=False):
                for slot in range(TB * SLOTS):
                    b, part = slot // SLOTS, slot % SLOTS
                    now, before, before2, next1, next2 = (placed(t, b, k, inside) for k in (0, -1, -2, 1, 2))
                    if part == 0 and now:
                        scores(t, b, 0)
                        scores(t, b, 1)
                    if part == 0 and before2:
                        attend(*before2, 1)
                    if part == 1 and before:
                        probs_transposed(*before, 0)
                    if part == 1 and next1:
                        keys(*next1)
                    if part == 2 and now:
                        scores(t, b, 2)
                        scores(t, b, 3)
                    if part == 3 and before:
                        probs_transposed(*before, 1)
                    if part == 3 and next1:
                        values(*next1)
                    if part == 4 and next2:
                        context_transposed(*next2)
                    if part == 4 and before:
                        attend(*before, 0)
                    if job_of(t, slot, inside):
                        weights(*job_of(t, slot, inside))
                    if not inside and (t, slot) in ((0, 15), (1, 6), (1, 12)):
                        jobs = 1 + max(JOB_COUNT[t, s] for s in JOBS[t] if s < slot)
                        pe.wait_ge(sem("job_hi"), jobs)
                        pe.wait_ge(sem("job_lo"), jobs)
                    for name, u in due(PE_PLAN, slot, t, inside):
                        stages[name](u)

            run_steps(pe, step)

        @blk.scalar
        def _(act):
            def copy(o, i, scale=1.0):
                return nc.scalar.activation(o, i, ACT.Copy, scale=scale)

            def context_high(t, b):
                n, par = 4 * t + b, b % 2
                act.wait_ge(sem("ct_done"), n + 1)
                need(act, sem("v_done"), n - 1)
                copy(c_hi[:, par, :, :], p_ct[:, :].rearrange("p (j n) -> p j n", j=4)).then_inc(sem("hi_done"), 1)

            def keys_high(t, b):
                n, par = 4 * t + b, b % 2
                act.wait_ge(sem("k_done"), n + 1)
                need(act, sem("s_done"), 4 * (n - 1))
                copy(k_hi[:, par, :, 0:MF], p_kv[:, :].rearrange("p (m n) -> p m n", m=2),
                     1 / W_UP).then_inc(sem("k_hi_ready"), 1)

            def exps(t, b, g):
                n, par = 4 * t + b, b % 2
                act.wait_ge(sem("masked"), 4 * n + g + 1)
                if g == 0:
                    need(act, sem("pt_done"), 2 * (n - 1))
                    need(act, sem("last_pv_ready"), n - 1)
                    if par == 0:
                        need(act, sem("rsum_ready"), 2 * t + b // 2 - 1)
                nc.scalar.activation(prob[:, par, g, :], sm[:, g, :], ACT.Exp, bias=neg_max[:, g:g + 1], scale=-1.0,
                                     accum_out=sums[:, b, g:g + 1]).then_inc(sem("exp_done"), 1)

            def probs_high(t, b, pair):
                n = 4 * t + b
                act.wait_ge(sem("pt_done"), 2 * n + 1 + pair)
                need(act, sem("pv_done"), 2 * n - 1 + pair)
                copy(p_hi[:, pair, :, :], p_pt[:, :].rearrange("p (j n) -> p j n", j=4), P_UP
                     ).then_inc(sem(f"p_hi{pair}_ready"), 1)

            def values_high(t, b):
                n = 4 * t + b
                act.wait_ge(sem("v_done"), n + 1)
                need(act, sem("pv_done"), 2 * (n - 3))
                copy(v_s[:, b, :, :, 0, :], p_kv[:, :].rearrange("p (j g n) -> p j g n", j=2, g=G), 1 / W_UP
                     ).then_inc(sem("v_hi_ready"), 1)

            def XT(u):
                act.wait_ge(sem("xt_done"), u + 1)
                need(act, sem("q_done"), u)
                copy(xq_t[:, :, :], r0[:, 0:C].rearrange("p (k n) -> p k n", k=2)).then_inc(sem("xq_t_ready"), 1)

            def Q(u):
                act.wait_ge(sem("q_done"), u + 1)
                need(act, sem("qbd_ready"), 4 * u)
                copy(q_hi[:, :, :], r0[:, 0:C].rearrange("p (k n) -> p k n", k=2)).then_inc(sem("q_hi_ready"), 1)

            def T3(u):
                act.wait_ge(sem("t3_done"), u + 1)
                need(act, sem("h_done"), 2 * u)
                copy(f_hi[:, :, :], r1[:, 0:C].rearrange("p (k n) -> p k n", k=2)).then_inc(sem("f_hi_ready"), 1)

            def hidden(u, bank, first):
                act.wait_ge(sem("h_done"), 2 * u + 1 + first // 4)
                for m in range(4):
                    nc.scalar.activation(h_g[:, first + m, :], bank[:, P * m:P * m + P], ACT.Gelu,
                                         bias=b1[:, first + m:first + m + 1]).then_inc(sem("h_g_ready"), 1)

            def Ha(u):
                need(act, sem("h_lo_ready"), 2 * u)
                hidden(u, r1, 0)

            def Hb(u):
                hidden(u, r0, 4)

            def squares_sum(u):
                act.wait_ge(sem("xn_ready"), u + 1)
                need(act, sem("nrm_ready"), u)
                nc.scalar.activation(squares[:, :], xn[:, :], ACT.Square,
                                     accum_out=sum_sq[:, :]).then_inc(sem("ss_ready"), 1)

            def TR(u):
                act.wait_ge(sem("tr_done"), u + 1)
                need(act, sem("ff_done"), u)
                copy(x_hi[:, :, :], r0[:, :].rearrange("p (k n) -> p k n", k=4)).then_inc(sem("x_hi_ready"), 1)

            def GA(u):
                act.wait_ge(sem("gate_b_ready"), u + 1)
                need(act, sem("gate_ready"), u)
                nc.scalar.activation(gate_th[:, :, :], gate_b[:, :, :], ACT.Tanh,
                                     scale=0.5).then_inc(sem("gate_th_ready"), 1)

            def VR(u):
                act.wait_ge(sem("vr_done"), u + 1)
                need(act, sem("vbd_ready"), u)
                copy(vr[:, :], r1[:, 0:C], 1 / W_UP).then_inc(sem("vr_ready"), 1)

            def FFN(u):
                act.wait_ge(sem("ff_done"), u + 1)
                need(act, sem("acc_done"), u)
                nc.scalar.activation(ff_g[:, :, :], r0[:, :].rearrange("p (k n) -> p k n", k=4),
                                     ACT.Gelu, scale=1 / W_UP).then_inc(sem("ff_g_ready"), 1)

            def y_squares(u):
                act.wait_ge(sem("y_ctr_ready"), u + 1)
                need(act, sem("y_ss_ready"), u)
                nc.scalar.activation(y_sq[:, :, :], y_ctr[:, :, :], ACT.Square).then_inc(sem("y_sq_ready"), 1)

            def weights(job, name, part):
                bank = bank_of(job)
                act.wait_ge(sem("job_done"), job + 1)
                if name == "qkvff":
                    k, lot = part // 3, part % 3
                    w = 512 if lot < 2 else 256
                    if job == 0:
                        act.wait_ge(sem("rms_ready"), 1)
                    last = copy(qkvff_hi[:, k, 512 * lot:512 * lot + w], bank[:, 0:w], rms_up[:, k:k + 1])
                elif name == "gated":
                    for k in range(2):
                        for o, i in zip(by_group(gated_hi, k), by_head(bank[:, 256 * k:256 * k + 256])):
                            last = copy(o, i, W_UP)
                elif name == "wff":
                    last = copy(wff[:, 0:2, :], bank[:, :].rearrange("p (k n) -> p k n", k=2))
                elif name == "proj":
                    last = copy(wproj[:, 0, :], bank[:, 0:C])
                elif name == "w1":
                    last = copy(w1[:, part, 0:512], bank.bitcast(F16)[:, 0:512])
                elif name == "w2":
                    last = copy(w2[:, 4 * part:4 * part + 2, :],
                                bank.bitcast(F16)[:, 0:512].rearrange("p (k n) -> p k n", k=2))
                else:
                    act.sem_inc(sem("job_hi"), 1)
                    return
                last.then_inc(sem("job_hi"), 1)

            load_kv_weights(act, "wk", 0)
            context_high(0, 0)
            act.wait_ge(sem("wk_in"), 48)
            act.wait_ge(sem("wv_in"), 48)
            copy(wkv_hi[:, :, :], wkv32[:, :, :], W_UP).then_inc(sem("wkv_split"), 1)
            keys_high(0, 0)
            act.wait_ge(sem("v_last_ready"), 1)
            copy(kl_hi[:, :, :], r1[:, 0:2 * B].rearrange("p (m n) -> p m n", m=2)).then_inc(sem("kl_hi_ready"), 1)
            XT(0)
            values_high(0, 0)
            Q(0)
            context_high(0, 1)

            stages = {"T3": T3, "XT": XT, "squares_sum": squares_sum, "Q": Q, "Ha": Ha, "Hb": Hb, "T": TR,
                      "G": GA, "VR": VR,
                      "FF": FFN, "y_squares": y_squares}

            def step(t, inside=False):
                for slot in range(TB * SLOTS):
                    b, part = slot // SLOTS, slot % SLOTS
                    now, before, next1, next2 = (placed(t, b, k, inside) for k in (0, -1, 1, 2))
                    if part == 0 and before:
                        exps(*before, 2)
                        exps(*before, 3)
                    if part == 1 and before:
                        probs_high(*before, 0)
                    if part == 2 and next1:
                        keys_high(*next1)
                    if part == 2 and now:
                        exps(t, b, 0)
                        exps(t, b, 1)
                    if part == 3 and before:
                        probs_high(*before, 1)
                    if part == 4 and next1:
                        values_high(*next1)
                    if part == 4 and next2:
                        context_high(*next2)
                    if not inside and t == 0 and slot in (9, 11):
                        i, w = (0, w1_n) if slot == 9 else (1, w2_n)
                        act.wait_ge(sem("w_in2"), 32)
                        need(act, sem("abs_ready"), i)
                        nc.scalar.activation(scratch[:, :], w[:, :, :].rearrange("p k n -> p (k n)"), ACT.Abs,
                                             accum_out=abs_sum[:, i:i + 1]).then_inc(sem("abs_ready"), 1)
                    if job_of(t, slot, inside):
                        weights(*job_of(t, slot, inside))
                    for name, u in due(ACT_PLAN, slot, t, inside):
                        stages[name](u)

            run_steps(act, step)

        @blk.vector
        def _(dve):
            PASSED[dve] = sem("dve_passed")
            v = nc.vector

            def low_part(o, x, high, scale):
                return v.scalar_tensor_tensor(out=o, in0=x, scalar=scale, in1=high, op0=ALU.mult, op1=ALU.subtract)

            def context_low(t, b):
                n, par = 4 * t + b, b % 2
                dve.wait_ge(sem("hi_done"), n + 1)
                need(dve, sem("v_done"), n - 1)
                v.tensor_tensor(c_lo[:, par, :, :], p_ct[:, 0:256].rearrange("p (j n) -> p j n", j=2),
                                c_hi[:, par, 0:2, :], ALU.subtract).then_inc(sem("lo_done"), 1)
                v.tensor_tensor(c_hi[64:P, par, 2:4, :], p_ct[64:P, 256:512].rearrange("p (j n) -> p j n", j=2),
                                c_hi[64:P, par, 2:4, :], ALU.subtract).then_inc(sem("lo_done"), 1)

            def keys_low(t, b):
                n, par = 4 * t + b, b % 2
                dve.wait_ge(sem("k_hi_ready"), n + 1)
                need(dve, sem("s_done"), 4 * (n - 1))
                low_part(k_lo[:, par, :, 0:MF], p_kv[:, :].rearrange("p (m n) -> p m n", m=2),
                         k_hi[:, par, :, 0:MF], 1 / W_UP).then_inc(sem("k_lo_ready"), 1)

            def values_low(t, b):
                n = 4 * t + b
                dve.wait_ge(sem("v_hi_ready"), n + 1)
                need(dve, sem("pv_done"), 2 * (n - 3))
                low_part(v_s[:, b, :, :, 1, :], p_kv[:, :].rearrange("p (j g n) -> p j g n", j=2, g=G),
                         v_s[:, b, :, :, 0, :], 1 / W_UP).then_inc(sem("v_lo_ready"), 1)

            def mask_scores(t, b, g):
                n, par, half = 4 * t + b, b % 2, g % 2
                apart(dve, (sem("s_done"), 4 * n + g + 1), (sem(f"mask_in{b}"), 16 * (t + 1)),
                      (sem("exp_done"), 4 * (n - 1) + g + 1))
                v.tensor_tensor_reduce(sm[:, g, :], p_s[half][:, 0:M], mask_b[:, b, :], -(HD ** -0.5), HUGE,
                                       ALU.add, ALU.min, neg_max[:, g:g + 1]).then_inc(sem("masked"), 1)

            def probs_low(t, b, pair):
                n = 4 * t + b
                dve.wait_ge(sem(f"p_hi{pair}_ready"), n + 1)
                need(dve, sem("pv_done"), 2 * n - 1 + pair)
                low_part(p_lo[:, pair, :, :], p_pt[:, :].rearrange("p (j n) -> p j n", j=4),
                         p_hi[:, pair, :, :], P_UP).then_inc(sem(f"p_lo{pair}_ready"), 1)

            def output_taken(t, b):
                n, par = 4 * t + b, b % 2
                if par == 1:
                    dve.wait_ge(sem("exp_done"), 4 * n + 4)
                    need(dve, sem("oc_ready"), 2 * t + b // 2)
                    v.reciprocal(rsum[:, :, :], sums[:, b - 1:b + 1, :]).then_inc(sem("rsum_ready"), 1)
                dve.wait_ge(sem("pv_done"), 2 * n + 2)
                need(dve, sem("o_summed"), 2 * t + b // 2)
                for a in range(A):
                    rows = slice(32 * a, 32 * a + 32)
                    own = p_o[rows, :].rearrange("p (g l n) -> p g n l", g=G, l=2)[:, :, 16 * a:16 * a + 16, :]
                    v.tensor_reduce(o_raw[rows, par, :, :], own, AX_X, ALU.add).then_inc(sem("o_taken"), 1)

            def statistics(u, x, st_, mv_, stats_sem, mv_sem, used_sem):
                need(dve, used_sem, u)
                v.bn_stats(st_[:, :], x[:, :]).then_inc(stats_sem, 1)
                apart(dve, (stats_sem, u + 1))
                v.bn_aggr(mv_[:, :], st_[:, :]).then_inc(mv_sem, 1)

            def q_stats_(u):
                dve.wait_ge(sem("xq_in"), 16 * (u + 1))
                statistics(u, xq, q_stats, q_mv, sem("q_stats_ready"), sem("q_mv_ready"), sem("xnq_ready"))

            def q_norm(u):
                dve.wait_ge(sem("q_rstd_ready"), u + 1)
                need(dve, sem("xt_done"), u)
                v.tensor_scalar(xnq[:, :], xq[:, :], q_mv[:, 0:1], q_rstd[:, 0:1], ALU.subtract, ALU.mult
                                ).then_inc(sem("xnq_ready"), 1)

            def Q(u):
                dve.wait_ge(sem("q_hi_ready"), u + 1)
                need(dve, sem("qbd_ready"), 4 * u)
                v.tensor_tensor(q_lo[:, :, :], r0[:, 0:C].rearrange("p (k n) -> p k n", k=2), q_hi[:, :, :],
                                ALU.subtract).then_inc(sem("q_lo_ready"), 1)

            def OT(u):
                dve.wait_ge(sem("ot_done"), u + 1)
                need(dve, sem("wo_done"), u)
                v.tensor_copy(o_t[:, :, :, :], r1[:, 0:C].rearrange("p (b h r) -> p h b r", b=TB, h=2)
                              ).then_inc(sem("ot_ready"), 1)

            def WO(u):
                dve.wait_ge(sem("wo_done"), u + 1)
                dve.wait_ge(sem("xr_in"), 16 * (u + 1))
                need(dve, sem("xres_ready"), 2 * u)
                v.tensor_tensor(x1[:, :], r1[:, 0:C], xr[:, :], ALU.add).then_inc(sem("x1_ready"), 1)
                dve.wait_ge(sem("x1_ready"), u + 1)
                statistics(u, x1, stats, mv, sem("stats_ready"), sem("mv_ready"), sem("xn_ready"))

            def T3(u):
                dve.wait_ge(sem("f_hi_ready"), u + 1)
                need(dve, sem("h_done"), 2 * u)
                v.tensor_tensor(f_lo[:, :, :], r1[:, 0:C].rearrange("p (k n) -> p k n", k=2), f_hi[:, :, :],
                                ALU.subtract).then_inc(sem("f_lo_ready"), 1)

            def norm(u):
                dve.wait_ge(sem("rstd_ready"), u + 1)
                need(dve, sem("tr_done"), u)
                need(dve, sem("xres_ready"), 2 * u)
                v.tensor_scalar(xn[:, :], x1[:, :], mv[:, 0:1], rstd[:, 0:1], ALU.subtract, ALU.mult
                                ).then_inc(sem("xn_ready"), 1)

            def rms_norm(u):
                dve.wait_ge(sem("nrm_ready"), u + 1)
                v.tensor_scalar(nrm_c[:, :], nrm[:, :], C ** -0.5, 1e-8, ALU.mult, ALU.max
                                ).then_inc(sem("nrm_c_ready"), 1)
                dve.wait_ge(sem("nrm_c_ready"), u + 1)
                v.reciprocal(rnrm[:, :], nrm_c[:, :]).then_inc(sem("rnrm_ready"), 1)
                dve.wait_ge(sem("rnrm_ready"), u + 1)
                v.tensor_scalar(xu[:, :], xn[:, :], rnrm[:, 0:1], None, ALU.mult).then_inc(sem("xu_ready"), 1)

            def high_hidden(u, half):
                dve.wait_ge(sem("h_g_ready"), 8 * u + 4 * half + 4)
                if half == 0:
                    need(dve, sem("o2_done"), u)
                part = slice(4 * half, 4 * half + 4)
                v.tensor_copy(h_hi[:, part, :], h_g[:, part, :]).then_inc(sem("h_hi_ready"), 1)

            def Ha(u):
                high_hidden(u, 0)

            def Hb(u):
                high_hidden(u, 1)

            def TR(u):
                dve.wait_ge(sem("x_hi_ready"), u + 1)
                need(dve, sem("ff_done"), u)
                v.tensor_tensor(x_lo[:, :, :], r0[:, :].rearrange("p (k n) -> p k n", k=4), x_hi[:, :, :],
                                ALU.subtract).then_inc(sem("x_lo_ready"), 1)

            def T2(u):
                dve.wait_ge(sem("t2_done"), u + 1)
                need(dve, sem("st_done"), u)
                need(dve, sem("rbd_ready"), u)
                v.tensor_copy(qk_t[:, :, :], r1[:, :].rearrange("p (k n) -> p k n", k=4)).then_inc(sem("qk_t_ready"), 1)

            def GA(u):
                dve.wait_ge(sem("g_done"), u + 1)
                need(dve, sem("gate_ready"), u)
                v.scalar_tensor_tensor(out=gate_b[:, :, :], in0=r0[:, 0:C].rearrange("p (h n) -> p h n", h=2),
                                       scalar=1 / W_UP, in1=ax(b_gate[:, :], P), op0=ALU.mult, op1=ALU.add
                                       ).then_inc(sem("gate_b_ready"), 1)

            def QK(u):
                dve.wait_ge(sem("qk_done"), u + 1)
                need(dve, sem("qk_ready"), u)
                v.tensor_tensor(qk_cos[:, :], r1[:, :], cos_t[:, :], ALU.mult).then_inc(sem("qk_taken"), 1)
                v.tensor_tensor(qk_sin[:, 0::2], r1[:, 1::2], sin_t[:, 0::2], ALU.mult).then_inc(sem("qk_taken"), 1)
                v.tensor_tensor(qk_sin[:, 1::2], r1[:, 0::2], sin_t[:, 1::2], ALU.mult).then_inc(sem("qk_taken"), 1)

            def gate_out(u):
                dve.wait_ge(sem("gate_th_ready"), u + 1)
                need(dve, sem("gate_w_ready"), u)
                need(dve, sem("gate_o_ready"), u)
                v.scalar_tensor_tensor(out=gate[:, :, :], in0=gate_th[:, :, :], scalar=1.0, in1=gate_b[:, :, :],
                                       op0=ALU.add, op1=ALU.mult).then_inc(sem("gate_ready"), 1)

            def O2(u):
                dve.wait_ge(sem("o2_done"), u + 1)
                dve.wait_ge(sem("x2b_ready"), u + 1)
                dve.wait_ge(sem("out_free"), 16 * (u + 1))
                v.tensor_tensor(y_out[:, :], r1[:, 0:C], x2b[:, :], ALU.add).then_inc(sem("y_ready"), 1)

            def ST(u):
                dve.wait_ge(sem("st_done"), u + 1)
                need(dve, sem("y_done"), u)
                for half in range(2):
                    v.tensor_tensor(st[:, half, :, :].rearrange("p m n -> p (m n)"),
                                    p_r[:, 512 * half:512 * half + 256], decay[:, half, :], ALU.mult
                                    ).then_inc(sem("st_ready"), 1)

            def Y(u):
                dve.wait_ge(sem("y_done"), u + 1)
                grouped = r0[:, 0:C].rearrange("p (i n) -> p i n", n=HD)
                v.tensor_reduce(y_sum[:, :], grouped, AX_X, ALU.add).then_inc(sem("y_sum_ready"), 1)
                dve.wait_ge(sem("y_sum_ready"), u + 1)
                v.tensor_scalar(y_mean[:, :], y_sum[:, :], 1.0 / HD, None, ALU.mult).then_inc(sem("y_mean_ready"), 1)
                dve.wait_ge(sem("y_mean_ready"), u + 1)
                need(dve, sem("y_sq_ready"), u)
                v.tensor_tensor(y_ctr[:, :, :], grouped, ax(y_mean[:, :], HD), ALU.subtract
                                ).then_inc(sem("y_ctr_ready"), 1)

            def y_variance(u):
                dve.wait_ge(sem("y_sq_ready"), u + 1)
                need(dve, sem("y_ve_ready"), u)
                v.tensor_reduce(y_ss[:, :], y_sq[:, :, :], AX_X, ALU.add).then_inc(sem("y_ss_ready"), 1)

            def y_norm(u):
                dve.wait_ge(sem("y_rstd_ready"), u + 1)
                need(dve, sem("yt_done"), u)
                v.tensor_tensor(y_n[:, :, :, :].rearrange("p b g n -> p g b n"),
                                y_ctr[:, :, :].rearrange("p (g b) n -> p g b n", g=G),
                                y_rstd[:, :].rearrange("p (g b) -> p g b", g=G).unsqueeze(3).broadcast_to([P, G, TB, HD]),
                                ALU.mult
                                ).then_inc(sem("y_n_ready"), 1)

            def YT(u):
                dve.wait_ge(sem("yt_done"), u + 1)
                dve.wait_ge(sem("gate_w_ready"), u + 1)
                need(dve, sem("acc_done"), u)
                v.tensor_tensor(y_g[:, :, :, :], r1[:, 0:C].rearrange("p (b h r) -> p h b r", b=TB, h=2),
                                gate_w[:, :, :].rearrange("p h (b r) -> p h b r", b=TB), ALU.mult
                                ).then_inc(sem("y_g_ready"), 1)
                dve.wait_ge(sem("y_g_ready"), u + 1)
                dve.wait_ge(sem("gate_o_ready"), u + 1)
                v.tensor_tensor(y_t[:, :, :, :].rearrange("p h b r -> p h (b r)"),
                                y_g[:, :, :, :].rearrange("p h b r -> p h (b r)"), gate_o[:, :, :], ALU.add
                                ).then_inc(sem("y_t_ready"), 1)

            def ACC(u):
                dve.wait_ge(sem("acc_done"), u + 1)
                dve.wait_ge(sem("xres_ready"), 2 * (u + 1))
                need(dve, sem("x2b_ready"), u)
                v.tensor_tensor(x2[:, :], r0[:, 0:C], x_resb[:, :], ALU.add).then_inc(sem("x2_ready"), 1)
                dve.wait_ge(sem("x2_ready"), u + 1)
                statistics(u, x2, f_stats, f_mv, sem("f_stats_ready"), sem("f_mv_ready"), sem("f_xn_ready"))

            def ffn_norm(u):
                dve.wait_ge(sem("f_rstd_ready"), u + 1)
                need(dve, sem("t3_done"), u)
                v.tensor_scalar(f_xn[:, :], x2[:, :], f_mv[:, 0:1], f_rstd[:, 0:1], ALU.subtract, ALU.mult
                                ).then_inc(sem("f_xn_ready"), 1)

            def ternary(i, half):
                w, tern, n = ((w1_n, w1_t, 4), (w2_n, w2_t, 1))[i]
                blocks = slice(n * half, n * half + n)
                cols = slice(FF * half, FF * half + FF)
                flat = w[:, blocks, :].rearrange("p k n -> p (k n)")
                if i == 0:
                    v.tensor_scalar(below[:, cols], flat, thr_down[:, 0:1], None, ALU.is_lt
                                    ).then_inc(sem("below_ready"), 1)
                    dve.wait_ge(sem("below_ready"), half + 1)
                else:
                    dve.wait_ge(sem("below2_ready"), half + 1)
                v.scalar_tensor_tensor(out=tern[:, blocks, :].rearrange("p k n -> p (k n)"), in0=flat,
                                       scalar=thr_up[:, i:i + 1], in1=(below if i == 0 else below2)[:, cols], op0=ALU.is_gt,
                                       op1=ALU.subtract).then_inc(sem("ternary_ready"), 1)

            def weights(job, name, part):
                bank = bank_of(job)
                dve.wait_ge(sem("job_done"), job + 1)
                dve.wait_ge(sem("job_hi"), job + 1)
                if name == "qkvff":
                    k, lot = part // 3, part % 3
                    w = 512 if lot < 2 else 256
                    cols = slice(512 * lot, 512 * lot + w)
                    if job == 0:
                        dve.wait_ge(sem("rms_ready"), 1)
                    last = low_part(qkvff_lo[:, k, cols], bank[:, 0:w], qkvff_hi[:, k, cols], rms_up[:, k:k + 1])
                elif name == "gated":
                    for k in range(2):
                        for o, i, hi in zip(by_group(gated_lo, k), by_head(bank[:, 256 * k:256 * k + 256]),
                                            by_group(gated_hi, k)):
                            last = low_part(o, i, hi, W_UP)
                elif name == "wff":
                    last = v.tensor_copy(wff[:, 2:4, :], r1[:, :].rearrange("p (k n) -> p k n", k=2))
                elif name == "proj":
                    last = v.tensor_copy(wproj[:, 1, :], bank[:, C:2 * C])
                elif name == "w1":
                    last = v.tensor_copy(w1[:, part, 512:1024], bank.bitcast(F16)[:, 512:1024])
                elif name == "w2":
                    last = v.tensor_copy(w2[:, 4 * part + 2:4 * part + 4, :],
                                         bank.bitcast(F16)[:, 512:1024].rearrange("p (k n) -> p k n", k=2))
                else:
                    v.tensor_scalar(mean_abs[:, :], bank[:, 0:2], 1.0 / (FF * C), 1e-8, ALU.mult, ALU.max
                                    ).then_inc(sem("mean_abs_ready"), 1)
                    dve.wait_ge(sem("mean_abs_ready"), 1)
                    v.tensor_scalar(thr_up[:, :], mean_abs[:, :], 0.5, None, ALU.mult).then_inc(sem("thr_ready"), 1)
                    v.tensor_scalar(thr_down[:, :], mean_abs[:, :], -0.5, None, ALU.mult).then_inc(sem("thr_ready"), 1)
                    dve.wait_ge(sem("thr_ready"), 2)
                    dve.sem_inc(sem("job_lo"), 1)
                    return
                last.then_inc(sem("job_lo"), 1)

            context_low(0, 0)
            dve.wait_ge(sem("last_tr"), 1)
            v.tensor_copy(last_t[:, 0, :], r0[:, 0:B]).then_inc(sem("last_t_ready"), 1)
            v.tensor_copy(last_t[0:64, 1, :], r0[0:64, B:2 * B]).then_inc(sem("last_t_ready"), 1)
            dve.wait_ge(sem("wkv_split"), 1)
            low_part(wkv_lo[:, :, :], wkv32[:, :, :], wkv_hi[:, :, :], W_UP).then_inc(sem("wkv_split"), 1)
            q_stats_(0)
            q_norm(0)
            keys_low(0, 0)
            dve.wait_ge(sem("last_kv"), 1)
            for a in range(A):
                last = v.tensor_scalar(v_last[:, 64 * a:64 * a + 64].rearrange("p (g n) -> p g n", g=G),
                                       r1[0:B, 256:512].rearrange("p (g a n) -> p a g n", g=G, a=A)[:, a, :, :],
                                       P_UP, None, ALU.mult)
            last.then_inc(sem("v_last_ready"), 1)
            dve.wait_ge(sem("kl_hi_ready"), 1)
            v.tensor_tensor(kl_lo[:, :, :], r1[:, 0:2 * B].rearrange("p (m n) -> p m n", m=2), kl_hi[:, :, :],
                            ALU.subtract).then_inc(sem("k_last_ready"), 1)
            values_low(0, 0)
            Q(0)
            context_low(0, 1)
            v.tensor_copy(ident16[:, :], ident[:, :]).then_inc(sem("ident16_ready"), 1)

            stages = {"Q": Q, "OT": OT, "WO": WO, "T3": T3, "norm": norm, "rms_norm": rms_norm,
                      "Ha": Ha, "Hb": Hb, "T": TR, "T2": T2, "G": GA,
                      "QK": QK, "gate": gate_out, "O2": O2, "q_stats": q_stats_, "q_norm": q_norm, "ST": ST, "Y": Y,
                      "y_variance": y_variance, "y_norm": y_norm, "YT": YT, "ACC": ACC, "ffn_norm": ffn_norm}

            def step(t, inside=False):
                for slot in range(TB * SLOTS):
                    b, part = slot // SLOTS, slot % SLOTS
                    now, before, before2, next1, next2 = (placed(t, b, k, inside) for k in (0, -1, -2, 1, 2))
                    if part == 0 and now:
                        mask_scores(t, b, 0)
                        mask_scores(t, b, 1)
                    if part == 1 and before:
                        probs_low(*before, 0)
                    if part == 1 and before2:
                        output_taken(*before2)
                    if part == 2 and next1:
                        keys_low(*next1)
                    if part == 2 and now:
                        mask_scores(t, b, 2)
                        mask_scores(t, b, 3)
                    if part == 3 and before:
                        probs_low(*before, 1)
                    if part == 4 and next1:
                        values_low(*next1)
                    if part == 4 and next2:
                        context_low(*next2)
                    if job_of(t, slot, inside):
                        weights(*job_of(t, slot, inside))
                    if not inside and t == 0 and slot in TERNARY:
                        ternary(*TERNARY[slot])
                    for name, u in due(DVE_PLAN, slot, t, inside):
                        stages[name](u)

            run_steps(dve, step)

        @blk.gpsimd
        def _(pool):
            PASSED[pool] = sem("pool_passed")
            g_ = nc.gpsimd

            def rstd_of(u, mv_, ve, rs, mv_sem, used_sem, ve_sem, rs_sem):
                apart(pool, (mv_sem, u + 1), (used_sem, u))
                g_.tensor_scalar(ve[:, :], mv_[:, 1:2], EPS, None, ALU.add).then_inc(ve_sem, 1)
                pool.wait_ge(ve_sem, u + 1)
                g_.tensor_tensor(rs[:, :], ve[:, :], halves[:, 0, 0:1], ALU.pow).then_inc(rs_sem, 1)

            def last_key(t, b):
                n, par = 4 * t + b, b % 2
                need(pool, sem("s_done"), 4 * (n - 1))
                g_.tensor_copy(k_hi[:, par, :, MF:M], kl_hi[:, :, bass.ds(n, 1)])
                g_.tensor_copy(k_lo[:, par, :, MF:M], kl_lo[:, :, bass.ds(n, 1)]).then_inc(sem("klast_ready"), 1)

            def last_value(t, b):
                n, par = 4 * t + b, b % 2
                pool.wait_ge(sem("exp_done"), 4 * n + 4)
                need(pool, sem("o_summed"), 2 * t + b // 2 - 1)
                g_.tensor_tensor(last_pv[:, b, :, :], vl[:, bass.ds(n, 1), :].rearrange("p o (g n) -> p (o g) n", g=G),
                                 prob[:, par, :, MF:M].broadcast_to([P, G, HD]), ALU.mult
                                 ).then_inc(sem("last_pv_ready"), 1)

            def output_scaled(t, b):
                pair = 2 * t + b // 2
                pool.wait_ge(sem("rsum_ready"), pair + 1)
                pool.wait_ge(sem("o_taken"), 4 * (4 * t + b + 1))
                pool.wait_ge(sem("last_pv_ready"), 4 * t + b + 1)
                need(pool, sem("oc_ready"), pair)
                g_.tensor_tensor(o_sum[:, :, :, :], o_raw[:, :, :, :], last_pv[:, b - 1:b + 1, :, :], ALU.add
                                 ).then_inc(sem("o_summed"), 1)
                pool.wait_ge(sem("o_summed"), pair + 1)
                need(pool, sem("ot_done"), t)
                g_.tensor_tensor(o_c[:, b - 1:b + 1, :].rearrange("p b (g n) -> p (b g) n", g=G),
                                 o_sum[:, :, :, :].rearrange("p b g n -> p (b g) n"),
                                 ax(rsum[:, :, :].rearrange("p b g -> p (b g)"), HD), ALU.mult
                                 ).then_inc(sem("oc_ready"), 1)

            def queries(u, b):
                n = 4 * u + b
                if b == 0:
                    pool.wait_ge(sem("q_lo_ready"), u + 1)
                need(pool, sem("s_done"), 4 * (n - 4) + 4)
                for q, spread in ((q_hi, qbd_hi), (q_lo, qbd_lo)):
                    last = g_.tensor_tensor(spread[:, :, b, :, :],
                                            q[:, :, S * b:S * b + S].unsqueeze(2).broadcast_to([P, 2, A, S]),
                                            head_mask[:, :].unsqueeze(1).unsqueeze(3).broadcast_to([P, 2, A, S]),
                                            ALU.mult)
                last.then_inc(sem("qbd_ready"), 1)

            def norm(u):
                rstd_of(u, mv, var_eps, rstd, sem("mv_ready"), sem("xn_ready"), sem("var_eps_ready"), sem("rstd_ready"))

            def nrm_(u):
                pool.wait_ge(sem("ss_ready"), u + 1)
                need(pool, sem("nrm_c_ready"), u)
                g_.tensor_tensor(nrm[:, :], sum_sq[:, :], halves[:, 1, 0:1], ALU.pow).then_inc(sem("nrm_ready"), 1)

            def low_hidden(u, half):
                pool.wait_ge(sem("h_hi_ready"), 2 * u + half + 1)
                if half == 0:
                    need(pool, sem("o2_done"), u)
                part = slice(4 * half, 4 * half + 4)
                g_.tensor_tensor(h_lo[:, part, :], h_g[:, part, :], h_hi[:, part, :], ALU.subtract
                                 ).then_inc(sem("h_lo_ready"), 1)

            def low_a(u):
                low_hidden(u, 0)

            def low_b(u):
                low_hidden(u, 1)

            def ternary_below(half):
                if half == 0:
                    pool.wait_ge(sem("thr_ready"), 2)
                g_.tensor_scalar(below2[:, FF * half:FF * half + FF], w2_n[:, half, :], thr_down[:, 1:2],
                                 None, ALU.is_lt).then_inc(sem("below2_ready"), 1)

            def q_norm(u):
                rstd_of(u, q_mv, q_ve, q_rstd, sem("q_mv_ready"), sem("xnq_ready"), sem("q_ve_ready"), sem("q_rstd_ready"))

            def residual(u):
                pool.wait_ge(sem("xn_ready"), u + 1)
                need(pool, sem("x2_ready"), u)
                g_.tensor_tensor(x_res[:, :], x1[:, :], xn[:, :], ALU.add).then_inc(sem("xres_ready"), 1)
                pool.wait_ge(sem("xres_ready"), 2 * u + 1)
                g_.tensor_tensor(x_resb[:, :], x_res[:, :], b_proj[:, :], ALU.add).then_inc(sem("xres_ready"), 1)

            def qk_sum(u):
                pool.wait_ge(sem("qk_taken"), 3 * (u + 1))
                need(pool, sem("t2_done"), u)
                g_.tensor_tensor(qk[:, :, :].rearrange("p k n -> p (k n)"), qk_cos[:, :], qk_sin[:, :], ALU.add
                                 ).then_inc(sem("qk_ready"), 1)

            def v_blocks(u):
                pool.wait_ge(sem("vr_ready"), u + 1)
                need(pool, sem("y_done"), u)
                g_.tensor_tensor(vbd[:, :, :, :],
                                 vr[:, :].rearrange("p (g n) -> p g n", g=G).unsqueeze(2).broadcast_to([P, G, TB, 64]),
                                 batch_mask[:, :].unsqueeze(1).unsqueeze(3).broadcast_to([P, G, TB, 64]), ALU.mult
                                 ).then_inc(sem("vbd_ready"), 1)

            def gates(u):
                pool.wait_ge(sem("gate_ready"), u + 1)
                need(pool, sem("y_t_ready"), u)
                g_.tensor_tensor(gate_w[:, :, :], gate[:, :, :], ax(gn_w2[:, :], P), ALU.mult
                                 ).then_inc(sem("gate_w_ready"), 1)
                g_.tensor_tensor(gate_o[:, :, :], gate[:, :, :], ax(gn_b2[:, :], P), ALU.mult
                                 ).then_inc(sem("gate_o_ready"), 1)

            def r_queries(u):
                pool.wait_ge(sem("qk_t_ready"), u + 1)
                need(pool, sem("st_done"), u)
                for m in range(2):
                    last = g_.tensor_tensor(
                        rbd[:, m, :, :, :],
                        qk_t[:, m, :].rearrange("p (b r) -> p b r", b=TB).unsqueeze(2).broadcast_to([P, TB, A, S]),
                        head_mask[:, :].unsqueeze(1).unsqueeze(3).broadcast_to([P, TB, A, S]), ALU.mult)
                last.then_inc(sem("rbd_ready"), 1)

            def y_rstd_(u):
                apart(pool, (sem("y_ss_ready"), u + 1), (sem("y_n_ready"), u))
                g_.tensor_scalar(y_ve[:, :], y_ss[:, :], 1.0 / HD, EPS, ALU.mult, ALU.add).then_inc(sem("y_ve_ready"), 1)
                pool.wait_ge(sem("y_ve_ready"), u + 1)
                g_.tensor_tensor(y_rstd[:, :], y_ve[:, :], halves[:, 0, :], ALU.pow).then_inc(sem("y_rstd_ready"), 1)

            def ffn_norm(u):
                rstd_of(u, f_mv, f_ve, f_rstd, sem("f_mv_ready"), sem("f_xn_ready"), sem("f_ve_ready"), sem("f_rstd_ready"))

            def out_bias(u):
                pool.wait_ge(sem("x2_ready"), u + 1)
                need(pool, sem("y_ready"), u)
                g_.tensor_tensor(x2b[:, :], x2[:, :], b2[:, :], ALU.add).then_inc(sem("x2b_ready"), 1)

            g_.memset(halves[:, 0, :], -0.5).then_inc(sem("halves_ready"), 1)
            g_.memset(halves[:, 1, :], 0.5).then_inc(sem("halves_ready"), 1)
            g_.memset(ones[:, :], 1.0).then_inc(sem("ones_ready"), 1)
            pool.wait_ge(sem("halves_ready"), 2)
            pool.wait_ge(sem("mask_u8_in"), 16)
            g_.tensor_scalar(mask_all[:, :], mask_u8[:, :], 1.0, BIG, ALU.subtract, ALU.mult
                             ).then_inc(sem("mask_ready"), 1)
            q_norm(0)
            pool.wait_ge(sem("k_last_ready"), 1)
            last_key(0, 0)
            pool.wait_ge(sem("masks_in"), 32)
            for b in range(TB):
                queries(0, b)

            stages = {"norm": norm, "nrm": nrm_, "low_a": low_a, "low_b": low_b, "q_norm": q_norm, "residual": residual,
                      "qk_sum": qk_sum, "v_blocks": v_blocks, "gates": gates, "r_queries": r_queries,
                      "y_rstd": y_rstd_, "ffn_norm": ffn_norm, "out_bias": out_bias}
            queries_at = {9: [0, 1], 13: [2], 18: [3]}

            def step(t, inside=False):
                for slot in range(TB * SLOTS):
                    b, part = slot // SLOTS, slot % SLOTS
                    before, next1 = placed(t, b, -1, inside), placed(t, b, 1, inside)
                    pair = placed(t, b, -2, inside) if b % 2 == 1 else None
                    if part == 1 and before:
                        if not inside and before in ((0, 0), (1, 0)):
                            pool.wait_ge(sem("vl_in" if t == 0 else "vl_rest_in"), 64)
                        last_value(*before)
                    if part == 2 and pair:
                        output_scaled(*pair)
                    if part == 2 and next1:
                        last_key(*next1)
                    if inside or t + 1 < T:
                        first = not inside and t == 0
                        for place in (range(TB) if slot == 18 else []) if first else queries_at.get(slot, []):
                            queries(t + 1, place)
                    if not inside and t == 0 and slot == 15:
                        pool.wait_ge(sem("vec_in"), 16 * 3 * A)
                        g_.tensor_scalar(gn_w2[:, :], gn_w[:, :], 0.5, None, ALU.mult).then_inc(sem("gn_ready"), 1)
                        g_.tensor_scalar(gn_b2[:, :], gn_b[:, :], 0.5, None, ALU.mult).then_inc(sem("gn_ready"), 1)
                        pool.wait_ge(sem("gn_ready"), 2)
                    if not inside and t == 0 and slot in (14, 15):
                        ternary_below(slot - 14)
                    if not inside and t == 0 and slot == 1:
                        pool.wait_ge(sem("w_in0"), 32)
                        g_.tensor_scalar(rms_up[:, :], rms[:, :], W_UP, None, ALU.mult).then_inc(sem("rms_ready"), 1)
                    if not inside and t == 1 and slot == 0:
                        pool.wait_ge(sem("wo_in"), 64)
                        g_.tensor_scalar(wo[:, :, :], wo[:, :, :], 1 / P_UP, None, ALU.mult).then_inc(sem("wo_ready"), 1)
                    for name, u in due(POOL_PLAN, slot, t, inside):
                        stages[name](u)

            run_steps(pool, step)


def tables():
    f = np.float32
    p = np.arange(P)
    t = {"ident": np.eye(P, dtype=f)}
    t["head_mask"] = ((p[:, None] % 64) // HD == np.arange(A)[None, :]).astype(f)
    t["batch_mask"] = (p[:, None] // S == np.arange(TB)[None, :]).astype(f)
    half = C // 2
    pos = np.arange(S, dtype=f)
    angle = pos[:, None] * (f(1.0) / f(10000.0) ** (np.arange(half, dtype=f) / f(half)))[None, :]
    base = (np.arange(0, C, 2, dtype=f) + f(0.4 * C)) / f(1.4 * C)
    scale = base[None, :] ** ((pos - f(S // 2)) / f(128))[:, None]
    cos = np.repeat(np.concatenate([np.cos(angle) * scale, np.cos(angle) / scale], 1), 2, axis=1)
    sin = np.repeat(np.concatenate([np.sin(angle) * scale, np.sin(angle) / scale], 1), 2, axis=1)
    sin = sin * np.tile(np.array([-1.0, 1.0], f), C)[None, :]
    t["cos_t"] = np.tile(cos, (TB, 1)).astype(f) / f(W_UP)
    t["sin_t"] = np.tile(sin, (TB, 1)).astype(f) / f(W_UP)
    gamma = f(1.0) - f(2.0) ** (f(-5.0) - np.arange(H, dtype=f))
    diff = np.arange(S)[None, :] - np.arange(S)[:, None]
    by_head = np.where(diff[None] >= 0, gamma[:, None, None] ** np.maximum(diff, 0)[None].astype(f), 0) * HD ** -0.5
    by_head = by_head.reshape(2, 2, A, S, S).transpose(3, 1, 0, 2, 4).reshape(S, 2 * 2 * A * S)
    t["decay"] = np.tile(by_head, (TB, 1)).astype(f)
    return t


def kernel(**inputs):
    import concourse.bacc as bacc
    from concourse.bass_utils import run_bass_kernel_spmd as run

    nc = bacc.Bacc("TRN2", target_bir_lowering=False, num_devices=1)
    names = {"x": "x", "ctx": "ctx_768", "mask": "mask_BxS2_bf1", "wq": "L0_xattn_Wq", "wk": "L0_xattn_Wk",
             "wv": "L0_xattn_Wv", "wo": "L0_xattn_Wo", "qkvff": "L0_attn_w_qkvff", "gated": "L0_attn_w_gated",
             "b_gate": "L0_attn_b_gated", "proj": "L0_attn_w_proj", "b_proj": "L0_attn_b_proj",
             "gn_w": "L0_attn_gn_w", "gn_b": "L0_attn_gn_b", "wff": "L0_attn_w_ff", "rms": "L0_attn_rms_w",
             "w1": "L0_ffn_W1", "b1": "L0_ffn_b1", "w2": "L0_ffn_W2", "b2": "L0_ffn_b2"}
    host = {k: np.ascontiguousarray(inputs[v]) for k, v in names.items()}
    host["x"] = host["x"].reshape(B * S, C)
    host["mask"] = host["mask"].view(np.uint8)
    host.update(tables())
    arrays, d = {}, {}
    for k, a in host.items():
        arrays[f"in_{k}"] = a
        d[k] = nc.dram_tensor(f"in_{k}", a.shape, mybir.dt.from_np(a.dtype), kind="ExternalInput").ap()
    out = nc.dram_tensor("out", (B * S, C), F32, kind="ExternalOutput").ap()
    vl_dram = nc.dram_tensor("vl_dram", (B, C), F32, kind="Internal").ap()
    mask_dram = nc.dram_tensor("mask_dram", (B, M), BF16, kind="Internal").ap()
    block_kernel(nc, d, out, vl_dram, mask_dram)
    r = run(nc, [arrays], core_ids=[0])
    return r.results[0]["out"].reshape(B, S, C)
```
